# Optimizing a Trainium2 kernel written in Bass

```python
import numpy as np
import jax
import jax.numpy as jnp

def _softmax(x, axis=-1):
    return jax.nn.softmax(x, axis=axis)

def _gelu(x):
    return jax.nn.gelu(x, approximate=True)

def _silu(x):
    return jax.nn.silu(x)

def _sigmoid(x):
    return jax.nn.sigmoid(x)

def _layernorm(x, axis=-1, eps=1e-05):
    m = jnp.mean(x, axis=axis, keepdims=True)
    v = jnp.var(x, axis=axis, keepdims=True)
    return (x - m) / jnp.sqrt(v + eps)

def _scatter_add(tgt, idx, src, axis=0):
    return tgt.at[idx].add(src)

def _segment_sum(src, seg, n):
    return jax.ops.segment_sum(src, seg, n)
kernel_name = 'mk_prb_d4_jaxref_r4_5b6fe6'

def setup_inputs(seed: int=0):
    np.random.seed(seed)
    _w = jnp.asarray

    def _L0_attn_setup():
        import jax, jax.numpy as jnp
        import numpy as np
        B, S, E = (2, 512, 256)
        H = 16
        D = E // H
        key = jax.random.key(seed)
        ks = jax.random.split(key, 11)
        s = 1.0 / np.sqrt(E)
        return {'x': jax.random.normal(ks[0], (B, S, E), dtype=jnp.float32), 'Wq': jax.random.uniform(ks[1], (E, E), jnp.float32, -s, s), 'bq': jnp.zeros((E,), jnp.float32), 'Wk': jax.random.uniform(ks[2], (E, E), jnp.float32, -s, s), 'bk': jnp.zeros((E,), jnp.float32), 'Wv': jax.random.uniform(ks[3], (E, E), jnp.float32, -s, s), 'bv': jnp.zeros((E,), jnp.float32), 'Wo': jax.random.uniform(ks[4], (E, E), jnp.float32, -s, s), 'bo': jnp.zeros((E,), jnp.float32), 'J_attn': jax.random.normal(ks[5], (H, D, D), jnp.float32) * 0.02, 'lambda_attn': jnp.float32(0.5)}
    _L0_attn_in = _L0_attn_setup()

    def _L0_ffn_setup():
        import jax, jax.numpy as jnp
        import numpy as np
        LORA_DIM = 16
        LORA_TOKEN_INDEX = 1
        B, S, D, H = (4, 512, 256, 1024)
        key = jax.random.key(seed)
        ks = jax.random.split(key, 6)
        x = jax.random.normal(ks[0], (B, S, D), dtype=jnp.float32)
        W1 = jax.random.normal(ks[1], (H, D), dtype=jnp.float32) * 0.02
        b1 = jnp.zeros((H,), dtype=jnp.float32)
        W2 = jax.random.normal(ks[2], (D, H), dtype=jnp.float32) * 0.02
        b2 = jnp.zeros((D,), dtype=jnp.float32)
        scale = jnp.asarray(0.001, dtype=jnp.float32)
        return {'x': x, 'W1': W1, 'b1': b1, 'W2': W2, 'b2': b2, 'scale': scale}
    _L0_ffn_in = _L0_ffn_setup()

    def _L1_attn_setup():
        import jax, jax.numpy as jnp
        import numpy as np
        H = 16
        G = 4
        THETA = 10000.0

        def _rope(x, cos, sin):
            x0 = x[..., ::2]
            x1 = x[..., 1::2]
            r0 = x0 * cos - x1 * sin
            r1 = x0 * sin + x1 * cos
            return jnp.stack([r0, r1], axis=-1).reshape(x.shape)
        key = jax.random.key(seed)
        ks = jax.random.split(key, 5)
        B, S, D = (2, 512, 256)
        return {'x': jax.random.normal(ks[0], (B, S, D), jnp.float32), 'Wq': jax.random.normal(ks[1], (D, D), jnp.float32) * 0.02, 'Wk': jax.random.normal(ks[2], (D, D // G), jnp.float32) * 0.02, 'Wv': jax.random.normal(ks[3], (D, D // G), jnp.float32) * 0.02, 'Wo': jax.random.normal(ks[4], (D, D), jnp.float32) * 0.02}
    _L1_attn_in = _L1_attn_setup()

    def _L1_ffn_setup():
        import jax, jax.numpy as jnp
        import numpy as np
        D_MODEL = 256
        NUM_SLOTS = 64
        TOP_K = 8
        B, T = (4, 1024)

        def _forward(x, slot_init, slot_scale, w1, b1, w2, b2, gru_wih, gru_whh, gru_bih, gru_bhh, wv, bv, wo, bo, tau):
            Bn, Tn, D = x.shape
            Sn = slot_init.shape[0]
            S = jnp.broadcast_to((slot_init * slot_scale)[None], (Bn, Sn, D)).astype(x.dtype)
            slot_mean = S.mean(axis=1, keepdims=True)
            ctx = jnp.concatenate([x, jnp.broadcast_to(slot_mean, x.shape)], axis=-1)
            h = jax.nn.gelu(ctx @ w1.T + b1, approximate=False)
            route_logits = (h @ w2.T + b2) / (jnp.abs(tau) + 0.1)
            topk_vals, topk_idx = jax.lax.top_k(route_logits, TOP_K)
            topk_w = jax.nn.softmax(topk_vals, axis=-1)
            alpha = jnp.sum(topk_w[..., None] * jax.nn.one_hot(topk_idx, Sn, dtype=x.dtype), axis=-2)
            slot_input = jnp.einsum('bts,btd->bsd', alpha, x)
            slot_wsum = alpha.sum(axis=1) + 1e-08
            gi = (slot_input / slot_wsum[..., None]).reshape(Bn * Sn, D)
            hs = S.reshape(Bn * Sn, D)
            gx = gi @ gru_wih.T + gru_bih
            gh = hs @ gru_whh.T + gru_bhh
            xr, xz, xn = jnp.split(gx, 3, axis=-1)
            hr, hz, hn = jnp.split(gh, 3, axis=-1)
            r = jax.nn.sigmoid(xr + hr)
            z = jax.nn.sigmoid(xz + hz)
            n = jnp.tanh(xn + r * hn)
            h_new = (1.0 - z) * n + z * hs
            S_new = h_new.reshape(Bn, Sn, D)
            slot_values = S_new @ wv.T + bv
            out = jnp.einsum('bts,bsd->btd', alpha, slot_values)
            return out @ wo.T + bo
        key = jax.random.key(seed)
        ks = jax.random.split(key, 16)
        D, S = (D_MODEL, NUM_SLOTS)
        H = D // 2
        sc = lambda fan_in: 1.0 / np.sqrt(fan_in)
        inp = {'x': jax.random.normal(ks[0], (B, T, D), dtype=jnp.float32), 'slot_init': jax.random.normal(ks[1], (S, D), dtype=jnp.float32) * 0.1, 'slot_scale': jnp.ones((S, 1), dtype=jnp.float32), 'w1': jax.random.normal(ks[2], (H, 2 * D), dtype=jnp.float32) * sc(2 * D), 'b1': jnp.zeros((H,), dtype=jnp.float32), 'w2': jax.random.normal(ks[3], (S, H), dtype=jnp.float32) * sc(H), 'b2': jnp.zeros((S,), dtype=jnp.float32), 'gru_wih': jax.random.normal(ks[4], (3 * D, D), dtype=jnp.float32) * sc(D), 'gru_whh': jax.random.normal(ks[5], (3 * D, D), dtype=jnp.float32) * sc(D), 'gru_bih': jnp.zeros((3 * D,), dtype=jnp.float32), 'gru_bhh': jnp.zeros((3 * D,), dtype=jnp.float32), 'wv': jax.random.normal(ks[6], (D, D), dtype=jnp.float32) * sc(D), 'bv': jnp.zeros((D,), dtype=jnp.float32), 'wo': jax.random.normal(ks[7], (D, D), dtype=jnp.float32) * sc(D), 'bo': jnp.zeros((D,), dtype=jnp.float32), 'tau': jnp.ones((1,), dtype=jnp.float32)}
        return inp
    _L1_ffn_in = _L1_ffn_setup()

    def _L2_attn_setup():
        import jax, jax.numpy as jnp
        import numpy as np
        D_MODEL, D_STATE, D_CONV, D_INNER = (256, 16, 4, 512)
        BATCH, SEQLEN = (4, 512)

        def _mamba_fwd(x, W_in, conv_w, W_x, W_dt, b_dt, W_Bp, D_param, W_out):
            B, L, _ = x.shape
            xz = x @ W_in
            xc, z = jnp.split(xz, 2, axis=-1)
            xt = jnp.transpose(xc, (0, 2, 1))
            xt = jax.lax.conv_general_dilated(xt, conv_w, window_strides=(1,), padding=[(D_CONV - 1, 0)], dimension_numbers=('NCH', 'OIH', 'NCH'), feature_group_count=D_INNER)
            u = jax.nn.silu(jnp.transpose(xt, (0, 2, 1)))
            xp = u @ W_x
            dt_raw, B_raw = jnp.split(xp, 2, axis=-1)
            dt = jax.nn.softplus(dt_raw @ W_dt + b_dt)
            Bp = B_raw @ W_Bp
            dt = jnp.clip(dt, 0.0001, 1.0)
            ub = u * Bp

            def step(h, inp):
                d_t, ub_t = inp
                h = h * (1.0 - d_t) + ub_t
                return (h, h)
            _, ys = jax.lax.scan(step, jnp.zeros((B, D_INNER), x.dtype), (jnp.transpose(dt, (1, 0, 2)), jnp.transpose(ub, (1, 0, 2))))
            y = jnp.transpose(ys, (1, 0, 2)) + D_param * u
            y = y * jax.nn.silu(z)
            return y @ W_out
        key = jax.random.key(seed)
        ks = jax.random.split(key, 8)
        x = jax.random.normal(ks[0], (BATCH, SEQLEN, D_MODEL), jnp.float32)
        W_in = jax.random.normal(ks[1], (D_MODEL, 2 * D_INNER), jnp.float32) / np.float32(np.sqrt(D_MODEL))
        conv_w = jax.random.normal(ks[2], (D_INNER, 1, D_CONV), jnp.float32) * np.float32(0.3)
        W_x = jax.random.normal(ks[3], (D_INNER, 2 * D_STATE), jnp.float32) / np.float32(np.sqrt(D_INNER))
        W_dt = jax.random.normal(ks[4], (D_STATE, D_INNER), jnp.float32) / np.float32(np.sqrt(D_STATE))
        b_dt = jax.random.normal(ks[5], (D_INNER,), jnp.float32) * np.float32(0.1)
        W_Bp = jax.random.normal(ks[6], (D_STATE, D_INNER), jnp.float32) / np.float32(np.sqrt(D_STATE))
        D_param = jnp.ones((D_INNER,), jnp.float32)
        W_out = jax.random.normal(ks[7], (D_INNER, D_MODEL), jnp.float32) / np.float32(np.sqrt(D_INNER))
        return {'x': x, 'W_in': W_in, 'conv_w': conv_w, 'W_x': W_x, 'W_dt': W_dt, 'b_dt': b_dt, 'W_Bp': W_Bp, 'D_param': D_param, 'W_out': W_out}
    _L2_attn_in = _L2_attn_setup()

    def _L2_ffn_setup():
        import jax, jax.numpy as jnp
        import numpy as np
        B, T, C = (4, 512, 256)
        E = 8
        K = 2
        H = 352
        HS = 352 * 2
        key = jax.random.key(seed)
        k = jax.random.split(key, 8)
        s = 0.02
        return {'x': jax.random.normal(k[0], (B, T, C), jnp.float32), 'Wg': jax.random.normal(k[1], (C, E), jnp.float32) * s, 'W1': jax.random.normal(k[2], (E, C, H), jnp.float32) * s, 'W2': jax.random.normal(k[3], (E, C, H), jnp.float32) * s, 'W3': jax.random.normal(k[4], (E, H, C), jnp.float32) * s, 'Ws1': jax.random.normal(k[5], (C, HS), jnp.float32) * s, 'Ws2': jax.random.normal(k[6], (C, HS), jnp.float32) * s, 'Ws3': jax.random.normal(k[7], (HS, C), jnp.float32) * s}
    _L2_ffn_in = _L2_ffn_setup()

    def _L3_attn_setup():
        import jax, jax.numpy as jnp
        import numpy as np
        WINDOW = 128

        def _block_local_attn(q, k, v, window):
            B, H, T, D = q.shape
            W = window
            nb = T // W
            scale = 1.0 / jnp.sqrt(jnp.asarray(D, q.dtype))
            qb = q.reshape(B, H, nb, W, D)
            kb = k.reshape(B, H, nb, W, D)
            vb = v.reshape(B, H, nb, W, D)
            kp = jnp.pad(kb, ((0, 0), (0, 0), (1, 0), (0, 0), (0, 0)))[:, :, :nb]
            vp = jnp.pad(vb, ((0, 0), (0, 0), (1, 0), (0, 0), (0, 0)))[:, :, :nb]
            k2 = jnp.concatenate([kp, kb], axis=3)
            v2 = jnp.concatenate([vp, vb], axis=3)
            i = jnp.arange(W)[:, None]
            j = jnp.arange(2 * W)[None, :]
            base = (j > i) & (j <= i + W)
            prev_ok = (jnp.arange(nb)[:, None] > 0) | (jnp.arange(2 * W)[None, :] >= W)
            mask = base[None, :, :] & prev_ok[:, None, :]
            scores = jnp.einsum('bhnqd,bhnkd->bhnqk', qb, k2) * scale
            scores = jnp.where(mask[None, None], scores, jnp.asarray(-1e+30, scores.dtype))
            p = jax.nn.softmax(scores, axis=-1)
            out = jnp.einsum('bhnqk,bhnkd->bhnqd', p, v2)
            return out.reshape(B, H, T, D)
        key = jax.random.key(seed)
        ks = jax.random.split(key, 5)
        B, T, C = (2, 2048, 256)
        s = 1.0 / np.sqrt(C)
        return {'x': jax.random.normal(ks[0], (B, T, C), dtype=jnp.float32), 'Wq': jax.random.normal(ks[1], (C, C), dtype=jnp.float32) * s, 'Wk': jax.random.normal(ks[2], (C, C), dtype=jnp.float32) * s, 'Wv': jax.random.normal(ks[3], (C, C), dtype=jnp.float32) * s, 'Wo': jax.random.normal(ks[4], (C, C), dtype=jnp.float32) * s}
    _L3_attn_in = _L3_attn_setup()

    def _L3_ffn_setup():
        import jax, jax.numpy as jnp
        import numpy as np
        B, S, H, F, G = (8, 512, 256, 1024, 128)
        EPS = 1e-05

        def _dequant(q, scales, g):
            K, N = q.shape
            w = (q.astype(jnp.float32) - 128.0).reshape(K // g, g, N) * scales[:, None, :]
            return w.reshape(K, N)
        key = jax.random.key(seed)
        ks = jax.random.split(key, 8)
        x = jax.random.normal(ks[0], (B, S, H), dtype=jnp.float32)
        ln_gamma = jnp.ones((H,), jnp.float32)
        ln_beta = jnp.zeros((H,), jnp.float32)
        fc1_q = jax.random.randint(ks[1], (H, F), 0, 64, dtype=jnp.int32)
        fc2_q = jax.random.randint(ks[2], (F, H), 0, 64, dtype=jnp.int32)
        fc1_scales = jax.random.uniform(ks[3], (H // G, F), jnp.float32) * 0.02 + 0.001
        fc2_scales = jax.random.uniform(ks[4], (F // G, H), jnp.float32) * 0.02 + 0.001
        fc1_bias = jax.random.normal(ks[5], (F,), jnp.float32) * 0.02
        fc2_bias = jax.random.normal(ks[6], (H,), jnp.float32) * 0.02
        return {'x': x, 'ln_gamma': ln_gamma, 'ln_beta': ln_beta, 'fc1_q': fc1_q, 'fc1_scales': fc1_scales, 'fc1_bias': fc1_bias, 'fc2_q': fc2_q, 'fc2_scales': fc2_scales, 'fc2_bias': fc2_bias}
    _L3_ffn_in = _L3_ffn_setup()
    _d = {'L0_attn_x': _L0_attn_in['x'], 'L0_attn_Wq': _L0_attn_in['Wq'], 'L0_attn_bq': _L0_attn_in['bq'], 'L0_attn_Wk': _L0_attn_in['Wk'], 'L0_attn_bk': _L0_attn_in['bk'], 'L0_attn_Wv': _L0_attn_in['Wv'], 'L0_attn_bv': _L0_attn_in['bv'], 'L0_attn_Wo': _L0_attn_in['Wo'], 'L0_attn_bo': _L0_attn_in['bo'], 'L0_attn_J_attn': _L0_attn_in['J_attn'], 'L0_attn_lambda_attn': _L0_attn_in['lambda_attn'], 'L0_ffn_W1': _L0_ffn_in['W1'], 'L0_ffn_b1': _L0_ffn_in['b1'], 'L0_ffn_W2': _L0_ffn_in['W2'], 'L0_ffn_b2': _L0_ffn_in['b2'], 'L0_ffn_scale': _L0_ffn_in['scale'], 'L1_attn_Wq': _L1_attn_in['Wq'], 'L1_attn_Wk': _L1_attn_in['Wk'], 'L1_attn_Wv': _L1_attn_in['Wv'], 'L1_attn_Wo': _L1_attn_in['Wo'], 'L1_ffn_slot_init': _L1_ffn_in['slot_init'], 'L1_ffn_slot_scale': _L1_ffn_in['slot_scale'], 'L1_ffn_w1': _L1_ffn_in['w1'], 'L1_ffn_b1': _L1_ffn_in['b1'], 'L1_ffn_w2': _L1_ffn_in['w2'], 'L1_ffn_b2': _L1_ffn_in['b2'], 'L1_ffn_gru_wih': _L1_ffn_in['gru_wih'], 'L1_ffn_gru_whh': _L1_ffn_in['gru_whh'], 'L1_ffn_gru_bih': _L1_ffn_in['gru_bih'], 'L1_ffn_gru_bhh': _L1_ffn_in['gru_bhh'], 'L1_ffn_wv': _L1_ffn_in['wv'], 'L1_ffn_bv': _L1_ffn_in['bv'], 'L1_ffn_wo': _L1_ffn_in['wo'], 'L1_ffn_bo': _L1_ffn_in['bo'], 'L1_ffn_tau': _L1_ffn_in['tau'], 'L2_attn_W_in': _L2_attn_in['W_in'], 'L2_attn_conv_w': _L2_attn_in['conv_w'], 'L2_attn_W_x': _L2_attn_in['W_x'], 'L2_attn_W_dt': _L2_attn_in['W_dt'], 'L2_attn_b_dt': _L2_attn_in['b_dt'], 'L2_attn_W_Bp': _L2_attn_in['W_Bp'], 'L2_attn_D_param': _L2_attn_in['D_param'], 'L2_attn_W_out': _L2_attn_in['W_out'], 'L2_ffn_Wg': _L2_ffn_in['Wg'], 'L2_ffn_W1': _L2_ffn_in['W1'], 'L2_ffn_W2': _L2_ffn_in['W2'], 'L2_ffn_W3': _L2_ffn_in['W3'], 'L2_ffn_Ws1': _L2_ffn_in['Ws1'], 'L2_ffn_Ws2': _L2_ffn_in['Ws2'], 'L2_ffn_Ws3': _L2_ffn_in['Ws3'], 'L3_attn_Wq': _L3_attn_in['Wq'], 'L3_attn_Wk': _L3_attn_in['Wk'], 'L3_attn_Wv': _L3_attn_in['Wv'], 'L3_attn_Wo': _L3_attn_in['Wo'], 'L3_ffn_ln_gamma': _L3_ffn_in['ln_gamma'], 'L3_ffn_ln_beta': _L3_ffn_in['ln_beta'], 'L3_ffn_fc1_q': _L3_ffn_in['fc1_q'], 'L3_ffn_fc1_scales': _L3_ffn_in['fc1_scales'], 'L3_ffn_fc1_bias': _L3_ffn_in['fc1_bias'], 'L3_ffn_fc2_q': _L3_ffn_in['fc2_q'], 'L3_ffn_fc2_scales': _L3_ffn_in['fc2_scales'], 'L3_ffn_fc2_bias': _L3_ffn_in['fc2_bias']}
    _x0 = _d['L0_attn_x']
    _d['L0_attn_x'] = jax.random.normal(jax.random.fold_in(jax.random.key(seed), 1), (8, 512, 256), dtype=_x0.dtype)
    del _x0
    return _d

def reference(L0_attn_x, L0_attn_Wq, L0_attn_bq, L0_attn_Wk, L0_attn_bk, L0_attn_Wv, L0_attn_bv, L0_attn_Wo, L0_attn_bo, L0_attn_J_attn, L0_attn_lambda_attn, L0_ffn_W1, L0_ffn_b1, L0_ffn_W2, L0_ffn_b2, L0_ffn_scale, L1_attn_Wq, L1_attn_Wk, L1_attn_Wv, L1_attn_Wo, L1_ffn_slot_init, L1_ffn_slot_scale, L1_ffn_w1, L1_ffn_b1, L1_ffn_w2, L1_ffn_b2, L1_ffn_gru_wih, L1_ffn_gru_whh, L1_ffn_gru_bih, L1_ffn_gru_bhh, L1_ffn_wv, L1_ffn_bv, L1_ffn_wo, L1_ffn_bo, L1_ffn_tau, L2_attn_W_in, L2_attn_conv_w, L2_attn_W_x, L2_attn_W_dt, L2_attn_b_dt, L2_attn_W_Bp, L2_attn_D_param, L2_attn_W_out, L2_ffn_Wg, L2_ffn_W1, L2_ffn_W2, L2_ffn_W3, L2_ffn_Ws1, L2_ffn_Ws2, L2_ffn_Ws3, L3_attn_Wq, L3_attn_Wk, L3_attn_Wv, L3_attn_Wo, L3_ffn_ln_gamma, L3_ffn_ln_beta, L3_ffn_fc1_q, L3_ffn_fc1_scales, L3_ffn_fc1_bias, L3_ffn_fc2_q, L3_ffn_fc2_scales, L3_ffn_fc2_bias):

    def _L0_attn_ref(x, Wq, bq, Wk, bk, Wv, bv, Wo, bo, J_attn, lambda_attn):
        import jax, jax.numpy as jnp
        import numpy as np
        B, S, E = (2, 512, 256)
        H = 16
        D = E // H
        b, s, _ = x.shape
        scale = jnp.sqrt(jnp.float32(D))

        def split_heads(y):
            return y.reshape(b, s, H, D).transpose(0, 2, 1, 3)
        Q = split_heads(x @ Wq.T + bq)
        K = split_heads(x @ Wk.T + bk)
        V = split_heads(x @ Wv.T + bv)
        attn_scores = jnp.einsum('bhid,bhjd->bhij', Q, K) / scale
        Qn = jnp.tanh(Q)
        Kn = jnp.tanh(K)
        QJ = jnp.einsum('bhid,hde->bhie', Qn, J_attn)
        delta = jnp.einsum('bhie,bhje->bhij', QJ, Kn)
        attn_scores = attn_scores + lambda_attn * delta
        attn_probs = jax.nn.softmax(attn_scores, axis=-1)
        out = jnp.einsum('bhij,bhjd->bhid', attn_probs, V)
        out = out.transpose(0, 2, 1, 3).reshape(b, s, E)
        return out @ Wo.T + bo

    def _L0_ffn_ref(x, W1, b1, W2, b2, scale):
        import jax, jax.numpy as jnp
        import numpy as np
        LORA_DIM = 16
        LORA_TOKEN_INDEX = 1
        B, S, D, H = (4, 512, 256, 1024)
        Bx, Sx, Dx = x.shape
        Hx = W1.shape[0]
        lt = jax.lax.dynamic_slice_in_dim(x, LORA_TOKEN_INDEX, LORA_DIM, axis=1)
        even = lt[:, ::2, :]
        odd = lt[:, 1::2, :]
        m1 = (even[:, :4, :, None] * odd[:, :4, None, :]).reshape(Bx, Hx, Dx)
        m2 = (even[:, 4:, :, None] * odd[:, 4:, None, :]).reshape(Bx, Dx, Hx)
        h = jnp.einsum('bsd,hd->bsh', x, W1) + scale * jnp.einsum('bsd,bhd->bsh', x, m1) + b1
        h = jax.nn.gelu(h, approximate=False)
        out = jnp.einsum('bsh,oh->bso', h, W2) + scale * jnp.einsum('bsh,boh->bso', h, m2) + b2
        return out

    def _L1_attn_ref(x, Wq, Wk, Wv, Wo):
        import jax, jax.numpy as jnp
        import numpy as np
        H = 16
        G = 4
        THETA = 10000.0

        def _rope(x, cos, sin):
            x0 = x[..., ::2]
            x1 = x[..., 1::2]
            r0 = x0 * cos - x1 * sin
            r1 = x0 * sin + x1 * cos
            return jnp.stack([r0, r1], axis=-1).reshape(x.shape)
        B, S, D = x.shape
        hd = D // H
        Hkv = H // G
        q = x @ Wq
        k = x @ Wk
        v = x @ Wv
        k = jnp.repeat(k.reshape(B, S, Hkv, hd), G, axis=2)
        v = jnp.repeat(v.reshape(B, S, Hkv, hd), G, axis=2)
        inv = 1.0 / THETA ** (jnp.arange(0, D, 2, dtype=jnp.float32) / D)
        ang = jnp.arange(S, dtype=jnp.float32)[:, None] * inv[None, :]
        q = _rope(q, jnp.cos(ang)[None], jnp.sin(ang)[None])
        angk = ang[:, :hd // 2]
        k = _rope(k, jnp.cos(angk)[None, :, None, :], jnp.sin(angk)[None, :, None, :])
        q = q.reshape(B, S, H, hd).transpose(0, 2, 1, 3)
        k = k.transpose(0, 2, 1, 3)
        v = v.transpose(0, 2, 1, 3)
        scores = jnp.einsum('bhqd,bhkd->bhqk', q, k) / jnp.sqrt(jnp.float32(D))
        p = jax.nn.softmax(scores, axis=-1)
        o = jnp.einsum('bhqk,bhkd->bhqd', p, v)
        o = o.transpose(0, 2, 1, 3).reshape(B, S, D)
        return o @ Wo

    def _L1_ffn_ref(x, slot_init, slot_scale, w1, b1, w2, b2, gru_wih, gru_whh, gru_bih, gru_bhh, wv, bv, wo, bo, tau):
        import jax, jax.numpy as jnp
        import numpy as np
        D_MODEL = 256
        NUM_SLOTS = 64
        TOP_K = 8
        B, T = (4, 1024)

        def _forward(x, slot_init, slot_scale, w1, b1, w2, b2, gru_wih, gru_whh, gru_bih, gru_bhh, wv, bv, wo, bo, tau):
            Bn, Tn, D = x.shape
            Sn = slot_init.shape[0]
            S = jnp.broadcast_to((slot_init * slot_scale)[None], (Bn, Sn, D)).astype(x.dtype)
            slot_mean = S.mean(axis=1, keepdims=True)
            ctx = jnp.concatenate([x, jnp.broadcast_to(slot_mean, x.shape)], axis=-1)
            h = jax.nn.gelu(ctx @ w1.T + b1, approximate=False)
            route_logits = (h @ w2.T + b2) / (jnp.abs(tau) + 0.1)
            topk_vals, topk_idx = jax.lax.top_k(route_logits, TOP_K)
            topk_w = jax.nn.softmax(topk_vals, axis=-1)
            alpha = jnp.sum(topk_w[..., None] * jax.nn.one_hot(topk_idx, Sn, dtype=x.dtype), axis=-2)
            slot_input = jnp.einsum('bts,btd->bsd', alpha, x)
            slot_wsum = alpha.sum(axis=1) + 1e-08
            gi = (slot_input / slot_wsum[..., None]).reshape(Bn * Sn, D)
            hs = S.reshape(Bn * Sn, D)
            gx = gi @ gru_wih.T + gru_bih
            gh = hs @ gru_whh.T + gru_bhh
            xr, xz, xn = jnp.split(gx, 3, axis=-1)
            hr, hz, hn = jnp.split(gh, 3, axis=-1)
            r = jax.nn.sigmoid(xr + hr)
            z = jax.nn.sigmoid(xz + hz)
            n = jnp.tanh(xn + r * hn)
            h_new = (1.0 - z) * n + z * hs
            S_new = h_new.reshape(Bn, Sn, D)
            slot_values = S_new @ wv.T + bv
            out = jnp.einsum('bts,bsd->btd', alpha, slot_values)
            return out @ wo.T + bo
        return _forward(x, slot_init, slot_scale, w1, b1, w2, b2, gru_wih, gru_whh, gru_bih, gru_bhh, wv, bv, wo, bo, tau)

    def _L2_attn_ref(x, W_in, conv_w, W_x, W_dt, b_dt, W_Bp, D_param, W_out):
        import jax, jax.numpy as jnp
        import numpy as np
        D_MODEL, D_STATE, D_CONV, D_INNER = (256, 16, 4, 512)
        BATCH, SEQLEN = (4, 512)

        def _mamba_fwd(x, W_in, conv_w, W_x, W_dt, b_dt, W_Bp, D_param, W_out):
            B, L, _ = x.shape
            xz = x @ W_in
            xc, z = jnp.split(xz, 2, axis=-1)
            xt = jnp.transpose(xc, (0, 2, 1))
            xt = jax.lax.conv_general_dilated(xt, conv_w, window_strides=(1,), padding=[(D_CONV - 1, 0)], dimension_numbers=('NCH', 'OIH', 'NCH'), feature_group_count=D_INNER)
            u = jax.nn.silu(jnp.transpose(xt, (0, 2, 1)))
            xp = u @ W_x
            dt_raw, B_raw = jnp.split(xp, 2, axis=-1)
            dt = jax.nn.softplus(dt_raw @ W_dt + b_dt)
            Bp = B_raw @ W_Bp
            dt = jnp.clip(dt, 0.0001, 1.0)
            ub = u * Bp

            def step(h, inp):
                d_t, ub_t = inp
                h = h * (1.0 - d_t) + ub_t
                return (h, h)
            _, ys = jax.lax.scan(step, jnp.zeros((B, D_INNER), x.dtype), (jnp.transpose(dt, (1, 0, 2)), jnp.transpose(ub, (1, 0, 2))))
            y = jnp.transpose(ys, (1, 0, 2)) + D_param * u
            y = y * jax.nn.silu(z)
            return y @ W_out
        return _mamba_fwd(x, W_in, conv_w, W_x, W_dt, b_dt, W_Bp, D_param, W_out)

    def _L2_ffn_ref(x, Wg, W1, W2, W3, Ws1, Ws2, Ws3):
        import jax, jax.numpy as jnp
        import numpy as np
        B, T, C = (4, 512, 256)
        E = 8
        K = 2
        H = 352
        HS = 352 * 2
        b, t, c = x.shape
        xf = x.reshape(-1, c)
        n = xf.shape[0]
        router = xf @ Wg
        top_logits, idx = jax.lax.top_k(router, K)
        probs = jax.nn.softmax(top_logits.astype(jnp.float32), axis=-1).astype(x.dtype)
        w = jnp.zeros((n, E), x.dtype).at[jnp.arange(n)[:, None], idx].add(probs)
        h = jax.nn.silu(jnp.einsum('tc,ech->eth', xf, W1)) * jnp.einsum('tc,ech->eth', xf, W2)
        y = jnp.einsum('eth,ehc,te->tc', h, W3, w)
        y = y.reshape(b, t, c)
        hs = jax.nn.silu(xf @ Ws1) * (xf @ Ws2)
        y = y + (hs @ Ws3).reshape(b, t, c)
        return y

    def _L3_attn_ref(x, Wq, Wk, Wv, Wo):
        import jax, jax.numpy as jnp
        import numpy as np
        WINDOW = 128

        def _block_local_attn(q, k, v, window):
            B, H, T, D = q.shape
            W = window
            nb = T // W
            scale = 1.0 / jnp.sqrt(jnp.asarray(D, q.dtype))
            qb = q.reshape(B, H, nb, W, D)
            kb = k.reshape(B, H, nb, W, D)
            vb = v.reshape(B, H, nb, W, D)
            kp = jnp.pad(kb, ((0, 0), (0, 0), (1, 0), (0, 0), (0, 0)))[:, :, :nb]
            vp = jnp.pad(vb, ((0, 0), (0, 0), (1, 0), (0, 0), (0, 0)))[:, :, :nb]
            k2 = jnp.concatenate([kp, kb], axis=3)
            v2 = jnp.concatenate([vp, vb], axis=3)
            i = jnp.arange(W)[:, None]
            j = jnp.arange(2 * W)[None, :]
            base = (j > i) & (j <= i + W)
            prev_ok = (jnp.arange(nb)[:, None] > 0) | (jnp.arange(2 * W)[None, :] >= W)
            mask = base[None, :, :] & prev_ok[:, None, :]
            scores = jnp.einsum('bhnqd,bhnkd->bhnqk', qb, k2) * scale
            scores = jnp.where(mask[None, None], scores, jnp.asarray(-1e+30, scores.dtype))
            p = jax.nn.softmax(scores, axis=-1)
            out = jnp.einsum('bhnqk,bhnkd->bhnqd', p, v2)
            return out.reshape(B, H, T, D)
        B, T, C = x.shape
        H = 16
        D = C // H
        q = (x @ Wq.T).reshape(B, T, H, D).transpose(0, 2, 1, 3)
        k = (x @ Wk.T).reshape(B, T, H, D).transpose(0, 2, 1, 3)
        v = (x @ Wv.T).reshape(B, T, H, D).transpose(0, 2, 1, 3)
        out = _block_local_attn(q, k, v, WINDOW)
        out = out.transpose(0, 2, 1, 3).reshape(B, T, C)
        return out @ Wo.T

    def _L3_ffn_ref(x, ln_gamma, ln_beta, fc1_q, fc1_scales, fc1_bias, fc2_q, fc2_scales, fc2_bias):
        import jax, jax.numpy as jnp
        import numpy as np
        B, S, H, F, G = (8, 512, 256, 1024, 128)
        EPS = 1e-05

        def _dequant(q, scales, g):
            K, N = q.shape
            w = (q.astype(jnp.float32) - 128.0).reshape(K // g, g, N) * scales[:, None, :]
            return w.reshape(K, N)
        residual = x
        mu = jnp.mean(x, axis=-1, keepdims=True)
        var = jnp.mean(jnp.square(x - mu), axis=-1, keepdims=True)
        h = (x - mu) * jax.lax.rsqrt(var + EPS) * ln_gamma + ln_beta
        hf = h.reshape(-1, H)
        w1 = _dequant(fc1_q, fc1_scales, G)
        y = hf @ w1 + fc1_bias
        y = jax.nn.silu(y)
        w2 = _dequant(fc2_q, fc2_scales, G)
        z = y @ w2 + fc2_bias
        return residual + 0.5 * z.reshape(residual.shape)
    x = L0_attn_x
    xn = _layernorm(x, axis=-1)
    x = x + _L0_attn_ref(xn, L0_attn_Wq, L0_attn_bq, L0_attn_Wk, L0_attn_bk, L0_attn_Wv, L0_attn_bv, L0_attn_Wo, L0_attn_bo, L0_attn_J_attn, L0_attn_lambda_attn) + _L0_ffn_ref(xn, L0_ffn_W1, L0_ffn_b1, L0_ffn_W2, L0_ffn_b2, L0_ffn_scale)
    xn = _layernorm(x, axis=-1)
    x = x + _L1_attn_ref(xn, L1_attn_Wq, L1_attn_Wk, L1_attn_Wv, L1_attn_Wo) + _L1_ffn_ref(xn, L1_ffn_slot_init, L1_ffn_slot_scale, L1_ffn_w1, L1_ffn_b1, L1_ffn_w2, L1_ffn_b2, L1_ffn_gru_wih, L1_ffn_gru_whh, L1_ffn_gru_bih, L1_ffn_gru_bhh, L1_ffn_wv, L1_ffn_bv, L1_ffn_wo, L1_ffn_bo, L1_ffn_tau)
    xn = _layernorm(x, axis=-1)
    x = x + _L2_attn_ref(xn, L2_attn_W_in, L2_attn_conv_w, L2_attn_W_x, L2_attn_W_dt, L2_attn_b_dt, L2_attn_W_Bp, L2_attn_D_param, L2_attn_W_out) + _L2_ffn_ref(xn, L2_ffn_Wg, L2_ffn_W1, L2_ffn_W2, L2_ffn_W3, L2_ffn_Ws1, L2_ffn_Ws2, L2_ffn_Ws3)
    xn = _layernorm(x, axis=-1)
    x = x + _L3_attn_ref(xn, L3_attn_Wq, L3_attn_Wk, L3_attn_Wv, L3_attn_Wo) + _L3_ffn_ref(xn, L3_ffn_ln_gamma, L3_ffn_ln_beta, L3_ffn_fc1_q, L3_ffn_fc1_scales, L3_ffn_fc1_bias, L3_ffn_fc2_q, L3_ffn_fc2_scales, L3_ffn_fc2_bias)
    return x

_drawn_inputs = setup_inputs


def setup_inputs(seed=0):
    import zlib

    import numpy as np

    out = dict(_drawn_inputs(seed))
    spreads = {'L0_attn_bq': (0.0, 0.8),
     'L0_attn_bk': (0.0, 0.8),
     'L0_attn_bv': (0.0, 0.1),
     'L0_attn_bo': (0.0, 0.1),
     'L0_ffn_b1': (0.0, 0.1),
     'L0_ffn_b2': (0.0, 0.1),
     'L1_ffn_slot_scale': (1.0, 0.6),
     'L1_ffn_b1': (0.0, 0.784),
     'L1_ffn_b2': (0.0, 0.575),
     'L1_ffn_gru_bih': (0.0, 0.295),
     'L1_ffn_gru_bhh': (0.0, 0.545),
     'L1_ffn_bv': (0.0, 0.1),
     'L1_ffn_bo': (0.0, 0.295),
     'L2_attn_D_param': (1.0, 0.6),
     'L3_ffn_ln_gamma': (1.0, 0.2),
     'L3_ffn_ln_beta': (0.0, 0.1)}
    factors = {'L0_attn_Wq': 8.0,
     'L0_attn_Wk': 7.973,
     'L0_attn_Wv': 4.322,
     'L0_attn_J_attn': 8.0,
     'L1_attn_Wq': 8.0,
     'L1_attn_Wk': 8.0,
     'L1_attn_Wv': 7.224,
     'L1_attn_Wo': 7.905,
     'L1_ffn_slot_init': 4.612,
     'L1_ffn_w1': 2.717,
     'L1_ffn_w2': 2.935,
     'L1_ffn_gru_whh': 8.0,
     'L2_attn_W_dt': 44.603,
     'L2_attn_b_dt': 64.0,
     'L2_ffn_Wg': 7.147,
     'L2_ffn_W1': 6.174,
     'L2_ffn_W2': 6.178,
     'L2_ffn_W3': 6.163,
     'L2_ffn_Ws1': 3.14,
     'L2_ffn_Ws2': 3.081,
     'L2_ffn_Ws3': 3.019,
     'L3_attn_Wq': 8.0,
     'L3_attn_Wk': 8.0,
     'L3_attn_Wv': 8.0,
     'L3_attn_Wo': 8.0,
     'L3_ffn_fc1_bias': 64.0,
     'L3_ffn_fc2_bias': 64.0,
     'L2_attn_W_x': 3.859,
     'L2_attn_W_Bp': 3.627}
    for name, (base, spread) in spreads.items():
        noise = np.random.default_rng([zlib.crc32(name.encode()), seed]).standard_normal(out[name].shape)
        drawn = base * np.exp(spread * noise) if base else spread * noise
        out[name] = jnp.asarray(drawn.astype(out[name].dtype))
    for name, factor in factors.items():
        out[name] = (out[name] * factor).astype(out[name].dtype)
    return out
```

```python
from contextlib import ExitStack

import concourse.bass as bass
from concourse import mybir

F32 = mybir.dt.float32
BF16 = mybir.dt.bfloat16
I32 = mybir.dt.int32
U32 = mybir.dt.uint32
ACT = mybir.ActivationFunctionType
ALU = mybir.AluOpType
AX = mybir.AxisListType.X

P = 128
BATCH, SEQ, DIM = 8, 512, 256
TT = SEQ // P
KT = DIM // P
NH, HD = 16, 16
GROUPS, GH = 4, 4
EPS = 1e-5
LAYERS = 4
STEPS_DVE = [32, 47, 49, 28]


class Signal:

    def __init__(self, sem, per, start=1):
        self.sem, self.per, self.start = sem, per, start

    def at(self, l, it, k=0):
        base = self.start + BATCH * sum(self.per[:l])
        return self.sem, it * self.per[l] + (base + k)


class Ring:

    def __init__(self, sem, name, tiles, plan):
        self.tiles, self.plan = tiles, plan
        self.order = [{n: i for i, (n, _) in enumerate(p)} for p in plan]
        self.full = Signal(sem(f"{name}_full"), [len(p) for p in plan])
        self.free = {r: Signal(sem(f"{name}_free_{r}"), [sum(x == r for _, x in p) for p in plan])
                     for r in ("act", "dve")}

    def tile(self, l, name):
        return self.tiles[self.order[l][name] % len(self.tiles)]

    def filled(self, l, it, name):
        return self.full.at(l, it, self.order[l][name] + 1)

    def vacated(self, l, it, name):
        u = self.order[l][name] - len(self.tiles)
        if u < 0:
            return [s.at(l, it) for s in self.free.values()]
        reader = self.plan[l][u][1]
        return [self.free[reader].at(l, it, sum(x == reader for _, x in self.plan[l][:u + 1]))]


class Chain:

    def __init__(self, eng, sem, per, start=1):
        self.eng, self.sig, self.count = eng, Signal(sem, per, start), 0

    def begin(self, l, it):
        self.l, self.it, self.count = l, it, 0

    def end(self):
        assert self.count == self.sig.per[self.l], (self.l, self.count)

    def mark(self, ins):
        ins.then_inc(self.sig.sem, 1)
        self.count += 1
        return self.count

    def wait(self, k=None):
        self.eng.wait_ge(*self.sig.at(self.l, self.it, self.count if k is None else k))


PRODUCTS_A = [(0, 0), (0, 1), (1, 0)]
PRODUCTS_B = [(1, 1), (0, 2), (2, 0)]


def s_uses(g):
    return [(("S", g, i), "dve") for i in range(GH * TT)]


SC_PLAN0 = ([("Q0", "act"), ("K0", "act"), ("Q1", "act"), ("K1", "act")]
            + [(("W1", i), "dve") for i in range(4)] + [("J0", "act"), ("J1", "act")]
            + [(("H", i), "act") for i in range(3)] + [(("W2", i), "dve") for i in range(4)]
            + [u for j in range(4) for u in s_uses(0)[4 * j:4 * j + 4] + [(("H", 3 + j), "act")]]
            + s_uses(1)[:4] + [(("H", 7), "act")] + s_uses(1)[4:] + s_uses(2) + s_uses(3))
ST_PLAN0 = ([("T", "act"), ("V", "dve")]
            + [(("E", g, kt, hp), "act") for g in range(GROUPS) for kt in range(TT) for hp in range(2)]
            + [("OUT", "dve")])
PU_PLAN = [(("U", g), "dve") for g in range(GROUPS)]
PM_PLAN = [(("M", g), "act") for g in range(GROUPS)]
SPLITS0 = ["Q0", "K0", "Q1", "K1", "KN0", "KN1", "J0", "J1"]
SLOT0 = {"Q0": 0, "K0": 1, "Q1": 2, "K1": 3, "KN0": 4, "KN1": 5, "J0": 0, "J1": 2}
WHERE0 = {"Q0": (0, 0, 0), "K0": (1, 0, 0), "Q1": (0, 0, 1), "K1": (1, 0, 1),
          "KN0": (1, 1, 0), "KN1": (1, 1, 1), "J0": (0, 1, 0), "J1": (0, 1, 1)}


SC_PLAN1 = ([("QE", "act"), ("QO", "act"), ("KK", "act"), ("H", "act"), ("L", "dve")]
            + s_uses(0) + s_uses(1) + s_uses(2) + [("AT", "act"), ("SI", "dve")] + s_uses(3)
            + [("GX", "dve"), ("SV", "act"), ("Z2", "act")])
ST_PLAN1 = ST_PLAN0
NE = 10
HT = [(0, 128), (128, 128), (256, 96)]


def expert_uses(e):
    return [(u, r) for i in range(len(HT)) for u, r in ((("A", e, i), "act"), (("B", e, i), "dve"))]


CT = 4
SC_PLAN2 = ([("R", "dve")] + [(("XC", c), "act") for c in range(CT)] + [(("Z", c), "act") for c in range(CT)]
            + expert_uses(8) + expert_uses(9) + [("XP", "act")] + expert_uses(0)
            + [u for c in range(CT) for u in ((("DT", c), "dve"), (("BP", c), "dve"))]
            + [u for e in range(1, 8) for u in expert_uses(e)])
ST_PLAN2 = ([("T", "act"), (("Y", 8), "dve"), (("Y", 9), "dve"), (("Y", 0), "dve")]
            + [(("Y", e), "dve") for e in range(1, 7)] + [("OUT", "dve"), (("Y", 7), "dve")])


def s3_uses(g):
    return [(("S", g, i), "dve") for i in range(2 * GH)]


SC_PLAN3 = ([("Q0", "act"), ("K0", "act"), ("Q1", "act"), ("K1", "act"), (("H", 0), "act"), (("H", 1), "act")]
            + s3_uses(0)[:4] + [(("H", 2), "act")] + s3_uses(0)[4:] + [(("H", 3), "act")]
            + s3_uses(1)[:4] + [(("H", 4), "act")] + s3_uses(1)[4:] + [(("H", 5), "act"), (("H", 6), "act"), (("H", 7), "act")]
            + s3_uses(2) + s3_uses(3))
ST_PLAN3 = ([("T", "act"), ("V", "dve"), ("T2", "act")]
            + [(("E", g, h), "act") for g in range(GROUPS) for h in range(GH)] + [("OUT", "dve")])
PU_PLAN1 = PU_PLAN3 = PU_PLAN
PM_PLAN1 = PM_PLAN3 = PM_PLAN
PU_PLAN2 = PM_PLAN2 = []
NSPLIT = [8, 4, 0, 4]
NGROUPS = [4, 4, 0, 4]
STACK_DMAS = [[12, 12, 0, 12], [12, 0, 0, 0], [12, 0, 0, 0], [12, 0, 0, 0]]


def build(nc, d, out):
    ctx = ExitStack()
    with ctx:
        def sb(name, shape, dt=F32, stack=ctx):
            return stack.enter_context(nc.sbuf_tensor(name, shape, dt))

        def ps(name, n=512, dt=F32):
            return ctx.enter_context(nc.psum_tensor(name, [P, n], dt))

        def sem(name):
            return ctx.enter_context(nc.semaphore(name))

        def dram(name, shape, dt=F32):
            return nc.dram_tensor(name, shape, dt, kind="Internal")

        xs = dram("xs", [BATCH * LAYERS + 1, SEQ, DIM])
        parts_dram = dram("parts_dram", [2, 3, 2, DIM, SEQ], BF16)
        m_dram = dram("m_dram", [GROUPS, 8, SEQ], BF16)

        xl = sb("xl", [P, TT, DIM])
        xn = sb("xn", [P, TT, DIM + 4])
        xnT = sb("xnT", [P, KT, SEQ])
        xres = sb("xres", [P, TT, DIM])
        bias_bc = sb("bias_bc", [P, 2, DIM])
        ident = sb("ident", [P, P])
        ident_bf = sb("ident_bf", [P, P], BF16)
        stats = sb("stats", [P, TT, 6])
        mv = sb("mv", [P, TT, 2])
        veps = sb("veps", [P, TT])
        rstd = sb("rstd", [P, TT])
        mhalf = sb("mhalf", [P, TT])
        attn = ExitStack()
        probs = sb("probs", [P, 2, GH * SEQ], F32, attn)
        vext = sb("vext", [P, TT, NH, 32], F32, attn)
        vbias = sb("vbias", [P, DIM], F32, attn)
        un = sb("un", [P, 2, SEQ], F32, attn)
        oc = sb("oc", [P, KT, SEQ], F32, attn)
        den = sb("den", [P, SEQ], F32, attn)
        rden = sb("rden", [P, SEQ], F32, attn)
        nmax = sb("nmax", [P, 2, TT, GH], F32, attn)
        msplit = sb("msplit", [P, 2, TT, 2, GH], BF16, attn)
        mrow = sb("mrow", [8, 2, SEQ], BF16, attn)
        rest = sb("rest", [P, 2, SEQ], F32, attn)
        parts = sb("parts", [P, 2, 3, SEQ], BF16, attn)

        banks = [ps(f"bank{i}") for i in range(2)]
        pairs = [ps(f"pair{i}", 1024) for i in range(2)]
        bank_u = ps("bank_u")
        bank_m = ps("bank_m", 1024, BF16)

        sc = Ring(sem, "sc", banks, [SC_PLAN0, SC_PLAN1, SC_PLAN2, SC_PLAN3])
        st = Ring(sem, "st", pairs, [ST_PLAN0, ST_PLAN1, ST_PLAN2, ST_PLAN3])
        pu = Ring(sem, "pu", [bank_u], [PU_PLAN, PU_PLAN1, PU_PLAN2, PU_PLAN3])
        pm = Ring(sem, "pm", [bank_m], [PM_PLAN, PM_PLAN1, PM_PLAN2, PM_PLAN3])

        def done(ring, l, it, name):
            p, u = ring.plan[l], ring.order[l][name]
            return ring.free[p[u][1]].at(l, it, sum(x == p[u][1] for _, x in p[:u + 1]))

        opened = {by: [] for by in ("sync", "gpsimd", "scalar", "vector", "tensor")}
        opened["tensor"] += [sc.full, st.full, pu.full, pm.full]
        for ring in (sc, st, pu, pm):
            opened["scalar"].append(ring.free["act"])
            opened["vector"].append(ring.free["dve"])

        def sig(name, per, by):
            signal = Signal(sem(name), per)
            opened[by].append(signal)
            return signal

        def open_signals(eng, by):
            for signal in opened[by]:
                eng.sem_inc(signal.sem, 1)

        one = [1] * LAYERS
        x_loaded = Signal(sem("x_loaded"), [16] * LAYERS, 16)
        ln_moments = Signal(sem("ln_moments"), [TT] * LAYERS, TT)
        ln_rstd = Signal(sem("ln_rstd"), one, 1)
        xn_ready = Signal(sem("xn_ready"), [TT] * LAYERS, TT)
        xres_ready = sig("xres_ready", one, "gpsimd")
        y_stored = sig("y_stored", [16] * LAYERS, "sync")
        tanh_ready = sig("tanh_ready", [4, 0, 0, 0], "scalar")
        split_two = sig("split_two", NSPLIT, "vector")
        split_all = sig("split_all", NSPLIT, "gpsimd")
        parts_stored = [sig(f"parts_stored{i}", [16 * ((n + 1 - i) // 2) for n in NSPLIT], "sync") for i in range(2)]
        stack_loaded = [sig(f"stack_loaded{g}", [16 * n for n in STACK_DMAS[g]], "sync") for g in range(GROUPS)]
        m_ready = sig("m_ready", NGROUPS, "vector")
        m_stored = sig("m_stored", [16 * n for n in NGROUPS], "sync")
        m_loaded = [sig(f"m_loaded{i}", [8 * n for n in NGROUPS], "sync") for i in range(2)]
        pv_done = sig("pv_done", [16, 16, 0, 4], "tensor")
        oc_loaded = [sig(f"oc_loaded{i}", [16 * GH * n // 2 for n in NGROUPS], "sync") for i in range(2)]
        xs_copied = sem("xs_copied")
        consts = sem("consts")
        dve_setup = sem("dve_setup")
        pool_setup = sem("pool_setup")
        fences = sem("fences")

        def fence(eng):
            eng.sem_inc(fences, 1)

        block = ctx.enter_context(nc.Block())
        x_tok = d["x"].rearrange("b (t p) f -> b p t f", p=P)
        xs_tok = xs[:, :, :].rearrange("b (t p) f -> b p t f", p=P)
        out_tok = out.rearrange("b (t p) f -> b p t f", p=P)
        l0 = ExitStack()
        q_a = sb("q_a", [P, 3, GH, SEQ], BF16, l0)
        k_a = sb("k_a", [P, 3, GH, SEQ], BF16, l0)
        q_b = sb("q_b", [P, 3, GH, SEQ], BF16, l0)
        k_b = sb("k_b", [P, 3, GH, SEQ], BF16, l0)
        hid0 = sb("hid0", [P, 8, SEQ], F32, l0)
        src0 = sb("src0", [P, 6, SEQ], F32, l0)
        tq = sb("tq", [P, KT, SEQ], F32, l0)
        wq0 = sb("wq0", [P, KT, DIM], F32, l0)
        wk0 = sb("wk0", [P, KT, DIM], F32, l0)
        wv0 = sb("wv0", [P, KT, DIM], F32, l0)
        wo0 = sb("wo0", [P, KT, DIM], F32, l0)
        bq0 = sb("bq0", [P, KT], F32, l0)
        bk0 = sb("bk0", [P, KT], F32, l0)
        b10 = sb("b10", [P, 8], F32, l0)
        j_rows = sb("j_rows", [P, KT, HD], F32, l0)
        same_head = sb("same_head", [P, NH], F32, l0)
        lam = sb("lam", [P, 1], F32, l0)
        jbd = sb("jbd", [P, KT, HD, NH], F32, l0)
        w1 = sb("w1", [P, KT, 1024], F32, l0)
        w2 = sb("w2", [P, 8, DIM], F32, l0)
        w1e = sb("w1e", [P, KT, 1024], F32, l0)
        w2e = sb("w2e", [P, 8, DIM], F32, l0)
        rows = sb("rows", [4, 4, DIM], F32, l0)
        lscale = sb("lscale", [4, 1], F32, l0)
        lmask = sb("lmask", [4, 4], F32, l0)
        ev1 = sb("ev1", [4, 4, DIM], F32, l0)
        ev2 = sb("ev2", [4, 4, DIM], F32, l0)
        l0.close()
        rows_loaded = sig("rows_loaded", [64, 0, 0, 0], "sync")
        ev_ready = sig("ev_ready", [8, 0, 0, 0], "gpsimd")

        def ln_stats(dve, l, it, step, k):
            dve.wait_ge(*(x_loaded.at(l, it, 16) if k else (x_loaded.sem, 16)))
            for t in range(TT):
                step.mark(nc.vector.bn_stats(stats[:, t, :], xl[:, t, :]))
            step.wait()
            fence(dve)
            for t in range(TT):
                nc.vector.bn_aggr(mv[:, t, :], stats[:, t, :]).then_inc(ln_moments.sem, 1)

        def ln_rsqrt(pool, l, it, step, k):
            pool.wait_ge(*(ln_moments.at(l, it, TT) if k else (ln_moments.sem, TT)))
            fence(pool)
            step.mark(nc.gpsimd.tensor_scalar(veps[:], mv[:, :, 1], EPS, None, ALU.add))
            step.wait()
            nc.gpsimd.tensor_tensor(rstd[:], veps[:], mhalf[:], ALU.pow).then_inc(ln_rstd.sem, 1)

        def ln_normalise(dve, l, it, k):
            dve.wait_ge(*(ln_rstd.at(l, it, 1) if k else (ln_rstd.sem, 1)))
            for t in range(TT):
                nc.vector.tensor_scalar(xn[:, t, 0:DIM], xl[:, t, :], mv[:, t, 0:1], rstd[:, t:t + 1],
                                        ALU.subtract, ALU.mult).then_inc(xn_ready.sem, 1)

        def pe_transpose_xn(pe, l, it):
            pe.wait_ge(*xn_ready.at(l, it))
            for s in st.vacated(l, it, "T"):
                pe.wait_ge(*s)
            for f in range(KT):
                for t in range(TT):
                    ins = nc.tensor.transpose(st.tile(l, "T")[:, f * SEQ + t * P:f * SEQ + (t + 1) * P],
                                              xn[:, t, f * P:(f + 1) * P], ident[:])
            ins.then_inc(st.full.sem, 1)

        def pe_project(pe, l, it, name, weight, m, width=P, rhs=None, offset=0):
            rhs = xnT if rhs is None else rhs
            for s in sc.vacated(l, it, name):
                pe.wait_ge(*s)
            for k in range(KT):
                ins = nc.tensor.matmul(sc.tile(l, name)[0:width, :], weight[:, k, m * P + offset:m * P + offset + width],
                                       rhs[:, k, :], start=(k == 0), stop=(k == KT - 1))
            ins.then_inc(sc.full.sem, 1)

        def pe_values(pe, l, it, weight):
            for s in st.vacated(l, it, "V"):
                pe.wait_ge(*s)
            n = weight.shape[2]
            for t in range(TT):
                for k in range(KT):
                    ins = nc.tensor.matmul(st.tile(l, "V")[:, t * DIM:t * DIM + n], xnT[:, k, t * P:(t + 1) * P],
                                           weight[:, k, :], start=(k == 0), stop=(k == KT - 1))
            ins.then_inc(st.full.sem, 1)

        def pe_scores(pe, l, it, g, i, q, k):
            name = ("S", g, i)
            h, qt = i // TT, i % TT
            if i == 0:
                pe.wait_ge(*stack_loaded[g].at(l, it, stack_loaded[g].per[l]))
                if g and l:
                    pe.wait_ge(*stack_loaded[0].at(l, it, stack_loaded[0].per[l]))
            for s in sc.vacated(l, it, name):
                pe.wait_ge(*s)
            nc.tensor.matmul(sc.tile(l, name)[:], q(g, h)[:, qt * P:(qt + 1) * P], k(g, h),
                             start=True, stop=True).then_inc(sc.full.sem, 1)

        def pe_max_rows(pe, l, it, g):
            pe.wait_ge(*m_ready.at(l, it, g + 1))
            for s in pm.vacated(l, it, ("M", g)):
                pe.wait_ge(*s)
            for qt in range(TT):
                ins = nc.tensor.transpose(bank_m[0:8, qt * P:(qt + 1) * P],
                                          msplit[:, g % 2, qt, :, :].rearrange("p a h -> p (a h)"), ident_bf[:])
            ins.then_inc(pm.full.sem, 1)

        def pe_scores_t(pe, l, it, g, kt, pairs_of):
            if kt == 0:
                pe.wait_ge(*m_loaded[g % 2].at(l, it, 16 * (g // 2 + 1)))
            for hp in range(2):
                name = ("E", g, kt, hp)
                for s in st.vacated(l, it, name):
                    pe.wait_ge(*s)
                for hh in range(2):
                    passes = pairs_of(g, 2 * hp + hh)
                    for n, (k, q) in enumerate(passes):
                        ins = nc.tensor.matmul(st.tile(l, name)[:, hh * SEQ:(hh + 1) * SEQ],
                                               k[:, kt * P:(kt + 1) * P], q,
                                               start=(n == 0), stop=(n == len(passes) - 1))
                ins.then_inc(st.full.sem, 1)

        def pe_weigh_values(pe, l, it, g, kt, kv=lambda g, h: GH * g + h):
            for hp in range(2):
                pe.wait_ge(*done(st, l, it, ("E", g, kt, hp)))
            if kt == 0:
                if g == 0:
                    pe.wait_ge(*done(st, l, it, "V"))
                for s in pu.vacated(l, it, ("U", g)):
                    pe.wait_ge(*s)
            for h in range(GH):
                ins = nc.tensor.matmul(bank_u[32 * h:32 * h + 32, :], vext[:, kt, kv(g, h), :],
                                       probs[:, kt % 2, h * SEQ:(h + 1) * SEQ], start=(kt == 0), stop=(kt == TT - 1))
            ins.then_inc(pv_done.sem, 1)

        def pe0(pe, it):
            l = 0
            pe_transpose_xn(pe, l, it)
            pe.wait_ge(*done(st, l, it, "T"))
            pe_project(pe, l, it, "Q0", wq0, 0)
            pe_project(pe, l, it, "K0", wk0, 0)
            pe_project(pe, l, it, "Q1", wq0, 1)
            pe_project(pe, l, it, "K1", wk0, 1)
            pe_values(pe, l, it, wv0)
            for i in range(4):
                hb, k = i // 2, i % 2
                for s in sc.vacated(l, it, ("W1", i)):
                    pe.wait_ge(*s)
                if i == 0:
                    pe.wait_ge(*rows_loaded.at(l, it, 64))
                    pe.wait_ge(*ev_ready.at(l, it, 8))
                nc.tensor.matmul(sc.tile(l, ("W1", i))[:], rows[:, 1, k * P:(k + 1) * P],
                                 ev1[:, 2 * hb:2 * hb + 2, :].rearrange("p a n -> p (a n)"),
                                 start=True, stop=True).then_inc(sc.full.sem, 1)
            for m in range(KT):
                name = f"J{m}"
                for s in sc.vacated(l, it, name):
                    pe.wait_ge(*s)
                pe.wait_ge(*tanh_ready.at(l, it, 3))
                for k in range(KT):
                    ins = nc.tensor.matmul(sc.tile(l, name)[:], jbd[:, k, 8 * m:8 * m + 8, :].rearrange("p e h -> p (e h)"),
                                           tq[:, k, :], start=(k == 0), stop=(k == KT - 1))
                ins.then_inc(sc.full.sem, 1)

            def hidden(i):
                if i == 0:
                    pe.wait_ge(*done(sc, l, it, ("W1", 3)))
                pe_project(pe, l, it, ("H", i), w1e, i)

            for i in range(3):
                hidden(i)
            for i in range(4):
                for s in sc.vacated(l, it, ("W2", i)):
                    pe.wait_ge(*s)
                for half in range(2):
                    ins = nc.tensor.matmul(sc.tile(l, ("W2", i))[:, half * DIM:(half + 1) * DIM],
                                           rows[:, 3, half * P:(half + 1) * P], ev2[:, i, :], start=(half == 0), stop=(half == 1))
                ins.then_inc(sc.full.sem, 1)

            def q(g, h):
                return q_a[0:96, g % 3, h, :]

            def k(g, h):
                return k_a[0:96, g % 3, h, :]

            def passes(g, h):
                return [(k_a[0:98, g % 3, h, :], q_a[0:98, g % 3, h, :]),
                        (k_b[0:96, g % 3, h, :], q_b[0:96, g % 3, h, :])]

            for j in range(4):
                for i in range(4):
                    pe_scores(pe, l, it, 0, 4 * j + i, q, k)
                hidden(3 + j)
            for i in range(4):
                pe_scores(pe, l, it, 1, i, q, k)
            hidden(7)
            pe_max_rows(pe, l, it, 0)
            for i in range(4, 16):
                pe_scores(pe, l, it, 1, i, q, k)
            for g in range(GROUPS):
                for kt in range(TT):
                    pe_scores_t(pe, l, it, g, kt, passes)
                    if kt == 0 and g < GROUPS - 1:
                        pe_max_rows(pe, l, it, g + 1)
                    if g + 2 < GROUPS:
                        for i in range(4):
                            pe_scores(pe, l, it, g + 2, 4 * kt + i, q, k)
                    if g or kt:
                        pe_weigh(pe, l, it, GROUPS * g + kt - 1)
            for s in st.vacated(l, it, "OUT"):
                pe.wait_ge(*s)
            pe.wait_ge(*done(sc, l, it, ("W2", 3)))
            pe.wait_ge(*done(sc, l, it, ("H", 7)))
            for t in range(TT):
                for i in range(8):
                    nc.tensor.matmul(st.tile(l, "OUT")[:, t * DIM:(t + 1) * DIM], hid0[:, i, t * P:(t + 1) * P],
                                     w2e[:, i, :], start=(i == 0 and t % 2 == 0), stop=False)
                if t == 0:
                    pe_weigh(pe, l, it, GROUPS * TT - 1)
            pe_out_heads(pe, l, it, wo0)

        def pe_weigh(pe, l, it, n, kv=lambda g, h: GH * g + h):
            pe_weigh_values(pe, l, it, n // TT, n % TT, kv)

        def pe_out_heads(pe, l, it, weight):
            for p in range(2):
                pe.wait_ge(*oc_loaded[p].at(l, it, oc_loaded[p].per[l]))
            for t in range(TT):
                for k in range(KT):
                    ins = nc.tensor.matmul(st.tile(l, "OUT")[:, t * DIM:(t + 1) * DIM], oc[:, k, t * P:(t + 1) * P],
                                           weight[:, k, :], start=False, stop=(k == KT - 1 and t % 2 == 1))
            ins.then_inc(st.full.sem, 1)

        def act_copy_xnT(act, l, it):
            act.wait_ge(*st.filled(l, it, "T"))
            nc.scalar.activation(xnT[:, :, :].rearrange("p k n -> p (k n)"), st.tile(l, "T")[:],
                                 ACT.Copy).then_inc(st.free["act"].sem, 1)

        def act_max_rows(act, l, it, g):
            act.wait_ge(*pm.filled(l, it, ("M", g)))
            act.wait_ge(*m_stored.at(l, it, 16 * max(0, g - 1)))
            nc.scalar.activation(mrow[:, g % 2, :], bank_m[0:8, 0:SEQ], ACT.Copy).then_inc(pm.free["act"].sem, 1)

        def act_exp(act, l, it, g, kt, hp, n=2 * SEQ):
            name = ("E", g, kt, hp)
            act.wait_ge(*st.filled(l, it, name))
            if hp == 0:
                act.wait_ge(*pv_done.at(l, it, max(0, TT * g + kt - 1)))
            nc.scalar.activation(probs[:, kt % 2, hp * 2 * SEQ:hp * 2 * SEQ + n], st.tile(l, name)[:, 0:n],
                                 ACT.Exp).then_inc(st.free["act"].sem, 1)

        def act0(act, it, step):
            l = 0
            step.begin(l, it)
            act_copy_xnT(act, l, it)
            for m in range(KT):
                for name, bias in (("Q", bq0), ("K", bk0)):
                    act.wait_ge(*sc.filled(l, it, f"{name}{m}"))
                    if m == 0 and name == "Q":
                        act.wait_ge(*split_two.at(l, it))
                    nc.scalar.activation(src0[:, SLOT0[f"{name}{m}"], :], sc.tile(l, f"{name}{m}")[:], ACT.Identity,
                                         bias=bias[:, m:m + 1]).then_inc(sc.free["act"].sem, 1)
                for name in ("Q", "K"):
                    act.wait_ge(*done(sc, l, it, f"{name}{m}"))
                    dst = tq[:, m, :] if name == "Q" else src0[:, SLOT0[f"KN{m}"], :]
                    nc.scalar.activation(dst, src0[:, SLOT0[f"{name}{m}"], :], ACT.Tanh).then_inc(tanh_ready.sem, 1)
            for m in range(KT):
                act.wait_ge(*sc.filled(l, it, f"J{m}"))
                act.wait_ge(*split_two.at(l, it, 3))
                nc.scalar.activation(src0[:, SLOT0[f"J{m}"], :], sc.tile(l, f"J{m}")[:],
                                     ACT.Copy).then_inc(sc.free["act"].sem, 1)
            for i in range(8):
                act.wait_ge(*sc.filled(l, it, ("H", i)))
                nc.scalar.activation(hid0[:, i, :], sc.tile(l, ("H", i))[:], ACT.Gelu,
                                     bias=b10[:, i:i + 1]).then_inc(sc.free["act"].sem, 1)
            act_max_rows(act, l, it, 0)
            for g in range(GROUPS):
                for kt in range(TT):
                    for hp in range(2):
                        act_exp(act, l, it, g, kt, hp)
                    if kt == 0 and g < GROUPS - 1:
                        act_max_rows(act, l, it, g + 1)
            step.end()

        def dve_split(dve, l, it, step, i, src, scale, ready, n=P):
            dve.wait_ge(*ready)
            fence(dve)
            dve.wait_ge(*parts_stored[i % 2].at(l, it, 16 * max(0, i // 2)))
            fence(dve)
            dve.wait_ge(*split_all.at(l, it, max(0, i - 1)))
            step.mark(nc.vector.tensor_scalar(parts[0:n, i % 2, 0, :], src, scale, None, ALU.mult))
            step.wait()
            step.mark(nc.vector.scalar_tensor_tensor(rest[0:n, i % 2, :], src, scale, parts[0:n, i % 2, 0, :],
                                                     ALU.mult, ALU.subtract))
            step.wait()
            nc.vector.tensor_copy(parts[0:n, i % 2, 1, :], rest[0:n, i % 2, :]).then_inc(split_two.sem, 1)

        def pool_split(pool, l, it, i, n=P):
            pool.wait_ge(*split_two.at(l, it, i + 1))
            nc.gpsimd.tensor_tensor(parts[0:n, i % 2, 2, :], rest[0:n, i % 2, :], parts[0:n, i % 2, 1, :],
                                    ALU.subtract).then_inc(split_all.sem, 1)

        def dve_values(dve, l, it, bias, n=NH):
            dve.wait_ge(*st.filled(l, it, "V"))
            for t in range(TT):
                src = st.tile(l, "V")[:, t * DIM:t * DIM + n * HD].rearrange("p (h e) -> p h e", e=HD)
                dst = vext[:, t, 0:n, 0:HD]
                if bias is None:
                    ins = nc.vector.tensor_copy(dst, src)
                else:
                    ins = nc.vector.tensor_tensor(dst, src, bias[:, :].rearrange("p (h e) -> p h e", e=HD), ALU.add)
            ins.then_inc(st.free["dve"].sem, 1)

        def dve_max(dve, l, it, step, g, i):
            name = ("S", g, i)
            h, qt = i // TT, i % TT
            dve.wait_ge(*sc.filled(l, it, name))
            nc.vector.tensor_reduce(nmax[:, g % 2, qt, h:h + 1], sc.tile(l, name)[:], AX, ALU.max,
                                    negate=True).then_inc(sc.free["dve"].sem, 1)

        def dve_split_max(dve, l, it, step, g, last):
            dve.wait_ge(*done(sc, l, it, last))
            step.mark(nc.vector.tensor_copy(msplit[:, g % 2, :, 0, :], nmax[:, g % 2, :, :]))
            step.wait()
            nc.vector.tensor_tensor(msplit[:, g % 2, :, 1, :], nmax[:, g % 2, :, :], msplit[:, g % 2, :, 0, :],
                                    ALU.subtract).then_inc(m_ready.sem, 1)

        def dve_normalise_heads(dve, l, it, step, g):
            dve.wait_ge(*pv_done.at(l, it, pv_done.per[l] // GROUPS * (g + 1)))
            fence(dve)
            step.mark(nc.vector.stream_shuffle(den[:], bank_u[:], [HD] * 32))
            step.wait()
            step.mark(nc.vector.reciprocal(rden[:], den[:]))
            step.wait()
            dve.wait_ge(*oc_loaded[g % 2].at(l, it, 16 * GH * (g // 2)))
            nc.vector.tensor_tensor(un[:, g % 2, :], bank_u[:], rden[:], ALU.mult).then_inc(pu.free["dve"].sem, 1)

        def dve_add_out(dve, l, it):
            dve.wait_ge(*st.filled(l, it, "OUT"))
            fence(dve)
            dve.wait_ge(*xres_ready.at(l, it, 1))
            flat = xres[:, :, :].rearrange("p t f -> p (t f)")
            nc.vector.tensor_tensor(flat, st.tile(l, "OUT")[:], flat, ALU.add).then_inc(st.free["dve"].sem, 1)

        def dve0(dve, it, step):
            l = 0
            step.begin(l, it)

            def split(i):
                name = SPLITS0[i]
                ready = tanh_ready.at(l, it, 2 + 2 * (i - 4)) if name[:2] == "KN" else done(sc, l, it, name)
                dve_split(dve, l, it, step, i, src0[:, SLOT0[name], :], 0.25 if name[0] == "Q" else 1.0, ready)

            for i in range(4):
                split(i)
            dve_values(dve, l, it, vbias)
            for i in range(4):
                hb, k = i // 2, i % 2
                dve.wait_ge(*sc.filled(l, it, ("W1", i)))
                nc.vector.tensor_tensor(w1e[:, k, hb * 512:(hb + 1) * 512], sc.tile(l, ("W1", i))[:],
                                        w1[:, k, hb * 512:(hb + 1) * 512], ALU.add).then_inc(sc.free["dve"].sem, 1)
            for i in range(4, 8):
                split(i)
            for i in range(4):
                dve.wait_ge(*sc.filled(l, it, ("W2", i)))
                nc.vector.tensor_tensor(w2e[:, 2 * i:2 * i + 2, :].rearrange("p a n -> p (a n)"), sc.tile(l, ("W2", i))[:],
                                        w2[:, 2 * i:2 * i + 2, :].rearrange("p a n -> p (a n)"),
                                        ALU.add).then_inc(sc.free["dve"].sem, 1)
            for g in range(2):
                for i in range(16):
                    dve_max(dve, l, it, step, g, i)
                dve_split_max(dve, l, it, step, g, ("S", g, 15))
            ln_stats(dve, l, it, step, 1)
            for g in range(GROUPS):
                if g + 2 < GROUPS:
                    for i in range(8):
                        dve_max(dve, l, it, step, g + 2, i)
                if g:
                    dve_normalise_heads(dve, l, it, step, g - 1)
                if g + 2 < GROUPS:
                    for i in range(8, 16):
                        dve_max(dve, l, it, step, g + 2, i)
                    dve_split_max(dve, l, it, step, g + 2, ("S", g + 2, 15))
                if g == 1:
                    dve.wait_ge(*rows_loaded.at(l, it, 64))
                    ln_normalise(dve, l, it, 1)
            dve_normalise_heads(dve, l, it, step, GROUPS - 1)
            dve_add_out(dve, l, it)
            step.end()

        def pool_residual(pool, l, it, step):
            pool.wait_ge(*x_loaded.at(l, it))
            pool.wait_ge(*y_stored.at(l, it))
            nc.gpsimd.tensor_tensor(xres[:], xl[:], bias_bc[:, 0:1, :].to_broadcast([P, TT, DIM]),
                                    ALU.add).then_inc(xres_ready.sem, 1)

        def pool0(pool, it, step):
            l = 0
            step.begin(l, it)
            pool_residual(pool, l, it, step)
            pool.wait_ge(*rows_loaded.at(l, it, 64))
            pool.wait_ge(*sc.full.at(l, it))
            fence(pool)
            for i in range(4):
                nc.gpsimd.tensor_scalar(ev1[:, i, :], rows[:, 0, :], lmask[:, i:i + 1], None,
                                        ALU.mult).then_inc(ev_ready.sem, 1)
                nc.gpsimd.tensor_scalar(ev2[:, :, 64 * i:64 * i + 64],
                                        rows[:, 2, :].rearrange("p (r j) -> p j r", j=4), lmask[:, i:i + 1], None,
                                        ALU.mult).then_inc(ev_ready.sem, 1)
            for i in range(8):
                pool_split(pool, l, it, i)
            ln_rsqrt(pool, l, it, step, 1)
            step.end()

        def sp_load_next(sp, l, it):
            sp.wait_ge(*xres_ready.at(l, it, 1))
            fence(sp)
            sp.wait_ge(*xn_ready.at(l, it))
            fence(sp)
            sp.wait_ge(xs_copied, 32)
            sp.wait_ge(*y_stored.at(l, it))
            fence(sp)
            sp.dma_start(xl[:], xs_tok[it + (BATCH * l + 1)]).then_inc(x_loaded.sem, 16)

        def sp_store_parts(sp, l, it, i, where):
            side, s, m = where
            sp.wait_ge(*split_all.at(l, it, i + 1))
            sp.dma_start(parts_dram[side, :, s, m * P:(m + 1) * P, :].rearrange("a f n -> f a n"),
                         parts[:, i % 2, :, :]).then_inc(parts_stored[i % 2].sem, 16)

        def sp_max_rows(sp, l, it, g, q_rows):
            sp.wait_ge(*done(pm, l, it, ("M", g)))
            sp.dma_start(m_dram[g], mrow[:, g % 2, :]).then_inc(m_stored.sem, 16)
            sp.wait_ge(*m_stored.at(l, it, 16 * (g + 1)))
            sp.dma_start(q_rows(g), m_dram[g].rearrange("(a h) n -> a h n", a=2)).then_inc(m_loaded[g % 2].sem, 16)

        def sp_gather_heads(sp, l, it, g):
            sp.wait_ge(*done(pu, l, it, ("U", g)))
            for h in range(GH):
                at = 64 * (g % 2) + HD * h
                sp.dma_start(oc[at:at + HD, g // 2, :], un[32 * h:32 * h + HD, g % 2, :])\
                  .then_inc(oc_loaded[g % 2].sem, 16)

        def sp_store_out(sp, l, it):
            sp.wait_ge(*done(st, l, it, "OUT"))
            fence(sp)
            dst = xs_tok[it + BATCH * (l + 1)] if l < LAYERS - 1 else out_tok[it]
            sp.dma_start(dst, xres[:]).then_inc(y_stored.sem, 16)

        def sp0(sp, it):
            l = 0
            for j, first in enumerate((1, 2, 9, 10)):
                if j == 0:
                    sp.wait_ge(*xn_ready.at(l, it))
                    fence(sp)
                    sp.wait_ge(*sc.full.at(l, it))
                    fence(sp)
                    sp.wait_ge(*ev_ready.at(l, it))
                sp.dma_start(rows[:, j, :], xn[first:first + 7:2, 0, 0:DIM]).then_inc(rows_loaded.sem, 16)
            for i in range(8):
                sp_store_parts(sp, l, it, i, WHERE0[SPLITS0[i]])

            def stack(g):
                if g < 3:
                    sp.wait_ge(*st.full.at(l, it))
                    fence(sp)
                else:
                    sp.wait_ge(*st.filled(l, it, ("E", g - 3, TT - 1, 1)))
                for prods, tiles in ((PRODUCTS_A, (q_a, k_a)), (PRODUCTS_B, (q_b, k_b))):
                    for n, pair in enumerate(prods):
                        for side in range(2):
                            src = parts_dram[side, pair[side]].rearrange("s (e h) n -> (s e) h n", h=NH)
                            sp.dma_start(tiles[side][32 * n:32 * n + 32, g % 3, :, :], src[:, GH * g:GH * g + GH, :])\
                              .then_inc(stack_loaded[g].sem, 16)

            for i in range(2):
                sp.wait_ge(*parts_stored[i].at(l, it, 16 * 4))
                fence(sp)
            for g in range(3):
                stack(g)
            sp_load_next(sp, l, it)

            def q_rows(g):
                return q_a[96:98, g % 3, :, :]

            sp_max_rows(sp, l, it, 0, q_rows)
            sp_max_rows(sp, l, it, 1, q_rows)
            stack(3)
            sp_gather_heads(sp, l, it, 0)
            sp_max_rows(sp, l, it, 2, q_rows)
            sp_gather_heads(sp, l, it, 1)
            sp_max_rows(sp, l, it, 3, q_rows)
            sp_gather_heads(sp, l, it, 2)
            sp_gather_heads(sp, l, it, 3)
            sp_store_out(sp, l, it)

        l1 = ExitStack()
        q_1 = sb("q_1", [P, GROUPS, GH, SEQ], BF16, l1)
        k_1 = sb("k_1", [P, GROUPS, SEQ], BF16, l1)
        raw1 = sb("raw1", [P, 2, SEQ], F32, l1)
        rawk = sb("rawk", [32, 2, SEQ], F32, l1)
        rot1 = sb("rot1", [P, 2, SEQ], F32, l1)
        rotk = sb("rotk", [32, 2, SEQ], F32, l1)
        mul1 = sb("mul1", [P, 4, SEQ], F32, l1)
        mulk = sb("mulk", [32, 4, SEQ], F32, l1)
        wq1 = sb("wq1", [P, KT, DIM], F32, l1)
        wk1 = sb("wk1", [P, KT, 64], F32, l1)
        wv1 = sb("wv1", [P, KT, 64], F32, l1)
        wo1 = sb("wo1", [P, KT, DIM], F32, l1)
        cos1 = sb("cos1", [P, SEQ], F32, l1)
        sin1 = sb("sin1", [P, SEQ], F32, l1)
        cosk = sb("cosk", [32, SEQ], F32, l1)
        sink = sb("sink", [32, SEQ], F32, l1)
        w1x = sb("w1x", [P, KT, P], F32, l1)
        w1s = sb("w1s", [P, KT, P], F32, l1)
        b11 = sb("b11", [P, 1], F32, l1)
        w21 = sb("w21", [P, 64], F32, l1)
        b21 = sb("b21", [P, 64], F32, l1)
        tau = sb("tau", [P, 4], F32, l1)
        wih = sb("wih", [P, KT, 3 * DIM], F32, l1)
        whh = sb("whh", [P, KT, 3 * DIM], F32, l1)
        bih = sb("bih", [P, 6], F32, l1)
        bhh = sb("bhh", [P, 6], F32, l1)
        wvs = sb("wvs", [P, KT, DIM], F32, l1)
        bvs = sb("bvs", [P, KT], F32, l1)
        wos = sb("wos", [P, KT, DIM], F32, l1)
        slots = sb("slots", [64, DIM], F32, l1)
        slot_scale = sb("slot_scale", [64, 1], F32, l1)
        sixty_fourth = sb("sixty_fourth", [64, 2], F32, l1)
        ones_sq = sb("ones_sq", [P, P], F32, l1)
        slot_mean = sb("slot_mean", [P, KT], F32, l1)
        hsT = sb("hsT", [P, KT, 64], F32, l1)
        ghb = sb("ghb", [P, 6, 64], F32, l1)
        hid1 = sb("hid1", [P, SEQ], F32, l1)
        logits = sb("logits", [P, TT, 64], F32, l1)
        logits_r = sb("logits_r", [P, TT, 64], F32, l1)
        top = sb("top", [P, TT, 8], F32, l1)
        ntop = sb("ntop", [P, TT], F32, l1)
        e_all = sb("e_all", [P, TT, 64], F32, l1)
        e_rest = sb("e_rest", [P, TT, 64], F32, l1)
        asum = sb("asum", [P, 2, TT], F32, l1)
        alpha = sb("alpha", [P, TT, 64], F32, l1)
        alphaT = sb("alphaT", [64, SEQ], F32, l1)
        wsum = sb("wsum", [P, 2, 64], F32, l1)
        gi = sb("gi", [P, KT, 64], F32, l1)
        rz = sb("rz", [P, 4, 64], F32, l1)
        gru = sb("gru", [P, 6, 64], F32, l1)
        h_new = sb("h_new", [P, KT, 64], F32, l1)
        svT = sb("svT", [P, KT, 64], F32, l1)
        sv2 = sb("sv2", [64, DIM], F32, l1)
        l1.close()

        def bc(name, n, parts_n=P):
            return d[name].rearrange("(a n) -> a n", a=1).to_broadcast([parts_n, n])

        loads1 = [(wq1, d["wq1"]), (wk1, d["wk1"]), (wv1, d["wv1"]), (cos1, d["cos1"]), (sin1, d["sin1"]),
                  (cosk, d["cosk"]), (sink, d["sink"]), (w1x, d["w1x"]), (w1s, d["w1s"]), (b11, d["b11"]),
                  (w21, d["w21"]), (b21, bc("b21", 64)), (slots, d["slots"]), (slot_scale, d["slot_scale"]),
                  (whh, d["whh"]), (bih, d["bih"]), (bhh, d["bhh"]), (wih, d["wih"]), (wvs, d["wvs"]),
                  (bvs, d["bvs"]), (wos, d["wos"]), (wo1, d["wo1"])]
        loaded1 = sem("loaded1")
        N1 = 16 * (len(loads1) + 2)
        pe_set1, dve_set1, dve_pre1 = sem("pe_set1"), sem("dve_set1"), sem("dve_pre1")
        layer_left = [sem(f"layer_left{i}") for i in range(3)]
        logits_done = sig("logits_done", [0, 2, 0, 0], "vector")
        e_done = sig("e_done", [0, 1, 0, 0], "scalar")
        alpha_done = sig("alpha_done", [0, 1, 0, 0], "vector")
        gi_done = sig("gi_done", [0, 1, 0, 0], "vector")
        gates_in = sig("gates_in", [0, 2, 0, 0], "vector")
        gates_out = sig("gates_out", [0, 2, 0, 0], "scalar")
        h_done = sig("h_done", [0, 1, 0, 0], "vector")
        rotated = sig("rotated", [0, 4, 0, 0], "vector")

        def sp_setup1(sp):
            sp.wait_ge(*y_stored.at(1, 0))
            for dst, src in loads1:
                sp.dma_start(dst[:], src).then_inc(loaded1, 16)
            sp.dma_start(bias_bc[:, 0, :], bc("bo1", DIM)).then_inc(loaded1, 16)
            sp.dma_start(tau[:, 0:1], bc("tau", 1)).then_inc(loaded1, 16)

        def pe_setup1(pe):
            pe.wait_ge(dve_pre1, 5)
            for f in range(KT):
                nc.tensor.transpose(banks[0][:, f * 64:(f + 1) * 64], slots[:, f * P:(f + 1) * P], ident[0:64, 0:64])
            for f in range(KT):
                ins = nc.tensor.matmul(banks[0][:, 2 * P + f:2 * P + f + 1], slots[:, f * P:(f + 1) * P],
                                       sixty_fourth[:, 0:1], start=True, stop=True)
            ins.then_inc(pe_set1, 1)
            pe.wait_ge(dve_set1, 2)
            for k in range(KT):
                nc.tensor.matmul(banks[1][:, 0:1], w1s[:, k, :], slot_mean[:, k:k + 1], start=(k == 0), stop=(k == 1))
            for j in range(6):
                for k in range(KT):
                    ins = nc.tensor.matmul(banks[1][:, 64 + j * 64:128 + j * 64] if j < 6 else None,
                                           whh[:, k, j * P:(j + 1) * P], hsT[:, k, :], start=(k == 0), stop=(k == 1))
            ins.then_inc(pe_set1, 1)

        def dve_setup1(dve):
            dve.wait_ge(loaded1, N1)
            nc.vector.tensor_scalar(slots[:], slots[:], slot_scale[:, 0:1], None, ALU.mult).then_inc(dve_pre1, 1)
            nc.vector.memset(sixty_fourth[:], 1.0 / 64).then_inc(dve_pre1, 1)
            nc.vector.memset(ones_sq[:], 1.0).then_inc(dve_pre1, 1)
            nc.vector.memset(k_1[96:98, :, :], 1.0).then_inc(dve_pre1, 1)
            nc.vector.tensor_scalar(tau[:, 1:2], tau[:, 0:1], -1.0, None, ALU.mult).then_inc(dve_pre1, 1)
            dve.wait_ge(dve_pre1, 5)
            nc.vector.tensor_tensor(tau[:, 2:3], tau[:, 0:1], tau[:, 1:2], ALU.max).then_inc(dve_pre1, 1)
            dve.wait_ge(dve_pre1, 6)
            nc.vector.tensor_scalar(tau[:, 2:3], tau[:, 2:3], 0.1, None, ALU.add).then_inc(dve_pre1, 1)
            dve.wait_ge(dve_pre1, 7)
            nc.vector.reciprocal(tau[:, 3:4], tau[:, 2:3]).then_inc(dve_pre1, 1)
            dve.wait_ge(dve_pre1, 8)
            nc.vector.tensor_scalar(b21[:], b21[:], tau[:, 3:4], None, ALU.mult).then_inc(dve_pre1, 1)
            dve.wait_ge(pe_set1, 1)
            nc.vector.tensor_copy(hsT[:, :, :].rearrange("p k n -> p (k n)"), banks[0][:, 0:P]).then_inc(dve_set1, 1)
            nc.vector.tensor_copy(slot_mean[:], banks[0][:, 2 * P:2 * P + KT]).then_inc(dve_set1, 1)
            dve.wait_ge(pe_set1, 2)
            nc.vector.tensor_tensor(b11[:], banks[1][:, 0:1], b11[:], ALU.add).then_inc(dve_set1, 1)
            nc.vector.tensor_tensor(ghb[:], banks[1][:, 64:448].rearrange("p (j n) -> p j n", j=6),
                                    bhh[:, :, None].to_broadcast([P, 6, 64]), ALU.add).then_inc(dve_set1, 1)
            dve.wait_ge(dve_set1, 4)
            nc.vector.tensor_tensor(ghb[:, 0:4, :], ghb[:, 0:4, :], bih[:, 0:4, None].to_broadcast([P, 4, 64]),
                                    ALU.add).then_inc(dve_set1, 1)
            dve.wait_ge(dve_set1, 5)
            dve.wait_ge(dve_pre1, 9)

        def kv_of_group(g, h):
            return g

        def pe1(pe, it):
            l = 1
            pe_transpose_xn(pe, l, it)
            pe.wait_ge(*done(st, l, it, "T"))
            pe_project(pe, l, it, "QE", wq1, 0)
            pe_project(pe, l, it, "QO", wq1, 1)
            pe_project(pe, l, it, "KK", wk1, 0, 64)
            pe_values(pe, l, it, wv1)
            pe_project(pe, l, it, "H", w1x, 0)
            for s in sc.vacated(l, it, "L"):
                pe.wait_ge(*s)
            pe.wait_ge(*done(sc, l, it, "H"))
            for t in range(TT):
                ins = nc.tensor.matmul(sc.tile(l, "L")[:, t * 64:(t + 1) * 64], hid1[:, t * P:(t + 1) * P], w21[:],
                                       start=True, stop=True)
            ins.then_inc(sc.full.sem, 1)

            def q(g, h):
                return q_1[0:96, g, h, :]

            def k(g, h):
                return k_1[0:96, g, :]

            def passes(g, h):
                return [(k_1[0:98, g, :], q_1[0:98, g, h, :])]

            for g in range(2):
                for i in range(16):
                    pe_scores(pe, l, it, g, i, q, k)
            pe_max_rows(pe, l, it, 0)
            for g in range(GROUPS):
                for kt in range(TT):
                    pe_scores_t(pe, l, it, g, kt, passes)
                    if kt == 0 and g < GROUPS - 1:
                        pe_max_rows(pe, l, it, g + 1)
                    if g + 2 < GROUPS:
                        for i in range(4):
                            pe_scores(pe, l, it, g + 2, 4 * kt + i, q, k)
                    if g or kt:
                        pe_weigh(pe, l, it, GROUPS * g + kt - 1, kv_of_group)
                if g == 0:
                    for s in sc.vacated(l, it, "AT"):
                        pe.wait_ge(*s)
                    pe.wait_ge(*alpha_done.at(l, it, 1))
                    fence(pe)
                    for t in range(TT):
                        ins = nc.tensor.transpose(sc.tile(l, "AT")[0:64, t * P:(t + 1) * P], alpha[:, t, :], ident[:])
                    ins.then_inc(sc.full.sem, 1)
                    for s in sc.vacated(l, it, "SI"):
                        pe.wait_ge(*s)
                    for f in range(KT + 1):
                        for t in range(TT):
                            lhs = xn[:, t, f * P:(f + 1) * P] if f < KT else ones_sq[:]
                            ins = nc.tensor.matmul(sc.tile(l, "SI")[:, f * 64:(f + 1) * 64], lhs, alpha[:, t, :],
                                                   start=(t == 0), stop=(t == TT - 1))
                    ins.then_inc(sc.full.sem, 1)
                if g == 1:
                    for s in sc.vacated(l, it, "GX"):
                        pe.wait_ge(*s)
                    pe.wait_ge(*gi_done.at(l, it, 1))
                    for j in range(6):
                        for k_ in range(KT):
                            ins = nc.tensor.matmul(sc.tile(l, "GX")[:, j * 64:(j + 1) * 64], wih[:, k_, j * P:(j + 1) * P],
                                                   gi[:, k_, :], start=(k_ == 0), stop=(k_ == 1))
                    ins.then_inc(sc.full.sem, 1)
                if g == 2:
                    for s in sc.vacated(l, it, "SV"):
                        pe.wait_ge(*s)
                    pe.wait_ge(*h_done.at(l, it, 1))
                    for m in range(KT):
                        for k_ in range(KT):
                            ins = nc.tensor.matmul(sc.tile(l, "SV")[:, m * 64:(m + 1) * 64], wvs[:, k_, m * P:(m + 1) * P],
                                                   h_new[:, k_, :], start=(k_ == 0), stop=(k_ == 1))
                    ins.then_inc(sc.full.sem, 1)
            for s in sc.vacated(l, it, "Z2"):
                pe.wait_ge(*s)
            pe.wait_ge(*done(sc, l, it, "SV"))
            for k_ in range(KT):
                ins = nc.tensor.matmul(sc.tile(l, "Z2")[0:64, 0:DIM], svT[:, k_, :], wos[:, k_, :],
                                       start=(k_ == 0), stop=(k_ == 1))
            ins.then_inc(sc.full.sem, 1)
            pe_weigh(pe, l, it, GROUPS * TT - 1, kv_of_group)
            for s in st.vacated(l, it, "OUT"):
                pe.wait_ge(*s)
            pe.wait_ge(*done(sc, l, it, "Z2"))
            for t in range(TT):
                nc.tensor.matmul(st.tile(l, "OUT")[:, t * DIM:(t + 1) * DIM], alphaT[:, t * P:(t + 1) * P], sv2[:],
                                 start=(t % 2 == 0), stop=False)
            pe_out_heads(pe, l, it, wo1)

        def act1(act, it, step):
            l = 1
            step.begin(l, it)
            act_copy_xnT(act, l, it)
            for m, name in enumerate(("QE", "QO")):
                act.wait_ge(*sc.filled(l, it, name))
                nc.scalar.activation(raw1[:, m, :], sc.tile(l, name)[:], ACT.Copy).then_inc(sc.free["act"].sem, 1)
            act.wait_ge(*sc.filled(l, it, "KK"))
            nc.scalar.activation(rawk[:, 0, :], sc.tile(l, "KK")[0:32, :], ACT.Copy)
            nc.scalar.activation(rawk[:, 1, :], sc.tile(l, "KK")[32:64, :], ACT.Copy).then_inc(sc.free["act"].sem, 1)
            act.wait_ge(*sc.filled(l, it, "H"))
            nc.scalar.activation(hid1[:], sc.tile(l, "H")[:], ACT.Gelu, bias=b11[:, 0:1]).then_inc(sc.free["act"].sem, 1)
            act.wait_ge(*logits_done.at(l, it, 2))
            for t in range(TT):
                nc.scalar.activation(e_all[:, t, :], logits[:, t, :], ACT.Exp, bias=ntop[:, t:t + 1])
                ins = nc.scalar.activation(e_rest[:, t, :], logits_r[:, t, :], ACT.Exp, bias=ntop[:, t:t + 1])
            ins.then_inc(e_done.sem, 1)
            act_max_rows(act, l, it, 0)
            for g in range(GROUPS):
                for kt in range(TT):
                    for hp in range(2):
                        act_exp(act, l, it, g, kt, hp)
                    if kt == 0 and g < GROUPS - 1:
                        act_max_rows(act, l, it, g + 1)
                if g == 0:
                    act.wait_ge(*sc.filled(l, it, "AT"))
                    nc.scalar.activation(alphaT[:], sc.tile(l, "AT")[0:64, :], ACT.Copy).then_inc(sc.free["act"].sem, 1)
                if g == 1:
                    act.wait_ge(*gates_in.at(l, it, 1))
                    nc.scalar.activation(rz[:], rz[:], ACT.Tanh, scale=0.5).then_inc(gates_out.sem, 1)
                    act.wait_ge(*gates_in.at(l, it, 2))
                    for j in range(2):
                        ins = nc.scalar.activation(gru[:, 2 + j, :], gru[:, j, :], ACT.Tanh, bias=bih[:, 4 + j:5 + j])
                    ins.then_inc(gates_out.sem, 1)
                if g == 2:
                    act.wait_ge(*sc.filled(l, it, "SV"))
                    for m in range(KT):
                        ins = nc.scalar.activation(svT[:, m, :], sc.tile(l, "SV")[:, m * 64:(m + 1) * 64], ACT.Identity,
                                                   bias=bvs[:, m:m + 1])
                    ins.then_inc(sc.free["act"].sem, 1)
            act.wait_ge(*sc.filled(l, it, "Z2"))
            nc.scalar.activation(sv2[:], sc.tile(l, "Z2")[0:64, 0:DIM], ACT.Copy).then_inc(sc.free["act"].sem, 1)
            step.end()

        def dve1(dve, it, step):
            l = 1
            step.begin(l, it)

            def rotate(raw, mul, rot, cos, sin):
                for j, (m, table) in enumerate(((0, cos), (1, sin), (0, sin), (1, cos))):
                    step.mark(nc.vector.tensor_tensor(mul[:, j, :], raw[:, m, :], table[:], ALU.mult))
                step.wait()
                nc.vector.tensor_tensor(rot[:, 0, :], mul[:, 0, :], mul[:, 1, :], ALU.subtract).then_inc(rotated.sem, 1)
                nc.vector.tensor_tensor(rot[:, 1, :], mul[:, 2, :], mul[:, 3, :], ALU.add).then_inc(rotated.sem, 1)

            dve.wait_ge(*done(sc, l, it, "QO"))
            rotate(raw1, mul1, rot1, cos1, sin1)
            for m in range(2):
                dve_split(dve, l, it, step, m, rot1[:, m, :], 1.0 / 16, rotated.at(l, it, 2))
            dve.wait_ge(*done(sc, l, it, "KK"))
            rotate(rawk, mulk, rotk, cosk, sink)
            for m in range(2):
                dve_split(dve, l, it, step, 2 + m, rotk[:, m, :], 1.0, rotated.at(l, it, 4), 32)
            dve_values(dve, l, it, None, 4)
            dve.wait_ge(*sc.filled(l, it, "L"))
            nc.vector.scalar_tensor_tensor(logits[:], sc.tile(l, "L")[:, 0:256].rearrange("p (t n) -> p t n", t=TT),
                                           tau[:, 3:4], b21[:, None, :].to_broadcast([P, TT, 64]),
                                           ALU.mult, ALU.add).then_inc(sc.free["dve"].sem, 1)
            dve.wait_ge(*done(sc, l, it, "L"))
            fence(dve)
            for t in range(TT):
                step.mark(nc.vector.max(top[:, t, :], logits[:, t, :]))
            step.wait()
            nc.vector.tensor_scalar(ntop[:], top[:, :, 0], -1.0, None, ALU.mult).then_inc(logits_done.sem, 1)
            for t in range(TT):
                ins = nc.vector.match_replace(logits_r[:, t, :], top[:, t, :], logits[:, t, :], -1e30)
            ins.then_inc(logits_done.sem, 1)
            for i in range(16):
                dve_max(dve, l, it, step, 0, i)
            dve_split_max(dve, l, it, step, 0, ("S", 0, 15))
            dve.wait_ge(*e_done.at(l, it, 1))
            step.mark(nc.vector.tensor_tensor(e_all[:], e_all[:], e_rest[:], ALU.subtract))
            step.wait()
            step.mark(nc.vector.tensor_reduce(asum[:, 0, :], e_all[:], AX, ALU.add))
            step.wait()
            step.mark(nc.vector.reciprocal(asum[:, 1, :], asum[:, 0, :]))
            step.wait()
            nc.vector.tensor_tensor(alpha[:], e_all[:], asum[:, 1, :, None].to_broadcast([P, TT, 64]),
                                    ALU.mult).then_inc(alpha_done.sem, 1)
            for i in range(16):
                dve_max(dve, l, it, step, 1, i)
            dve_split_max(dve, l, it, step, 1, ("S", 1, 15))
            ln_stats(dve, l, it, step, 1)
            for g in range(GROUPS):
                if g + 2 < GROUPS:
                    for i in range(8):
                        dve_max(dve, l, it, step, g + 2, i)
                if g:
                    dve_normalise_heads(dve, l, it, step, g - 1)
                if g + 2 < GROUPS:
                    for i in range(8, 16):
                        dve_max(dve, l, it, step, g + 2, i)
                    dve_split_max(dve, l, it, step, g + 2, ("S", g + 2, 15))
                if g == 0:
                    dve.wait_ge(*sc.filled(l, it, "SI"))
                    step.mark(nc.vector.tensor_scalar(wsum[:, 0, :], sc.tile(l, "SI")[:, 128:192], 1e-8, None, ALU.add))
                    step.wait()
                    step.mark(nc.vector.reciprocal(wsum[:, 1, :], wsum[:, 0, :]))
                    step.wait()
                    step.mark(nc.vector.tensor_tensor(gi[:], sc.tile(l, "SI")[:, 0:128].rearrange("p (k n) -> p k n", k=KT),
                                                      wsum[:, 1:2, :].to_broadcast([P, KT, 64]), ALU.mult))
                    step.wait()
                    dve.sem_inc(gi_done.sem, 1)
                    dve.sem_inc(sc.free["dve"].sem, 1)
                    ln_normalise(dve, l, it, 1)
                if g == 1:
                    gx = sc.tile(l, "GX")[:, 0:384].rearrange("p (j n) -> p j n", j=6)
                    dve.wait_ge(*sc.filled(l, it, "GX"))
                    nc.vector.tensor_tensor(rz[:], gx[:, 0:4, :], ghb[:, 0:4, :], ALU.add).then_inc(gates_in.sem, 1)
                    dve.wait_ge(*gates_out.at(l, it, 1))
                    step.mark(nc.vector.tensor_scalar(rz[:], rz[:], 0.5, 0.5, ALU.mult, ALU.add))
                    step.wait()
                    step.mark(nc.vector.tensor_tensor(gru[:, 4:6, :], rz[:, 0:2, :], ghb[:, 4:6, :], ALU.mult))
                    step.wait()
                    step.mark(nc.vector.tensor_tensor(gru[:, 0:2, :], gx[:, 4:6, :], gru[:, 4:6, :], ALU.add))
                    step.wait()
                    dve.sem_inc(gates_in.sem, 1)
                    dve.sem_inc(sc.free["dve"].sem, 1)
                    dve.wait_ge(*gates_out.at(l, it, 2))
                    step.mark(nc.vector.tensor_tensor(gru[:, 4:6, :], hsT[:], gru[:, 2:4, :], ALU.subtract))
                    step.wait()
                    step.mark(nc.vector.tensor_tensor(gru[:, 4:6, :], gru[:, 4:6, :], rz[:, 2:4, :], ALU.mult))
                    step.wait()
                    nc.vector.tensor_tensor(h_new[:], gru[:, 4:6, :], gru[:, 2:4, :], ALU.add).then_inc(h_done.sem, 1)
            dve_normalise_heads(dve, l, it, step, GROUPS - 1)
            dve_add_out(dve, l, it)
            step.end()

        def pool1(pool, it, step):
            l = 1
            step.begin(l, it)
            pool_residual(pool, l, it, step)
            for i in range(4):
                pool_split(pool, l, it, i, P if i < 2 else 32)
            ln_rsqrt(pool, l, it, step, 1)
            step.end()

        def sp1(sp, it):
            l = 1
            for i in range(4):
                side, s = i // 2, i % 2
                sp.wait_ge(*split_all.at(l, it, i + 1))
                n = P if i < 2 else 32
                sp.dma_start(parts_dram[side, :, 0, s * n:(s + 1) * n, :].rearrange("a f n -> f a n"),
                             parts[0:n, i % 2, :, :]).then_inc(parts_stored[i % 2].sem, 16)
            for i in range(2):
                sp.wait_ge(*parts_stored[i].at(l, it, 16 * 2))
                fence(sp)
            sp.wait_ge(*st.full.at(l, it))
            for n, (qp, kp) in enumerate(PRODUCTS_A + PRODUCTS_B):
                sp.dma_start(q_1[16 * n:16 * n + 16, :, :, :].rearrange("e g h n -> e (g h) n"),
                             parts_dram[0, qp, 0].rearrange("(e h) n -> e h n", h=NH)).then_inc(stack_loaded[0].sem, 16)
                sp.dma_start(k_1[16 * n:16 * n + 16, :, :],
                             parts_dram[1, kp, 0, 0:64, :].rearrange("(e h) n -> e h n", h=4)).then_inc(stack_loaded[0].sem, 16)
            sp_load_next(sp, l, it)

            def q_rows(g):
                return q_1[96:98, g, :, :]

            sp_max_rows(sp, l, it, 0, q_rows)
            sp_max_rows(sp, l, it, 1, q_rows)
            sp_gather_heads(sp, l, it, 0)
            sp_max_rows(sp, l, it, 2, q_rows)
            sp_gather_heads(sp, l, it, 1)
            sp_max_rows(sp, l, it, 3, q_rows)
            sp_gather_heads(sp, l, it, 2)
            sp_gather_heads(sp, l, it, 3)
            sp_store_out(sp, l, it)

        l3 = ExitStack()
        q_3 = sb("q_3", [P, GROUPS, GH, SEQ], BF16, l3)
        k_3 = sb("k_3", [P, GROUPS, GH, SEQ], BF16, l3)
        src3 = sb("src3", [P, 4, SEQ], F32, l3)
        wq3 = sb("wq3", [P, KT, DIM], F32, l3)
        wk3 = sb("wk3", [P, KT, DIM], F32, l3)
        wv3 = sb("wv3", [P, KT, DIM], F32, l3)
        wo3 = sb("wo3", [P, KT, DIM], F32, l3)
        mask_q = sb("mask_q", [P, 3, DIM], BF16, l3)
        mask_k = sb("mask_k", [P, 2, DIM], BF16, l3)
        gamma = sb("gamma", [P, KT], F32, l3)
        beta = sb("beta", [P, KT], F32, l3)
        hn = sb("hn", [P, TT, DIM], F32, l3)
        hT = sb("hT", [P, KT, SEQ], F32, l3)
        stats3 = sb("stats3", [P, TT, 6], F32, l3)
        mv3 = sb("mv3", [P, TT, 2], F32, l3)
        veps3 = sb("veps3", [P, TT], F32, l3)
        rstd3 = sb("rstd3", [P, TT], F32, l3)
        fc1 = sb("fc1", [P, KT, 1024], F32, l3)
        fc2 = sb("fc2", [P, 8, DIM], F32, l3)
        fc1_b = sb("fc1_b", [P, 8], F32, l3)
        raw = ExitStack()
        fc1_q = sb("fc1_q", [P, KT * 1024], I32, raw)
        fc1_s = sb("fc1_s", [P, KT * 1024], F32, raw)
        fc2_q = sb("fc2_q", [P, 8 * DIM], I32, raw)
        fc2_s = sb("fc2_s", [P, 8 * DIM], F32, raw)
        raw.close()
        hid3 = sb("hid3", [P, 8, SEQ], F32, l3)
        probs3 = sb("probs3", [P, 2, GH, 896], F32, l3)
        l3.close()
        attn.close()

        loads3 = [(wq3, d["wq3"]), (wk3, d["wk3"]), (wv3, d["wv3"]), (mask_q, d["mask_q"]), (mask_k, d["mask_k"]),
                  (gamma, d["gamma"]), (beta, d["beta"]), (fc1_q, d["fc1_q"]), (fc1_s, bc("fc1_s", KT * 1024)),
                  (fc1_b, d["fc1_b"]), (fc2_q, d["fc2_q"]), (fc2_s, bc("fc2_s", 8 * DIM)), (wo3, d["wo3"])]
        loaded3 = sem("loaded3")
        N3 = 16 * (len(loads3) + 1)
        dve_set3, pool_set3 = sem("dve_set3"), sem("pool_set3")
        moments3 = sig("moments3", [0, 0, 0, TT], "vector")
        rstd3_ready = sig("rstd3_ready", [0, 0, 0, 1], "gpsimd")
        hn_ready = sig("hn_ready", [0, 0, 0, TT], "vector")

        def sp_setup3(sp):
            sp.wait_ge(*y_stored.at(3, 0))
            for dst, src in loads3:
                sp.dma_start(dst[:], src).then_inc(loaded3, 16)
            sp.dma_start(bias_bc[:, 0, :], bc("fc2_b", DIM)).then_inc(loaded3, 16)

        def dve_setup3(dve):
            dve.wait_ge(loaded3, N3)
            nc.vector.memset(k_3[96:98, :, :, :], 1.0).then_inc(dve_set3, 1)
            nc.vector.scalar_tensor_tensor(fc1[:, :, :].rearrange("p k n -> p (k n)"), fc1_q[:], -128.0, fc1_s[:],
                                           ALU.add, ALU.mult).then_inc(dve_set3, 1)
            nc.vector.tensor_scalar(fc2_s[:], fc2_s[:], 0.5, None, ALU.mult).then_inc(dve_set3, 1)
            dve.wait_ge(dve_set3, 3)
            nc.vector.scalar_tensor_tensor(fc2[:, :, :].rearrange("p k n -> p (k n)"), fc2_q[:], -128.0, fc2_s[:],
                                           ALU.add, ALU.mult).then_inc(dve_set3, 1)

        def pool_setup3(pool):
            pool.wait_ge(loaded3, N3)
            nc.gpsimd.memset(vext[:, :, :, HD:32], 1.0).then_inc(pool_set3, 1)
            nc.gpsimd.tensor_scalar(bias_bc[:, 0, :], bias_bc[:, 0, :], 0.5, None, ALU.mult).then_inc(pool_set3, 1)

        def pe3(pe, it):
            l = 3
            pe_transpose_xn(pe, l, it)
            pe.wait_ge(*done(st, l, it, "T"))
            pe_project(pe, l, it, "Q0", wq3, 0)
            pe_project(pe, l, it, "K0", wk3, 0)
            pe_project(pe, l, it, "Q1", wq3, 1)
            pe_project(pe, l, it, "K1", wk3, 1)
            pe_values(pe, l, it, wv3)
            for s in st.vacated(l, it, "T2"):
                pe.wait_ge(*s)
            pe.wait_ge(*hn_ready.at(l, it, TT))
            for f in range(KT):
                for t in range(TT):
                    ins = nc.tensor.transpose(st.tile(l, "T2")[:, f * SEQ + t * P:f * SEQ + (t + 1) * P],
                                              hn[:, t, f * P:(f + 1) * P], ident[:])
            ins.then_inc(st.full.sem, 1)

            def hidden(i):
                if i == 0:
                    pe.wait_ge(*done(st, l, it, "T2"))
                pe_project(pe, l, it, ("H", i), fc1, i, P, hT)

            def scores(g, i):
                h, j = i // 2, i % 2
                name = ("S", g, i)
                if g == 0 and i == 0:
                    pe.wait_ge(*stack_loaded[0].at(l, it, stack_loaded[0].per[l]))
                for s in sc.vacated(l, it, name):
                    pe.wait_ge(*s)
                tile = sc.tile(l, name)
                nc.tensor.matmul(tile[:], ident_bf[:], mask_q[:, j:j + 2, :].rearrange("p a n -> p (a n)"),
                                 start=True, stop=False)
                for n in range(2):
                    qt = 2 * j + n
                    first = max(0, qt - 1) * P
                    width = (qt + 1) * P - first
                    ins = nc.tensor.matmul(tile[:, (n + 1) * DIM - width:(n + 1) * DIM], q_3[0:96, g, h, qt * P:(qt + 1) * P],
                                           k_3[0:96, g, h, first:first + width], start=False, stop=(n == 1))
                ins.then_inc(sc.full.sem, 1)

            def scores_t(g, h):
                name = ("E", g, h)
                if h == 0:
                    pe.wait_ge(*m_loaded[g % 2].at(l, it, 16 * (g // 2 + 1)))
                for s in st.vacated(l, it, name):
                    pe.wait_ge(*s)
                tile = st.tile(l, name)
                mask = mask_k[:, :, :].rearrange("p a n -> p (a n)")
                for j in range(2):
                    n = SEQ - P * j
                    nc.tensor.matmul(tile[:, j * SEQ:j * SEQ + n], ident_bf[:], mask[:, 0:n], start=True, stop=False)
                    for kt in (2 * j, 2 * j + 1):
                        w = min(2 * P, SEQ - kt * P)
                        ins = nc.tensor.matmul(tile[:, kt * DIM:kt * DIM + w], k_3[0:98, g, h, kt * P:(kt + 1) * P],
                                               q_3[0:98, g, h, kt * P:kt * P + w], start=False, stop=(kt % 2 == 1))
                ins.then_inc(st.full.sem, 1)

            def weigh(g):
                pe.wait_ge(*done(st, l, it, ("E", g, GH - 1)))
                for s in pu.vacated(l, it, ("U", g)):
                    pe.wait_ge(*s)
                for qt in range(TT):
                    for kt in range(max(0, qt - 1), qt + 1):
                        for h in range(GH):
                            at = kt * DIM + (qt - kt) * P
                            ins = nc.tensor.matmul(bank_u[32 * h:32 * h + 32, qt * P:(qt + 1) * P],
                                                   vext[:, kt, GH * g + h, :], probs3[:, g % 2, h, at:at + P],
                                                   start=(kt == max(0, qt - 1)), stop=(kt == qt))
                ins.then_inc(pv_done.sem, 1)

            hidden(0)
            hidden(1)
            for g in range(2):
                for j in range(2):
                    for i in range(4):
                        scores(g, 4 * j + i)
                    hidden(2 + 2 * g + j)
                if g == 0:
                    pe.wait_ge(*done(st, l, it, "V"))
            pe_max_rows(pe, l, it, 0)
            hidden(6)
            hidden(7)
            for g in range(GROUPS):
                for h in range(GH):
                    scores_t(g, h)
                    if h == 0 and g < GROUPS - 1:
                        pe_max_rows(pe, l, it, g + 1)
                    if g + 2 < GROUPS:
                        for i in range(2):
                            scores(g + 2, 2 * h + i)
                    if h == 0 and g:
                        weigh(g - 1)
            for s in st.vacated(l, it, "OUT"):
                pe.wait_ge(*s)
            pe.wait_ge(*done(sc, l, it, ("H", 7)))
            for t in range(TT):
                for i in range(8):
                    nc.tensor.matmul(st.tile(l, "OUT")[:, t * DIM:(t + 1) * DIM], hid3[:, i, t * P:(t + 1) * P],
                                     fc2[:, i, :], start=(i == 0 and t % 2 == 0), stop=False)
                if t == 0:
                    weigh(GROUPS - 1)
            pe_out_heads(pe, l, it, wo3)

        def act3(act, it, step):
            l = 3
            step.begin(l, it)
            act_copy_xnT(act, l, it)
            for i, name in enumerate(("Q0", "K0", "Q1", "K1")):
                act.wait_ge(*sc.filled(l, it, name))
                if i == 0:
                    act.wait_ge(*split_two.at(l, it))
                nc.scalar.activation(src3[:, i, :], sc.tile(l, name)[:], ACT.Copy).then_inc(sc.free["act"].sem, 1)
            act.wait_ge(*st.filled(l, it, "T2"))
            for f in range(KT):
                ins = nc.scalar.activation(hT[:, f, :], st.tile(l, "T2")[:, f * SEQ:(f + 1) * SEQ], ACT.Identity,
                                           bias=beta[:, f:f + 1], scale=gamma[:, f:f + 1])
            ins.then_inc(st.free["act"].sem, 1)
            for i in range(8):
                act.wait_ge(*sc.filled(l, it, ("H", i)))
                nc.scalar.activation(hid3[:, i, :], sc.tile(l, ("H", i))[:], ACT.Silu,
                                     bias=fc1_b[:, i:i + 1]).then_inc(sc.free["act"].sem, 1)
                if i == 5:
                    act_max_rows(act, l, it, 0)
            for g in range(GROUPS):
                for h in range(GH):
                    name = ("E", g, h)
                    act.wait_ge(*st.filled(l, it, name))
                    if h == 0:
                        act.wait_ge(*pv_done.at(l, it, max(0, g - 1)))
                    nc.scalar.activation(probs3[:, g % 2, h, :], st.tile(l, name)[:, 0:896],
                                         ACT.Exp).then_inc(st.free["act"].sem, 1)
                    if h == 0 and g < GROUPS - 1:
                        act_max_rows(act, l, it, g + 1)
            step.end()

        def dve3(dve, it, step):
            l = 3
            step.begin(l, it)
            dve.wait_ge(*xn_ready.at(l, it))
            for t in range(TT):
                step.mark(nc.vector.bn_stats(stats3[:, t, :], xn[:, t, 0:DIM]))
            step.wait()
            fence(dve)
            for t in range(TT):
                nc.vector.bn_aggr(mv3[:, t, :], stats3[:, t, :]).then_inc(moments3.sem, 1)
            for i in range(2):
                dve_split(dve, l, it, step, i, src3[:, i, :], 1.0 if i % 2 else 0.25, done(sc, l, it, ("Q0", "K0")[i]))
            dve.wait_ge(*rstd3_ready.at(l, it, 1))
            for t in range(TT):
                nc.vector.tensor_scalar(hn[:, t, :], xn[:, t, 0:DIM], mv3[:, t, 0:1], rstd3[:, t:t + 1],
                                        ALU.subtract, ALU.mult).then_inc(hn_ready.sem, 1)
            for i in range(2, 4):
                dve_split(dve, l, it, step, i, src3[:, i, :], 1.0 if i % 2 else 0.25, done(sc, l, it, ("Q1", "K1")[i - 2]))
            dve_values(dve, l, it, None)

            def maxima(g, first, last):
                for i in range(first, last):
                    h, j = i // 2, i % 2
                    dve.wait_ge(*sc.filled(l, it, ("S", g, i)))
                    nc.vector.tensor_reduce(nmax[:, g % 2, 2 * j:2 * j + 2, h],
                                            sc.tile(l, ("S", g, i))[:, :].rearrange("p (a n) -> p a n", a=2), AX, ALU.max,
                                            negate=True).then_inc(sc.free["dve"].sem, 1)
                if last == 8:
                    dve_split_max(dve, l, it, step, g, ("S", g, 7))

            maxima(0, 0, 8)
            maxima(1, 0, 8)
            ln_stats(dve, l, it, step, 1)
            for g in range(GROUPS):
                if g + 2 < GROUPS:
                    maxima(g + 2, 0, 4)
                if g:
                    dve_normalise_heads(dve, l, it, step, g - 1)
                if g + 2 < GROUPS:
                    maxima(g + 2, 4, 8)
                if g == 1:
                    dve.wait_ge(*xres_ready.at(l, it, 1))
                    ln_normalise(dve, l, it, 1)
            dve_normalise_heads(dve, l, it, step, GROUPS - 1)
            dve_add_out(dve, l, it)
            step.end()

        def pool3(pool, it, step):
            l = 3
            step.begin(l, it)
            pool.wait_ge(*moments3.at(l, it, TT))
            fence(pool)
            step.mark(nc.gpsimd.tensor_scalar(veps3[:], mv3[:, :, 1], EPS, None, ALU.add))
            step.wait()
            nc.gpsimd.tensor_tensor(rstd3[:], veps3[:], mhalf[:], ALU.pow).then_inc(rstd3_ready.sem, 1)
            pool.wait_ge(*x_loaded.at(l, it))
            pool.wait_ge(*y_stored.at(l, it))
            step.mark(nc.gpsimd.tensor_tensor(xres[:], xl[:], bias_bc[:, 0:1, :].to_broadcast([P, TT, DIM]), ALU.add))
            for i in range(4):
                pool_split(pool, l, it, i)
                if i == 1:
                    step.wait()
                    nc.gpsimd.tensor_tensor(xres[:], xres[:], xn[:, :, 0:DIM], ALU.add).then_inc(xres_ready.sem, 1)
            ln_rsqrt(pool, l, it, step, 1)
            step.end()

        def sp3(sp, it):
            l = 3
            for i in range(4):
                side, m = i % 2, i // 2
                sp_store_parts(sp, l, it, i, (side, 0, m))
            for i in range(2):
                sp.wait_ge(*parts_stored[i].at(l, it, 16 * 2))
                fence(sp)
            sp.wait_ge(*st.full.at(l, it))
            for n, pair in enumerate(PRODUCTS_A + PRODUCTS_B):
                for side, tile in enumerate((q_3, k_3)):
                    sp.dma_start(tile[16 * n:16 * n + 16, :, :, :].rearrange("e g h n -> e (g h) n"),
                                 parts_dram[side, pair[side], 0].rearrange("(e h) n -> e h n", h=NH))\
                      .then_inc(stack_loaded[0].sem, 16)
            sp_load_next(sp, l, it)

            def q_rows(g):
                return q_3[96:98, g, :, :]

            sp_max_rows(sp, l, it, 0, q_rows)
            sp_max_rows(sp, l, it, 1, q_rows)
            sp_gather_heads(sp, l, it, 0)
            sp_max_rows(sp, l, it, 2, q_rows)
            sp_gather_heads(sp, l, it, 1)
            sp_max_rows(sp, l, it, 3, q_rows)
            sp_gather_heads(sp, l, it, 2)
            sp_gather_heads(sp, l, it, 3)
            sp_store_out(sp, l, it)

        l2 = ExitStack()
        win = sb("win", [P, KT, 1024], F32, l2)
        conv = sb("conv", [P, CT, 4], F32, l2)
        wx = sb("wx", [P, CT, 48], F32, l2)
        wx_raw = sb("wx_raw", [P, CT, 32], F32, l2)
        wdb = sb("wdb", [48, SEQ], F32, l2)
        bdt = sb("bdt", [P, CT], F32, l2)
        dpar = sb("dpar", [P, CT], F32, l2)
        wout = sb("wout", [P, CT, DIM], F32, l2)
        wg = sb("wg", [P, KT, 8], F32, l2)
        prio = sb("prio", [P, 8], F32, l2)
        moe_a = sb("moe_a", [P, NE, KT, 352], F32, l2)
        moe_b = sb("moe_b", [P, NE, KT, 352], F32, l2)
        moe_c = sb("moe_c", [P, NE, 3, DIM], F32, l2)
        xc = sb("xc", [P, CT, SEQ + 3], F32, l2)
        cv = sb("cv", [P, CT, SEQ], F32, l2)
        u = sb("u", [P, CT, SEQ], F32, l2)
        sz = sb("sz", [P, CT, SEQ], F32, l2)
        xp = sb("xp", [48, SEQ], F32, l2)
        dtb = sb("dtb", [P, CT, SEQ], F32, l2)
        ub = sb("ub", [P, CT, SEQ], F32, l2)
        sil = sb("sil", [P, 2, SEQ], F32, l2)
        hm = sb("hm", [P, 2, 3, SEQ], F32, l2)
        rl = sb("rl", [P, TT, 8], F32, l2)
        hot = sb("hot", [P, 2, TT, 8], F32, l2)
        tmp8 = sb("tmp8", [P, 2, TT, 8], F32, l2)
        vtop = sb("vtop", [P, 8, TT], F32, l2)
        wtok = sb("wtok", [P, TT, 8], F32, l2)
        l2.close()

        loads2 = [(win, d["win"]), (wg, d["wg"]), (prio, bc("prio", 8)), (conv, d["conv"]), (wx_raw, d["wx"]),
                  (bdt, d["bdt"]), (dpar, d["dpar"])]
        loaded2, loaded2b, dve_set2 = sem("loaded2"), sem("loaded2b"), sem("dve_set2")
        N2 = 16 * len(loads2)
        moe_loaded = [sem(f"moe_loaded{e}") for e in range(NE)]
        cv_ready = sig("cv_ready", [0, 0, CT, 0], "vector")
        u_ready = sig("u_ready", [0, 0, CT, 0], "scalar")
        dt_raw = sig("dt_raw", [0, 0, CT, 0], "vector")
        dt_ready = sig("dt_ready", [0, 0, CT, 0], "scalar")
        gap_ready = sig("gap_ready", [0, 0, 1, 0], "vector")
        gap_exp = sig("gap_exp", [0, 0, 1, 0], "scalar")
        hm_ready = sig("hm_ready", [0, 0, 3 * NE, 0], "vector")
        y_ready = sig("y_ready", [0, 0, 1, 0], "vector")

        def sp_setup2(sp):
            sp.wait_ge(*y_stored.at(2, 0))
            for dst, src in loads2:
                sp.dma_start(dst[:], src).then_inc(loaded2, 16)
            for e in (8, 9, 0):
                for dst, name in ((moe_a, "moe_a"), (moe_b, "moe_b"), (moe_c, "moe_c")):
                    sp.dma_start(dst[:, e], d[name][:, e]).then_inc(moe_loaded[e], 16)
            sp.dma_start(wdb[0:16, :], d["wdt"]).then_inc(loaded2b, 16)
            sp.dma_start(wdb[32:48, :], d["wbp"]).then_inc(loaded2b, 16)
            sp.dma_start(wout[:], d["wout"]).then_inc(loaded2b, 16)
            for e in range(1, 8):
                for dst, name in ((moe_a, "moe_a"), (moe_b, "moe_b"), (moe_c, "moe_c")):
                    sp.dma_start(dst[:, e], d[name][:, e]).then_inc(moe_loaded[e], 16)

        def dve_setup2(dve):
            dve.wait_ge(loaded2, N2)
            nc.vector.memset(xc[:, :, 0:3], 0.0).then_inc(dve_set2, 1)
            nc.vector.memset(wx[:, :, 16:32], 0.0).then_inc(dve_set2, 1)
            nc.vector.tensor_copy(wx[:, :, 0:16], wx_raw[:, :, 0:16]).then_inc(dve_set2, 1)
            nc.vector.tensor_copy(wx[:, :, 32:48], wx_raw[:, :, 16:32]).then_inc(dve_set2, 1)

        def pe2(pe, it):
            l = 2
            pe_transpose_xn(pe, l, it)
            pe.wait_ge(*done(st, l, it, "T"))
            for s in sc.vacated(l, it, "R"):
                pe.wait_ge(*s)
            for t in range(TT):
                for k in range(KT):
                    ins = nc.tensor.matmul(sc.tile(l, "R")[:, t * 8:t * 8 + 8], xnT[:, k, t * P:(t + 1) * P], wg[:, k, :],
                                           start=(k == 0), stop=(k == 1))
            ins.then_inc(sc.full.sem, 1)
            for c in range(CT):
                pe_project(pe, l, it, ("XC", c), win, c)
            for c in range(CT):
                pe_project(pe, l, it, ("Z", c), win, CT + c)

            def expert_in(e):
                pe.wait_ge(moe_loaded[e], 48)
                for i, (at, n) in enumerate(HT):
                    pe_project(pe, l, it, ("A", e, i), moe_a[:, e], 0, n, None, at)
                    pe_project(pe, l, it, ("B", e, i), moe_b[:, e], 0, n, None, at)

            def expert_out(e, order):
                for s in st.vacated(l, it, ("Y", e)):
                    pe.wait_ge(*s)
                pe.wait_ge(*hm_ready.at(l, it, 3 * order + 3))
                for t in range(TT):
                    for i, (at, n) in enumerate(HT):
                        ins = nc.tensor.matmul(st.tile(l, ("Y", e))[:, t * DIM:(t + 1) * DIM],
                                               hm[0:n, order % 2, i, t * P:(t + 1) * P], moe_c[0:n, e, i, :],
                                               start=(i == 0), stop=(i == 2))
                ins.then_inc(st.full.sem, 1)

            expert_in(8)
            expert_in(9)
            expert_out(8, 0)
            for s in sc.vacated(l, it, "XP"):
                pe.wait_ge(*s)
            pe.wait_ge(*u_ready.at(l, it, CT))
            for c in range(CT):
                ins = nc.tensor.matmul(sc.tile(l, "XP")[0:48, :], wx[:, c, :], u[:, c, :], start=(c == 0), stop=(c == CT - 1))
            ins.then_inc(sc.full.sem, 1)
            expert_in(0)
            expert_out(9, 1)
            pe.wait_ge(loaded2b, 48)
            pe.wait_ge(*done(sc, l, it, "XP"))
            for c in range(CT):
                for s in sc.vacated(l, it, ("DT", c)):
                    pe.wait_ge(*s)
                nc.tensor.matmul(sc.tile(l, ("DT", c))[:], wdb[0:16, c * P:(c + 1) * P], xp[0:16, :],
                                 start=True, stop=True).then_inc(sc.full.sem, 1)
                for s in sc.vacated(l, it, ("BP", c)):
                    pe.wait_ge(*s)
                nc.tensor.matmul(sc.tile(l, ("BP", c))[:], wdb[32:48, c * P:(c + 1) * P], xp[32:48, :],
                                 start=True, stop=True).then_inc(sc.full.sem, 1)
            for e in range(1, 8):
                expert_in(e)
                expert_out(e - 1, e + 1)
            for s in st.vacated(l, it, "OUT"):
                pe.wait_ge(*s)
            pe.wait_ge(*y_ready.at(l, it, 1))
            for t in range(TT):
                for c in range(CT):
                    ins = nc.tensor.matmul(st.tile(l, "OUT")[:, t * DIM:(t + 1) * DIM], cv[:, c, t * P:(t + 1) * P],
                                           wout[:, c, :], start=(c == 0), stop=(c == CT - 1))
            ins.then_inc(st.full.sem, 1)
            expert_out(7, 9)

        def act2(act, it, step):
            l = 2
            step.begin(l, it)
            act_copy_xnT(act, l, it)
            for c in range(CT):
                act.wait_ge(*sc.filled(l, it, ("XC", c)))
                nc.scalar.activation(xc[:, c, 3:SEQ + 3], sc.tile(l, ("XC", c))[:], ACT.Copy).then_inc(sc.free["act"].sem, 1)
            for c in range(CT):
                act.wait_ge(*sc.filled(l, it, ("Z", c)))
                nc.scalar.activation(sz[:, c, :], sc.tile(l, ("Z", c))[:], ACT.Silu).then_inc(sc.free["act"].sem, 1)

            def expert(e, order):
                for i, (at, n) in enumerate(HT):
                    act.wait_ge(*sc.filled(l, it, ("A", e, i)))
                    act.wait_ge(*hm_ready.at(l, it, max(0, 3 * order + i - 1)))
                    nc.scalar.activation(sil[0:n, (3 * order + i) % 2, :], sc.tile(l, ("A", e, i))[0:n, :],
                                         ACT.Silu).then_inc(sc.free["act"].sem, 1)

            expert(8, 0)
            for c in range(CT):
                act.wait_ge(*cv_ready.at(l, it, c + 1))
                nc.scalar.activation(u[:, c, :], cv[:, c, :], ACT.Silu).then_inc(u_ready.sem, 1)
            expert(9, 1)
            act.wait_ge(*sc.filled(l, it, "XP"))
            nc.scalar.activation(xp[:], sc.tile(l, "XP")[0:48, :], ACT.Copy).then_inc(sc.free["act"].sem, 1)
            expert(0, 2)
            expert(1, 3)
            act.wait_ge(*gap_ready.at(l, it, 1))
            nc.scalar.activation(vtop[:, 4, :], vtop[:, 3, :], ACT.Exp).then_inc(gap_exp.sem, 1)
            act.wait_ge(*dt_raw.at(l, it, CT))
            for c in range(CT):
                step.mark(nc.scalar.activation(dtb[:, c, :], dtb[:, c, :], ACT.Exp))
            for c in range(CT):
                step.wait(c + 1)
                nc.scalar.activation(dtb[:, c, :], dtb[:, c, :], ACT.Ln, bias=1.0).then_inc(dt_ready.sem, 1)
            for e in range(2, 8):
                expert(e, e + 2)
            step.end()

        def dve2(dve, it, step):
            l = 2
            step.begin(l, it)
            dve.wait_ge(*sc.filled(l, it, "R"))
            nc.vector.tensor_copy(rl[:], sc.tile(l, "R")[:, 0:32].rearrange("p (t e) -> p t e", t=TT))\
              .then_inc(sc.free["dve"].sem, 1)
            dve.wait_ge(*done(sc, l, it, "R"))
            pr = prio[:, None, :].to_broadcast([P, TT, 8])
            for j in range(2):
                def col(r):
                    return vtop[:, r, :, None].to_broadcast([P, TT, 8])
                step.mark(nc.vector.tensor_reduce(vtop[:, j, :], rl[:], AX, ALU.max))
                step.wait()
                step.mark(nc.vector.tensor_tensor(tmp8[:, 0], rl[:], col(j), ALU.is_equal))
                step.wait()
                step.mark(nc.vector.tensor_tensor(tmp8[:, 1], tmp8[:, 0], pr, ALU.mult))
                step.wait()
                step.mark(nc.vector.tensor_reduce(vtop[:, 2, :], tmp8[:, 1], AX, ALU.max))
                step.wait()
                step.mark(nc.vector.tensor_tensor(hot[:, j], tmp8[:, 1], col(2), ALU.is_equal))
                step.wait()
                if j == 0:
                    step.mark(nc.vector.scalar_tensor_tensor(rl[:], hot[:, 0], -3.0e38, rl[:], ALU.mult, ALU.add))
                    step.wait()
            nc.vector.tensor_tensor(vtop[:, 3, :], vtop[:, 1, :], vtop[:, 0, :], ALU.subtract).then_inc(gap_ready.sem, 1)

            def convolve(c):
                dve.wait_ge(*done(sc, l, it, ("XC", c)))
                step.mark(nc.vector.tensor_scalar(cv[:, c, :], xc[:, c, 0:SEQ], conv[:, c, 0:1], None, ALU.mult))
                for j in range(1, 4):
                    step.wait()
                    ins = nc.vector.scalar_tensor_tensor(cv[:, c, :], xc[:, c, j:j + SEQ], conv[:, c, j:j + 1], cv[:, c, :],
                                                         ALU.mult, ALU.add)
                    if j < 3:
                        step.mark(ins)
                ins.then_inc(cv_ready.sem, 1)

            def expert(e, order):
                for i, (at, n) in enumerate(HT):
                    dve.wait_ge(*done(sc, l, it, ("A", e, i)))
                    fence(dve)
                    dve.wait_ge(*sc.filled(l, it, ("B", e, i)))
                    nc.vector.tensor_tensor(hm[0:n, order % 2, i, :], sc.tile(l, ("B", e, i))[0:n, :],
                                            sil[0:n, (3 * order + i) % 2, :], ALU.mult).then_inc(hm_ready.sem, 1)
                    dve.wait_ge(*hm_ready.at(l, it, 3 * order + i + 1))
                    dve.sem_inc(sc.free["dve"].sem, 1)

            def add(e):
                dve.wait_ge(*st.filled(l, it, ("Y", e)))
                fence(dve)
                dve.wait_ge(*xres_ready.at(l, it, 1))
                tile = st.tile(l, ("Y", e))
                if e >= 8:
                    flat = xres[:, :, :].rearrange("p t f -> p (t f)")
                    ins = nc.vector.tensor_tensor(flat, tile[:], flat, ALU.add)
                else:
                    for t in range(TT):
                        ins = nc.vector.scalar_tensor_tensor(xres[:, t, :], tile[:, t * DIM:(t + 1) * DIM],
                                                             wtok[:, t, e:e + 1], xres[:, t, :], ALU.mult, ALU.add)
                ins.then_inc(st.free["dve"].sem, 1)
                dve.wait_ge(*done(st, l, it, ("Y", e)))

            convolve(0)
            convolve(1)
            for order, e in enumerate((8,)):
                expert(e, 0)
            convolve(2)
            convolve(3)
            expert(9, 1)
            add(8)
            expert(0, 2)
            add(9)
            for c in range(CT):
                dve.wait_ge(*sc.filled(l, it, ("DT", c)))
                nc.vector.tensor_scalar(dtb[:, c, :], sc.tile(l, ("DT", c))[:], bdt[:, c:c + 1], 2.0, ALU.add, ALU.min)\
                  .then_inc(dt_raw.sem, 1)
                dve.wait_ge(*dt_raw.at(l, it, c + 1))
                dve.sem_inc(sc.free["dve"].sem, 1)
                dve.wait_ge(*sc.filled(l, it, ("BP", c)))
                nc.vector.tensor_tensor(ub[:, c, :], sc.tile(l, ("BP", c))[:], u[:, c, :], ALU.mult)\
                  .then_inc(sc.free["dve"].sem, 1)
            expert(1, 3)
            dve.wait_ge(*gap_exp.at(l, it, 1))
            step.mark(nc.vector.tensor_scalar(vtop[:, 5, :], vtop[:, 4, :], 1.0, None, ALU.add))
            step.wait()
            step.mark(nc.vector.reciprocal(vtop[:, 6, :], vtop[:, 5, :]))
            step.wait()
            step.mark(nc.vector.tensor_tensor(vtop[:, 7, :], vtop[:, 4, :], vtop[:, 6, :], ALU.mult))
            step.wait()
            for j in range(2):
                step.mark(nc.vector.tensor_tensor(hot[:, j], hot[:, j], vtop[:, 6 + j, :, None].to_broadcast([P, TT, 8]),
                                                  ALU.mult))
            step.wait()
            step.mark(nc.vector.tensor_tensor(wtok[:], hot[:, 0], hot[:, 1], ALU.add))
            step.wait()
            add(0)
            for e in range(2, 8):
                expert(e, e + 2)
                add(e - 1)
                if e - 2 < CT:
                    c = e - 2
                    dve.wait_ge(*dt_ready.at(l, it, c + 1))
                    step.mark(nc.vector.tensor_scalar(dtb[:, c, :], dtb[:, c, :], 1e-4, 1.0, ALU.max, ALU.min))
                    step.wait()
                    step.mark(nc.vector.tensor_scalar(dtb[:, c, :], dtb[:, c, :], -1.0, 1.0, ALU.mult, ALU.add))
                    step.wait()
                    step.mark(nc.vector.tensor_tensor_scan(cv[:, c, :], dtb[:, c, :], ub[:, c, :], 0.0, ALU.mult, ALU.add))
                    step.wait()
                    step.mark(nc.vector.scalar_tensor_tensor(cv[:, c, :], u[:, c, :], dpar[:, c:c + 1], cv[:, c, :],
                                                             ALU.mult, ALU.add))
                    step.wait()
                    ins = nc.vector.tensor_tensor(cv[:, c, :], cv[:, c, :], sz[:, c, :], ALU.mult)
                    if c == CT - 1:
                        ins.then_inc(y_ready.sem, 1)
                if e == 6:
                    ln_stats(dve, l, it, step, 1)
                if e == 7:
                    ln_normalise(dve, l, it, 1)
            dve.wait_ge(*st.filled(l, it, "OUT"))
            flat = xres[:, :, :].rearrange("p t f -> p (t f)")
            nc.vector.tensor_tensor(flat, st.tile(l, "OUT")[:], flat, ALU.add).then_inc(st.free["dve"].sem, 1)
            dve.wait_ge(*done(st, l, it, "OUT"))
            add(7)
            step.end()

        def pool2(pool, it, step):
            l = 2
            step.begin(l, it)
            pool.wait_ge(*x_loaded.at(l, it))
            pool.wait_ge(*y_stored.at(l, it))
            fence(pool)
            nc.gpsimd.tensor_copy(xres[:], xl[:]).then_inc(xres_ready.sem, 1)
            ln_rsqrt(pool, l, it, step, 1)
            step.end()

        def sp2(sp, it):
            l = 2
            sp_load_next(sp, l, it)
            sp.wait_ge(*st.full.at(l, it, st.full.per[l]))
            fence(sp)
            sp.wait_ge(*done(st, l, it, ("Y", 7)))
            fence(sp)
            dst = xs_tok[it + BATCH * (l + 1)] if l < LAYERS - 1 else out_tok[it]
            sp.dma_start(dst, xres[:]).then_inc(y_stored.sem, 16)

        loads0 = [(ident, d["ident"]), (wq0, d["wq0"]), (wk0, d["wk0"]), (wv0, d["wv0"]), (bq0, d["bq0"]), (bk0, d["bk0"]),
                  (vbias, bc("bv0", DIM)), (w1, d["w1"]), (j_rows, d["j0"]), (same_head, d["same_head"]),
                  (lam, bc("lam0", 1)), (lscale, bc("scale0", 1, 4)), (b10, d["b10"]), (w2, d["w2"]), (wo0, d["wo0"])]
        N0 = 16 * (len(loads0) + 2)

        @block.sync
        def _(sp):
            open_signals(sp, "sync")
            sp.dma_start(xl[:], x_tok[0]).then_inc(x_loaded.sem, 16)
            for dst, src in loads0:
                sp.dma_start(dst[:], src).then_inc(consts, 16)
            sp.dma_start(bias_bc[:, 0, :], bc("bo0", DIM)).then_inc(consts, 16)
            sp.dma_start(bias_bc[:, 1, :], bc("b20", DIM)).then_inc(consts, 16)
            with sp.Fori(0, BATCH) as it:
                sp0(sp, it)
            sp_setup1(sp)
            with sp.Fori(0, BATCH) as it:
                sp1(sp, it)
            sp_setup2(sp)
            with sp.Fori(0, BATCH) as it:
                sp2(sp, it)
            sp_setup3(sp)
            with sp.Fori(0, BATCH) as it:
                sp3(sp, it)
            sp.wait_ge(y_stored.sem, y_stored.start + 16 * BATCH * LAYERS)

        @block.gpsimd
        def _(pool):
            open_signals(pool, "gpsimd")
            step = Chain(pool, sem("pool_step"), [1, 1, 1, 3], 2)
            nc.gpsimd.memset(mhalf[:], -0.5).then_inc(step.sig.sem, 1)
            pool.wait_ge(step.sig.sem, 1)
            pool.wait_ge(ln_moments.sem, TT)
            fence(pool)
            nc.gpsimd.tensor_scalar(veps[:], mv[:, :, 1], EPS, None, ALU.add).then_inc(step.sig.sem, 1)
            pool.wait_ge(step.sig.sem, 2)
            nc.gpsimd.tensor_tensor(rstd[:], veps[:], mhalf[:], ALU.pow).then_inc(ln_rstd.sem, 1)
            pool.wait_ge(consts, N0)
            nc.gpsimd.memset(xn[:, :, DIM:DIM + 1], 1.0).then_inc(pool_setup, 1)
            nc.gpsimd.memset(vext[:, :, :, HD:32], 1.0).then_inc(pool_setup, 1)
            nc.gpsimd.tensor_tensor(bias_bc[:, 0, :], bias_bc[:, 0, :], bias_bc[:, 1, :], ALU.add).then_inc(pool_setup, 1)
            pool.wait_ge(dve_setup, 6)
            pool.wait_ge(pool_setup, 3)
            with pool.Fori(0, BATCH) as it:
                pool0(pool, it, step)
            pool.wait_ge(loaded1, N1)
            pool.wait_ge(dve_pre1, 9)
            with pool.Fori(0, BATCH) as it:
                pool1(pool, it, step)
            pool.wait_ge(loaded2, N2)
            with pool.Fori(0, BATCH) as it:
                pool2(pool, it, step)
            pool_setup3(pool)
            pool.wait_ge(pool_set3, 2)
            with pool.Fori(0, BATCH) as it:
                pool3(pool, it, step)

        @block.scalar
        def _(act):
            open_signals(act, "scalar")
            step = Chain(act, sem("act_step"), [0, 0, 4, 0])
            act.sem_inc(step.sig.sem, 1)
            act.dma_start(xs[0:BATCH, :, :], d["x"]).then_inc(xs_copied, 16)
            act.dma_start(xs[BATCH * LAYERS, :, :], d["x"][0]).then_inc(xs_copied, 16)
            act.wait_ge(dve_setup, 6)
            act.wait_ge(pool_setup, 3)
            with act.Fori(0, BATCH) as it:
                act0(act, it, step)
            act.wait_ge(dve_set1, 5)
            act.wait_ge(dve_pre1, 9)
            with act.Fori(0, BATCH) as it:
                act1(act, it, step)
            act.wait_ge(dve_set2, 4)
            with act.Fori(0, BATCH) as it:
                act2(act, it, step)
            act.wait_ge(dve_set3, 4)
            with act.Fori(0, BATCH) as it:
                act3(act, it, step)

        @block.vector
        def _(dve):
            open_signals(dve, "vector")
            step = Chain(dve, sem("dve_step"), STEPS_DVE, TT)
            dve.wait_ge(x_loaded.sem, 16)
            for t in range(TT):
                nc.vector.bn_stats(stats[:, t, :], xl[:, t, :]).then_inc(step.sig.sem, 1)
            dve.wait_ge(step.sig.sem, TT)
            fence(dve)
            for t in range(TT):
                nc.vector.bn_aggr(mv[:, t, :], stats[:, t, :]).then_inc(ln_moments.sem, 1)
            ln_normalise(dve, 0, 0, 0)
            dve.wait_ge(consts, N0)
            nc.vector.tensor_copy(ident_bf[:], ident[:]).then_inc(dve_setup, 1)
            nc.vector.memset(k_a[96:98, :, :, :], 1.0).then_inc(dve_setup, 1)
            nc.vector.tensor_scalar(lmask[:], ident[0:4, 0:4], lscale[:, 0:1], None, ALU.mult).then_inc(dve_setup, 1)
            nc.vector.tensor_scalar(same_head[:], same_head[:], lam[:, 0:1], None, ALU.mult).then_inc(dve_setup, 1)
            dve.wait_ge(dve_setup, 4)
            for k in range(KT):
                nc.vector.tensor_tensor(jbd[:, k, :, :], j_rows[:, k, :, None].to_broadcast([P, HD, NH]),
                                        same_head[:, None, :].to_broadcast([P, HD, NH]), ALU.mult).then_inc(dve_setup, 1)
            dve.wait_ge(pool_setup, 3)
            with dve.Fori(0, BATCH) as it:
                dve0(dve, it, step)
            dve_setup1(dve)
            with dve.Fori(0, BATCH) as it:
                dve1(dve, it, step)
            dve_setup2(dve)
            dve.wait_ge(dve_set2, 4)
            with dve.Fori(0, BATCH) as it:
                dve2(dve, it, step)
            dve_setup3(dve)
            dve.wait_ge(pool_set3, 2)
            with dve.Fori(0, BATCH) as it:
                dve3(dve, it, step)

        @block.tensor
        def _(pe):
            open_signals(pe, "tensor")
            pe.wait_ge(dve_setup, 6)
            pe.wait_ge(pool_setup, 3)
            with pe.Fori(0, BATCH) as it:
                pe0(pe, it)
            pe_setup1(pe)
            pe.wait_ge(dve_set1, 5)
            pe.wait_ge(dve_pre1, 9)
            with pe.Fori(0, BATCH) as it:
                pe1(pe, it)
            pe.wait_ge(dve_set2, 4)
            with pe.Fori(0, BATCH) as it:
                pe2(pe, it)
            pe.wait_ge(dve_set3, 4)
            pe.wait_ge(pool_set3, 2)
            with pe.Fori(0, BATCH) as it:
                pe3(pe, it)


def kernel(**inputs):
    import numpy as np
    from concourse import bacc
    from concourse.bass_utils import run_bass_kernel_spmd

    def arr(name):
        return np.ascontiguousarray(inputs[name])

    def by_rows(w):
        return np.ascontiguousarray(w.reshape(-1, P, w.shape[-1]).transpose(1, 0, 2))

    def columns(b):
        return np.ascontiguousarray(b.reshape(-1, P).T)

    def dim_major(w):
        return w.reshape(NH, HD, *w.shape[1:]).swapaxes(0, 1).reshape(w.shape)

    a = {
        "x": arr("L0_attn_x"),
        "ident": np.eye(P, dtype=np.float32),
        "wq0": by_rows(dim_major(arr("L0_attn_Wq")).T),
        "wk0": by_rows(dim_major(arr("L0_attn_Wk")).T),
        "wv0": by_rows(arr("L0_attn_Wv").T),
        "wo0": by_rows(arr("L0_attn_Wo").T),
        "bq0": columns(dim_major(arr("L0_attn_bq"))),
        "bk0": columns(dim_major(arr("L0_attn_bk"))),
        "bv0": arr("L0_attn_bv"),
        "bo0": arr("L0_attn_bo"),
        "j0": by_rows(arr("L0_attn_J_attn").swapaxes(0, 1).reshape(DIM, HD)),
        "same_head": np.tile(np.eye(NH, dtype=np.float32), (P // NH, 1)),
        "lam0": arr("L0_attn_lambda_attn").reshape(1),
        "w1": by_rows(arr("L0_ffn_W1").T),
        "b10": columns(arr("L0_ffn_b1")),
        "w2": by_rows(arr("L0_ffn_W2").T),
        "b20": arr("L0_ffn_b2"),
        "scale0": arr("L0_ffn_scale").reshape(1),
    }
    def even_odd(w, heads):
        return w.reshape(DIM, heads, HD // 2, 2).transpose(0, 3, 2, 1).reshape(DIM, heads * HD)

    inverse = (1.0 / 10000.0 ** (np.arange(0, DIM, 2, dtype=np.float32) / np.float32(DIM))).astype(np.float32)
    angle = np.arange(SEQ, dtype=np.float32)[:, None] * inverse[None, :]
    angle_q = angle.reshape(SEQ, NH, HD // 2).transpose(2, 1, 0).reshape(P, SEQ)
    angle_k = np.repeat(angle[:, :HD // 2].T, 4, axis=0)
    w1_1 = arr("L1_ffn_w1")
    a |= {
        "wq1": by_rows(even_odd(arr("L1_attn_Wq"), NH)),
        "wk1": by_rows(even_odd(arr("L1_attn_Wk"), 4)),
        "wv1": by_rows(arr("L1_attn_Wv")),
        "wo1": by_rows(arr("L1_attn_Wo")),
        "cos1": np.cos(angle_q), "sin1": np.sin(angle_q),
        "cosk": np.cos(angle_k), "sink": np.sin(angle_k),
        "w1x": by_rows(w1_1[:, :DIM].T), "w1s": by_rows(w1_1[:, DIM:].T),
        "b11": columns(arr("L1_ffn_b1")),
        "w21": np.ascontiguousarray(arr("L1_ffn_w2").T),
        "b21": arr("L1_ffn_b2"),
        "tau": arr("L1_ffn_tau"),
        "slots": arr("L1_ffn_slot_init"), "slot_scale": arr("L1_ffn_slot_scale"),
        "wih": by_rows(arr("L1_ffn_gru_wih").T), "whh": by_rows(arr("L1_ffn_gru_whh").T),
        "bih": columns(arr("L1_ffn_gru_bih")), "bhh": columns(arr("L1_ffn_gru_bhh")),
        "wvs": by_rows(arr("L1_ffn_wv").T), "bvs": columns(arr("L1_ffn_bv")),
        "wos": by_rows(arr("L1_ffn_wo").T), "bo1": arr("L1_ffn_bo"),
    }
    def experts(name, shared):
        w = np.concatenate([arr(name), shared], axis=0)
        return np.ascontiguousarray(w.reshape(NE, -1, P, w.shape[-1]).transpose(2, 0, 1, 3))

    def halves(name):
        return arr(name).reshape(DIM, 2, 352).transpose(1, 0, 2)

    w3 = np.concatenate([arr("L2_ffn_W3"), arr("L2_ffn_Ws3").reshape(2, 352, DIM)], axis=0)
    w3 = np.concatenate([w3, np.zeros((NE, 32, DIM), np.float32)], axis=1)
    conv_w = arr("L2_attn_conv_w").reshape(CT, P, 4).transpose(1, 0, 2)
    a |= {
        "win": by_rows(arr("L2_attn_W_in")),
        "conv": np.ascontiguousarray(conv_w),
        "wx": by_rows(arr("L2_attn_W_x")),
        "wdt": arr("L2_attn_W_dt"), "wbp": arr("L2_attn_W_Bp"),
        "bdt": columns(arr("L2_attn_b_dt")), "dpar": columns(arr("L2_attn_D_param")),
        "wout": by_rows(arr("L2_attn_W_out")),
        "wg": by_rows(arr("L2_ffn_Wg")),
        "prio": np.arange(8, 0, -1, dtype=np.float32),
        "moe_a": experts("L2_ffn_W1", halves("L2_ffn_Ws1")),
        "moe_b": experts("L2_ffn_W2", halves("L2_ffn_Ws2")),
        "moe_c": np.ascontiguousarray(w3.reshape(NE, 3, P, DIM).transpose(2, 0, 1, 3)),
    }
    import ml_dtypes
    key, query = np.arange(P)[:, None], np.arange(P)[None, :]
    low = np.float32(-1e30)
    own = np.where(key <= query, 0, low)
    after = np.where(key > query, 0, low)
    a |= {
        "wq3": by_rows(dim_major(arr("L3_attn_Wq")).T), "wk3": by_rows(dim_major(arr("L3_attn_Wk")).T),
        "wv3": by_rows(arr("L3_attn_Wv").T), "wo3": by_rows(arr("L3_attn_Wo").T),
        "mask_q": np.concatenate([np.full((P, P), low), own.T, after.T, own.T, after.T, own.T], axis=1)
        .reshape(P, 3, DIM).astype(ml_dtypes.bfloat16),
        "mask_k": np.concatenate([own, after, own, after], axis=1).reshape(P, 2, DIM).astype(ml_dtypes.bfloat16),
        "gamma": columns(arr("L3_ffn_ln_gamma")), "beta": columns(arr("L3_ffn_ln_beta")),
        "fc1_q": by_rows(arr("L3_ffn_fc1_q")).reshape(P, -1), "fc1_s": arr("L3_ffn_fc1_scales").reshape(-1),
        "fc2_q": by_rows(arr("L3_ffn_fc2_q")).reshape(P, -1), "fc2_s": arr("L3_ffn_fc2_scales").reshape(-1),
        "fc1_b": columns(arr("L3_ffn_fc1_bias")), "fc2_b": arr("L3_ffn_fc2_bias"),
    }
    nc = bacc.Bacc("TRN2", target_bir_lowering=False, num_devices=1)
    d = {n: nc.dram_tensor(f"in_{n}", v.shape, mybir.dt.from_np(v.dtype), kind="ExternalInput").ap()
         for n, v in a.items()}
    out = nc.dram_tensor("out_0", (BATCH, SEQ, DIM), F32, kind="ExternalOutput").ap()
    build(nc, d, out)
    r = run_bass_kernel_spmd(nc, [{f"in_{n}": v for n, v in a.items()}], core_ids=[0])
    return r.results[0]["out_0"]
```

```python
from contextlib import ExitStack

import concourse.bass as bass
from concourse import mybir

F32 = mybir.dt.float32
BF16 = mybir.dt.bfloat16
F32R = mybir.dt.float32r
I32 = mybir.dt.int32
U32 = mybir.dt.uint32
ACT = mybir.ActivationFunctionType
ALU = mybir.AluOpType
AX = mybir.AxisListType.X

P = 128
BATCH, SEQ, DIM = 8, 512, 256
TT = SEQ // P
KT = DIM // P
NH, HD = 16, 16
GROUPS, GH = 4, 4
EPS = 1e-5
BAND = (2 * TT - 1) * P
LAYERS = 4

ALL0, PRE1, MAIN1, POST1, ALL2, PRE3, MAIN3, POST3 = range(8)
ROUNDS = [BATCH, 1, BATCH - 1, 1, BATCH, 1, BATCH - 1, 1]
LAYER = [0, 1, 1, 1, 2, 3, 3, 3]
FRONT = [True, True, True, False, True, True, True, False]
BACK = [True, False, True, True, True, False, True, True]
STEPS_DVE = [16, (21, 14), 49, (6, 10)]


def spread(counts):
    per = []
    for s, l in enumerate(LAYER):
        c = counts[l]
        per.append((c[0] if FRONT[s] else 0) + (c[1] if BACK[s] else 0) if isinstance(c, tuple) else
                   c if s in (ALL0, ALL2) else c if BACK[s] else 0)
    return per


def plans(plan0, plan1, plan2, plan3):
    return [plan0] + [plan1(FRONT[s], BACK[s]) for s in (PRE1, MAIN1, POST1)] + [plan2] \
        + [plan3(FRONT[s], BACK[s]) for s in (PRE3, MAIN3, POST3)]


class Signal:

    def __init__(self, sem, per, start=1):
        self.sem, self.per, self.start = sem, per, start

    def at(self, l, it, k=0):
        base = self.start + sum(n * k for n, k in zip(ROUNDS[:l], self.per))
        return self.sem, it * self.per[l] + (base + k)


class Ring:

    def __init__(self, sem, name, tiles, plan):
        self.tiles, self.plan = tiles, plan
        self.order = [{n: i for i, (n, _) in enumerate(p)} for p in plan]
        self.full = Signal(sem(f"{name}_full"), [len(p) for p in plan])
        self.free = {r: Signal(sem(f"{name}_free_{r}"), [sum(x == r for _, x in p) for p in plan])
                     for r in ("act", "dve")}

    def tile(self, l, name):
        return self.tiles[self.order[l][name] % len(self.tiles)]

    def filled(self, l, it, name):
        return self.full.at(l, it, self.order[l][name] + 1)

    def vacated(self, l, it, name):
        u = self.order[l][name] - len(self.tiles)
        if u < 0:
            return [s.at(l, it) for s in self.free.values()]
        reader = self.plan[l][u][1]
        return [self.free[reader].at(l, it, sum(x == reader for _, x in self.plan[l][:u + 1]))]


class Chain:

    def __init__(self, eng, sem, per, start=1):
        self.eng, self.sig, self.count = eng, Signal(sem, per, start), 0

    def begin(self, l, it):
        self.l, self.it, self.count = l, it, 0

    def end(self):
        assert self.count == self.sig.per[self.l], (self.l, self.count)

    def mark(self, ins):
        ins.then_inc(self.sig.sem, 1)
        self.count += 1
        return self.count

    def wait(self, k=None):
        self.eng.wait_ge(*self.sig.at(self.l, self.it, self.count if k is None else k))




def s_uses(g):
    return [(("S", g, i), "dve") for i in range(GH * TT)]


S_AT = [0, 4, 8, 12, 16]
S3_AT = [0, 0, 4, 10, 16]


def turn_uses(g):
    return [(("DT", g), "dve")]


def spread_uses(g):
    return [(("RB", g), "dve")]


SC_PLAN0 = ([("Q0", "act"), ("K0", "act"), ("Q1", "act"), ("K1", "act")]
            + [(("W1", i), "dve") for i in range(4)] + [("J0", "act"), ("J1", "act")]
            + [(("H", i), "act") for i in range(8)] + [(("W2", i), "dve") for i in range(4)]
            + s_uses(0) + s_uses(1) + s_uses(2)
            + s_uses(3)[:S3_AT[2]] + turn_uses(0) + s_uses(3)[S3_AT[2]:S3_AT[3]] + spread_uses(0) + s_uses(3)[S3_AT[3]:]
            + [u for g in range(1, GROUPS) for u in turn_uses(g) + spread_uses(g)])
ST_PLAN0 = ([("T", "act"), ("V", "dve")]
            + [(("E", g, kt, hp), "act") for g in range(GROUPS) for kt in range(TT) for hp in range(2)]
            + [("OUT", "dve")])
PU_PLAN = [(("U", g), "act") for g in range(GROUPS)]
PM_PLAN = [(("M", g), "act") for g in range(GROUPS)]
SPLITS0 = ["Q0", "K0", "Q1", "K1", "KN0", "KN1", "J0", "J1"]
SLOT0 = {"Q0": 0, "K0": 1, "Q1": 2, "K1": 3, "KN0": 4, "KN1": 5, "J0": 0, "J1": 2}
WHERE0 = {"Q0": (0, 0, 0), "K0": (1, 0, 0), "Q1": (0, 0, 1), "K1": (1, 0, 1),
          "KN0": (1, 1, 0), "KN1": (1, 1, 1), "J0": (0, 1, 0), "J1": (0, 1, 1)}




def parts_of(front, back, *items):
    return [u for part, uses in items if (front if part == "front" else back) for u in uses]


def e_uses(g, first=0, last=TT):
    return [(("E", g, kt, hp), "act") for kt in range(first, last) for hp in range(2)]


def sc_plan1(front, back):
    return parts_of(front, back, ("back", [("AT", "act"), ("SI", "dve")] + s_uses(2)),
                    ("front", [("QE", "act"), ("QO", "act"), ("KK", "act"), ("H", "act")]),
                    ("back", s_uses(3)[:8]), ("front", [("L", "dve")]), ("back", turn_uses(0) + s_uses(3)[8:12]
                                                                          + spread_uses(0) + s_uses(3)[12:] + [("GX", "dve")]),
                    ("front", s_uses(0)[:8]), ("back", turn_uses(1)), ("front", s_uses(0)[8:12]), ("back", spread_uses(1)),
                    ("front", s_uses(0)[12:]), ("back", [("SV", "act")]),
                    ("front", s_uses(1)[:8]), ("back", turn_uses(2)), ("front", s_uses(1)[8:12]), ("back", spread_uses(2)),
                    ("front", s_uses(1)[12:]), ("back", [("Z2", "act")] + turn_uses(3) + spread_uses(3)))


def st_plan1(front, back):
    return parts_of(front, back, ("back", [("V", "dve")] + e_uses(0, 0, 2)), ("front", [("T", "act")]),
                    ("back", e_uses(0, 2) + e_uses(1) + e_uses(2) + e_uses(3) + [("OUT", "dve")]))


def pu_plan1(front, back):
    return parts_of(front, back, ("back", PU_PLAN))


def pm_plan1(front, back):
    return parts_of(front, back, ("back", PM_PLAN[1:]), ("front", PM_PLAN[:1]))


NE = 10
HT = [(0, 128), (128, 128), (256, 96)]


def expert_uses(e):
    return [(u, r) for i in range(len(HT)) for u, r in ((("A", e, i), "act"), (("B", e, i), "dve"))]


CT = 4
SC_PLAN2 = ([("R", "dve")] + [(("XC", c), "act") for c in range(CT)] + [(("Z", c), "act") for c in range(CT)]
            + expert_uses(8) + expert_uses(9) + [("XP", "act")] + expert_uses(0)
            + [u for c in range(CT) for u in ((("DT", c), "dve"), (("BP", c), "dve"))]
            + [u for e in range(1, 8) for u in expert_uses(e)])
ST_PLAN2 = ([("T", "act"), (("Y", 8), "dve"), (("Y", 9), "dve"), (("Y", 0), "dve")]
            + [(("Y", e), "dve") for e in range(1, 7)] + [("OUT", "dve"), (("Y", 7), "dve")])


def s3_uses(g):
    return [(("S", g, i), "dve") for i in range(2 * GH)]


def sc_plan3(front, back):
    return parts_of(front, back, ("back", [(("H", i), "act") for i in range(4)] + s3_uses(2)),
                    ("front", [("Q0", "act"), ("K0", "act"), ("Q1", "act"), ("K1", "act")]),
                    ("back", s3_uses(3)[:4] + turn_uses(0) + s3_uses(3)[4:6] + spread_uses(0) + s3_uses(3)[6:]
                     + [(("H", i), "act") for i in range(4, 8)]),
                    ("front", s3_uses(0)[:4]), ("back", turn_uses(1)), ("front", s3_uses(0)[4:6]), ("back", spread_uses(1)),
                    ("front", s3_uses(0)[6:] + s3_uses(1)[:4]), ("back", turn_uses(2)),
                    ("front", s3_uses(1)[4:6]), ("back", spread_uses(2)),
                    ("front", s3_uses(1)[6:]), ("back", turn_uses(3) + spread_uses(3)))


def e3_uses(g, first=0, last=GH):
    return [(("E", g, h), "act") for h in range(first, last)]


def st_plan3(front, back):
    return parts_of(front, back, ("back", [("V", "dve"), ("T2", "act")] + e3_uses(0)), ("front", [("T", "act")]),
                    ("back", e3_uses(1) + e3_uses(2) + e3_uses(3) + [("OUT", "dve")]))


NSPLIT = [8, (4, 0), 0, (4, 0)]
NGROUPS = [4, 4, 0, 4]


def build(nc, d, out):
    ctx = ExitStack()
    with ctx:
        def sb(name, shape, dt=F32, stack=ctx):
            return stack.enter_context(nc.sbuf_tensor(name, shape, dt))

        def ps(name, n=512, dt=F32):
            return ctx.enter_context(nc.psum_tensor(name, [P, n], dt))

        def sem(name):
            return ctx.enter_context(nc.semaphore(name))

        def dram(name, shape, dt=F32):
            return nc.dram_tensor(name, shape, dt, kind="Internal")

        xs = dram("xs", [BATCH * LAYERS + 1, SEQ, DIM])
        parts_dram = dram("parts_dram", [2, 4 * DIM, SEQ])
        m_dram = dram("m_dram", [GROUPS, 8, SEQ])

        xl = sb("xl", [P, TT, DIM])
        xn = sb("xn", [P, TT, DIM + 4])
        xnT = sb("xnT", [P, KT, SEQ])
        xres = sb("xres", [P, TT, DIM])
        bias_bc = sb("bias_bc", [P, 2, DIM])
        ident = sb("ident", [P, P])
        ident_bf = sb("ident_bf", [P, P], BF16)
        stats = sb("stats", [P, TT, 6])
        mv = sb("mv", [P, TT, 2])
        veps = sb("veps", [P, TT])
        rstd = sb("rstd", [P, TT])
        mhalf = sb("mhalf", [P, TT])
        attn = ExitStack()
        vext = sb("vext", [P, TT, NH, 32], F32, attn)
        vbias = sb("vbias", [P, DIM], F32, attn)
        un = sb("un", [P, 2, SEQ], F32, attn)
        oc = sb("oc", [P, KT, SEQ], F32, attn)
        uraw = sb("uraw", [P, 2, SEQ], F32, attn)
        rt = sb("rt", [P, 2, TT, GH], F32, attn)
        nmax = sb("nmax", [P, 2, TT, GH], F32, attn)
        msplit = sb("msplit", [P, 2, TT, 2, GH], F32, attn)
        mrow = sb("mrow", [8, 2, SEQ], F32, attn)
        parts = sb("parts", [P, 2, 2, SEQ], F32, attn)

        full = ExitStack()
        probs = sb("probs", [P, 2, GH * SEQ], F32, full)

        banks = [ps(f"bank{i}") for i in range(2)]
        pairs = [ps(f"pair{i}", 1024) for i in range(2)]
        bank_u = ps("bank_u")
        bank_m = ps("bank_m")

        sc = Ring(sem, "sc", banks, plans(SC_PLAN0, sc_plan1, SC_PLAN2, sc_plan3))
        st = Ring(sem, "st", pairs, plans(ST_PLAN0, st_plan1, ST_PLAN2, st_plan3))
        pu = Ring(sem, "pu", [bank_u], plans(PU_PLAN, pu_plan1, [], pu_plan1))
        pm = Ring(sem, "pm", [bank_m], plans(PM_PLAN, pm_plan1, [], pm_plan1))

        def done(ring, l, it, name):
            p, u = ring.plan[l], ring.order[l][name]
            return ring.free[p[u][1]].at(l, it, sum(x == p[u][1] for _, x in p[:u + 1]))

        opened = {by: [] for by in ("sync", "gpsimd", "scalar", "vector", "tensor")}
        opened["tensor"] += [sc.full, st.full, pu.full, pm.full]
        for ring in (sc, st, pu, pm):
            opened["scalar"].append(ring.free["act"])
            opened["vector"].append(ring.free["dve"])

        def sig(name, per, by):
            signal = Signal(sem(name), spread(per))
            opened[by].append(signal)
            return signal

        def open_signals(eng, by):
            for signal in opened[by]:
                eng.sem_inc(signal.sem, 1)

        one = [1] * LAYERS
        x_loaded = Signal(sem("x_loaded"), spread([16] * LAYERS), 16)
        ln_moments = Signal(sem("ln_moments"), spread([TT] * LAYERS), TT)
        ln_rstd = Signal(sem("ln_rstd"), spread(one), 1)
        xn_ready = Signal(sem("xn_ready"), spread([TT] * LAYERS), TT)
        xres_loaded = sig("xres_loaded", [16] * LAYERS, "sync")
        xres_ready = sig("xres_ready", [1, 1, 0, 1], "gpsimd")
        y_stored = sig("y_stored", [16] * LAYERS, "sync")
        tanh_ready = sig("tanh_ready", [4, 0, 0, 0], "scalar")
        split = sig("split", NSPLIT, "vector")
        parts_stored = [sig(f"parts_stored{i}", [64, (32, 0), 0, (32, 0)], "sync") for i in range(2)]
        stack_loaded = [sig(f"stack_loaded{g}", [64, (64, 0), 0, (64, 0)], "sync") for g in range(GROUPS)]
        m_ready = sig("m_ready", [4, (2, 2), 0, (2, 2)], "vector")
        m_stored = sig("m_stored", [64, (16, 48), 0, (16, 48)], "sync")
        m_loaded = [sig(f"m_loaded{i}", [32, (16 - 16 * i, 16 + 16 * i), 0, (16 - 16 * i, 16 + 16 * i)], "sync") for i in range(2)]
        pv_done = sig("pv_done", [16, 16, 0, 4], "tensor")
        oc_loaded = [sig(f"oc_loaded{i}", [16 * GH * n // 2 for n in NGROUPS], "sync") for i in range(2)]
        xs_copied = sem("xs_copied")
        consts = sem("consts")
        dve_setup = sem("dve_setup")
        pool_setup = sem("pool_setup")
        fences = sem("fences")

        def maxima_order(l):
            return list(range(GROUPS)) if l == ALL0 else [2, 3] * BACK[l] + [0, 1] * FRONT[l]

        def maxima_ready(l, it, g):
            return m_ready.at(l, it, 0 if l != ALL0 and g == 1 else maxima_order(l).index(g) + 1)

        def max_rows_loaded(l, it, g):
            return m_loaded[g % 2].at(l, it, 16 * (g // 2 + 1) if l == ALL0 or g % 2 else 8 * g)

        def stack_ready(l, it, g):
            return stack_loaded[g].at(l, it, 0 if l != ALL0 and g > 1 else stack_loaded[g].per[l])

        def fence(eng):
            eng.sem_inc(fences, 1)

        block = ctx.enter_context(nc.Block())
        x_tok = d["x"].rearrange("b (t p) f -> b p t f", p=P)
        xs_tok = xs[:, :, :].rearrange("b (t p) f -> b p t f", p=P)
        out_tok = out.rearrange("b (t p) f -> b p t f", p=P)
        l0 = ExitStack()
        q_a = sb("q_a", [P, 3, GH, SEQ], F32, l0)
        k_a = sb("k_a", [P, 3, GH, SEQ], F32, l0)
        hid0 = sb("hid0", [P, 8, SEQ], F32, l0)
        src0 = sb("src0", [P, 6, SEQ], F32, l0)
        tq = sb("tq", [P, KT, SEQ], F32, l0)
        wq0 = sb("wq0", [P, KT, DIM], F32, l0)
        wk0 = sb("wk0", [P, KT, DIM], F32, l0)
        wv0 = sb("wv0", [P, KT, DIM], F32, l0)
        wo0 = sb("wo0", [P, KT, DIM], F32, l0)
        bq0 = sb("bq0", [P, KT], F32, l0)
        bk0 = sb("bk0", [P, KT], F32, l0)
        b10 = sb("b10", [P, 8], F32, l0)
        j_rows = sb("j_rows", [P, KT, HD], F32, l0)
        same_head = sb("same_head", [P, NH], F32, l0)
        lam = sb("lam", [P, 1], F32, l0)
        jbd = sb("jbd", [P, KT, HD, NH], F32, l0)
        w1 = sb("w1", [P, KT, 1024], F32, l0)
        w2 = sb("w2", [P, 8, DIM], F32, l0)
        w1e = sb("w1e", [P, KT, 1024], F32, l0)
        w2e = sb("w2e", [P, 8, DIM], F32, l0)
        rows = sb("rows", [4, 4, DIM], F32, l0)
        lscale = sb("lscale", [4, 1], F32, l0)
        lmask = sb("lmask", [4, 4], F32, l0)
        ev1 = sb("ev1", [4, 4, DIM], F32, l0)
        ev2 = sb("ev2", [4, 4, DIM], F32, l0)
        l0.close()
        rows_loaded = sig("rows_loaded", [64, 0, 0, 0], "sync")
        ev_ready = sig("ev_ready", [8, 0, 0, 0], "gpsimd")

        def ln_stats(dve, l, it, step, k):
            dve.wait_ge(*(x_loaded.at(l, it, 16) if k else (x_loaded.sem, 16)))
            for t in range(TT):
                step.mark(nc.vector.bn_stats(stats[:, t, :], xl[:, t, :]))
            step.wait()
            fence(dve)
            for t in range(TT):
                nc.vector.bn_aggr(mv[:, t, :], stats[:, t, :]).then_inc(ln_moments.sem, 1)

        def ln_rsqrt(pool, l, it, step, k):
            pool.wait_ge(*(ln_moments.at(l, it, TT) if k else (ln_moments.sem, TT)))
            fence(pool)
            step.mark(nc.gpsimd.tensor_scalar(veps[:], mv[:, :, 1], EPS, None, ALU.add))
            step.wait()
            nc.gpsimd.tensor_tensor(rstd[:], veps[:], mhalf[:], ALU.pow).then_inc(ln_rstd.sem, 1)

        def ln_normalise(dve, l, it, k):
            dve.wait_ge(*(ln_rstd.at(l, it, 1) if k else (ln_rstd.sem, 1)))
            for t in range(TT):
                nc.vector.tensor_scalar(xn[:, t, 0:DIM], xl[:, t, :], mv[:, t, 0:1], rstd[:, t:t + 1],
                                        ALU.subtract, ALU.mult).then_inc(xn_ready.sem, 1)

        def pe_transpose_xn(pe, l, it):
            pe.wait_ge(*xn_ready.at(l, it, TT if l in (MAIN1, MAIN3) else 0))
            for s in st.vacated(l, it, "T"):
                pe.wait_ge(*s)
            for f in range(KT):
                for t in range(TT):
                    ins = nc.tensor.transpose(st.tile(l, "T")[:, f * SEQ + t * P:f * SEQ + (t + 1) * P],
                                              xn[:, t, f * P:(f + 1) * P], ident[:])
            ins.then_inc(st.full.sem, 1)

        def pe_project(pe, l, it, name, weight, m, width=P, rhs=None, offset=0):
            rhs = xnT if rhs is None else rhs
            for s in sc.vacated(l, it, name):
                pe.wait_ge(*s)
            for k in range(KT):
                ins = nc.tensor.matmul(sc.tile(l, name)[0:width, :], weight[:, k, m * P + offset:m * P + offset + width],
                                       rhs[:, k, :], start=(k == 0), stop=(k == KT - 1))
            ins.then_inc(sc.full.sem, 1)

        def pe_values(pe, l, it, weight):
            for s in st.vacated(l, it, "V"):
                pe.wait_ge(*s)
            n = weight.shape[2]
            for t in range(TT):
                for k in range(KT):
                    ins = nc.tensor.matmul(st.tile(l, "V")[:, t * DIM:t * DIM + n], xnT[:, k, t * P:(t + 1) * P],
                                           weight[:, k, :], start=(k == 0), stop=(k == KT - 1))
            ins.then_inc(st.full.sem, 1)

        def pe_scores(pe, l, it, g, i, q, k):
            name = ("S", g, i)
            h, qt = i // TT, i % TT
            if i == 0:
                pe.wait_ge(*stack_ready(l, it, g))
            for s in sc.vacated(l, it, name):
                pe.wait_ge(*s)
            nc.tensor.matmul(sc.tile(l, name)[:], q(g, h)[:, qt * P:(qt + 1) * P].bitcast(F32R), k(g, h).bitcast(F32R),
                             start=True, stop=True).then_inc(sc.full.sem, 1)

        def pe_max_rows(pe, l, it, g):
            pe.wait_ge(*maxima_ready(l, it, g))
            for s in pm.vacated(l, it, ("M", g)):
                pe.wait_ge(*s)
            for qt in range(TT):
                ins = nc.tensor.transpose(bank_m[0:8, qt * P:(qt + 1) * P],
                                          msplit[:, g % 2, qt, :, :].rearrange("p a h -> p (a h)"), ident[:])
            ins.then_inc(pm.full.sem, 1)

        def pe_scores_t(pe, l, it, g, kt, pair_of, between):
            if kt == 0:
                pe.wait_ge(*max_rows_loaded(l, it, g))
            for hp in range(2):
                name = ("E", g, kt, hp)
                for s in st.vacated(l, it, name):
                    pe.wait_ge(*s)
                for hh in range(2):
                    k, q = pair_of(g, 2 * hp + hh)
                    ins = nc.tensor.matmul(st.tile(l, name)[:, hh * SEQ:(hh + 1) * SEQ],
                                           k[:, kt * P:(kt + 1) * P].bitcast(F32R), q.bitcast(F32R), start=True, stop=True)
                ins.then_inc(st.full.sem, 1)
                if hp == 0:
                    between()

        def pe_weigh_values(pe, l, it, g, kt, kv=lambda g, h: GH * g + h):
            for hp in range(2):
                pe.wait_ge(*done(st, l, it, ("E", g, kt, hp)))
            if kt == 0:
                if g == 0:
                    pe.wait_ge(*done(st, l, it, "V"))
                for s in pu.vacated(l, it, ("U", g)):
                    pe.wait_ge(*s)
            for h in range(GH):
                ins = nc.tensor.matmul(bank_u[32 * h:32 * h + 32, :], vext[:, kt, kv(g, h), :],
                                       probs[:, kt % 2, h * SEQ:(h + 1) * SEQ], start=(kt == 0), stop=(kt == TT - 1))
            ins.then_inc(pv_done.sem, 1)

        def pe0(pe, it):
            l = ALL0
            pe_transpose_xn(pe, l, it)
            pe.wait_ge(*done(st, l, it, "T"))
            pe_project(pe, l, it, "Q0", wq0, 0)
            pe_project(pe, l, it, "K0", wk0, 0)
            pe_project(pe, l, it, "Q1", wq0, 1)
            pe_project(pe, l, it, "K1", wk0, 1)
            pe_values(pe, l, it, wv0)
            for i in range(4):
                hb, k = i // 2, i % 2
                for s in sc.vacated(l, it, ("W1", i)):
                    pe.wait_ge(*s)
                if i == 0:
                    pe.wait_ge(*rows_loaded.at(l, it, 64))
                    pe.wait_ge(*ev_ready.at(l, it, 8))
                nc.tensor.matmul(sc.tile(l, ("W1", i))[:], rows[:, 1, k * P:(k + 1) * P],
                                 ev1[:, 2 * hb:2 * hb + 2, :].rearrange("p a n -> p (a n)"),
                                 start=True, stop=True).then_inc(sc.full.sem, 1)
            for m in range(KT):
                name = f"J{m}"
                for s in sc.vacated(l, it, name):
                    pe.wait_ge(*s)
                pe.wait_ge(*tanh_ready.at(l, it, 3))
                for k in range(KT):
                    ins = nc.tensor.matmul(sc.tile(l, name)[:], jbd[:, k, 8 * m:8 * m + 8, :].rearrange("p e h -> p (e h)"),
                                           tq[:, k, :], start=(k == 0), stop=(k == KT - 1))
                ins.then_inc(sc.full.sem, 1)

            def hidden(i):
                if i == 0:
                    pe.wait_ge(*done(sc, l, it, ("W1", 3)))
                pe_project(pe, l, it, ("H", i), w1e, i)

            for i in range(8):
                hidden(i)
            for i in range(4):
                for s in sc.vacated(l, it, ("W2", i)):
                    pe.wait_ge(*s)
                for half in range(2):
                    ins = nc.tensor.matmul(sc.tile(l, ("W2", i))[:, half * DIM:(half + 1) * DIM],
                                           rows[:, 3, half * P:(half + 1) * P], ev2[:, i, :], start=(half == 0), stop=(half == 1))
                ins.then_inc(sc.full.sem, 1)

            def q(g, h):
                return q_a[0:96, g % 3, h, :]

            def k(g, h):
                return k_a[0:96, g % 3, h, :]

            def pair(g, h):
                return k_a[0:98, g % 3, h, :], q_a[0:98, g % 3, h, :]

            for i in range(16):
                pe_scores(pe, l, it, 0, i, q, k)
            for i in range(2):
                pe_scores(pe, l, it, 1, i, q, k)
            pe_max_rows(pe, l, it, 0)
            for i in range(2, 16):
                pe_scores(pe, l, it, 1, i, q, k)
            for g in range(GROUPS):
                for kt in range(TT):
                    at = S3_AT if g == 1 else S_AT
                    half = (at[kt] + at[kt + 1]) // 2

                    def maxima(first, last):
                        if g + 2 < GROUPS:
                            for i in range(first, last):
                                pe_scores(pe, l, it, g + 2, i, q, k)

                    pe_scores_t(pe, l, it, g, kt, pair, lambda: maxima(at[kt], half))
                    if kt == 0 and g < GROUPS - 1:
                        pe_max_rows(pe, l, it, g + 1)
                    if g or kt:
                        pe_weigh(pe, l, it, GROUPS * g + kt - 1)
                    maxima(half, at[kt + 1])
                    if g and kt == 1:
                        pe_turn_sums(pe, l, it, g - 1)
                    if g and kt == 2:
                        pe_spread_sums(pe, l, it, g - 1)
            for s in st.vacated(l, it, "OUT"):
                pe.wait_ge(*s)
            pe.wait_ge(*done(sc, l, it, ("W2", 3)))
            pe.wait_ge(*done(sc, l, it, ("H", 7)))
            for t in range(TT):
                for i in range(8):
                    nc.tensor.matmul(st.tile(l, "OUT")[:, t * DIM:(t + 1) * DIM], hid0[:, i, t * P:(t + 1) * P],
                                     w2e[:, i, :], start=(i == 0 and t % 2 == 0), stop=False)
                if t == 0:
                    pe_weigh(pe, l, it, GROUPS * TT - 1)
                if t == 1:
                    pe_turn_sums(pe, l, it, GROUPS - 1)
                if t == 2:
                    pe_spread_sums(pe, l, it, GROUPS - 1)
            pe_out_heads(pe, l, it, wo0)

        def pe_weigh(pe, l, it, n, kv=lambda g, h: GH * g + h):
            pe_weigh_values(pe, l, it, n // TT, n % TT, kv)

        def pe_turn_sums(pe, l, it, g):
            for s in sc.vacated(l, it, ("DT", g)):
                pe.wait_ge(*s)
            fence(pe)
            pe.wait_ge(*done(pu, l, it, ("U", g)))
            for t in range(TT):
                ins = nc.tensor.transpose(sc.tile(l, ("DT", g))[:, t * P:(t + 1) * P], uraw[:, g % 2, t * P:(t + 1) * P],
                                          ident[:])
            ins.then_inc(sc.full.sem, 1)

        def pe_spread_sums(pe, l, it, g):
            for s in sc.vacated(l, it, ("RB", g)):
                pe.wait_ge(*s)
            fence(pe)
            pe.wait_ge(*done(sc, l, it, ("DT", g)))
            for t in range(TT):
                for h in range(GH):
                    ins = nc.tensor.matmul(sc.tile(l, ("RB", g))[32 * h:32 * h + 32, t * P:(t + 1) * P],
                                           rt[:, g % 2, t, h:h + 1].to_broadcast([P, 32]), ident[:], start=True, stop=True)
            ins.then_inc(sc.full.sem, 1)

        def pe_out_heads(pe, l, it, weight):
            for p in range(2):
                pe.wait_ge(*oc_loaded[p].at(l, it, oc_loaded[p].per[l]))
            for t in range(TT):
                for k in range(KT):
                    ins = nc.tensor.matmul(st.tile(l, "OUT")[:, t * DIM:(t + 1) * DIM], oc[:, k, t * P:(t + 1) * P],
                                           weight[:, k, :], start=False, stop=(k == KT - 1 and t % 2 == 1))
            ins.then_inc(st.full.sem, 1)

        def act_copy_xnT(act, l, it):
            act.wait_ge(*st.filled(l, it, "T"))
            nc.scalar.activation(xnT[:, :, :].rearrange("p k n -> p (k n)"), st.tile(l, "T")[:],
                                 ACT.Copy).then_inc(st.free["act"].sem, 1)

        def act_max_rows(act, l, it, g):
            act.wait_ge(*pm.filled(l, it, ("M", g)))
            act.wait_ge(*m_stored.at(l, it, 16 * max(0, pm.order[l][("M", g)] - 1)))
            nc.scalar.activation(mrow[:, g % 2, :], bank_m[0:8, 0:SEQ], ACT.Copy).then_inc(pm.free["act"].sem, 1)

        def act_copy_sums(act, l, it, g):
            act.wait_ge(*pv_done.at(l, it, pv_done.per[POST1 if LAYER[l] == 1 else POST3 if LAYER[l] == 3 else l] // GROUPS * (g + 1)))
            act.wait_ge(*(done(sc, l, it, ("RB", g - 2)) if g > 1 else sc.free["dve"].at(l, it)))
            nc.scalar.activation(uraw[:, g % 2, :], bank_u[:], ACT.Copy).then_inc(pu.free["act"].sem, 1)

        def act_exp(act, l, it, g, kt, hp, n=2 * SEQ):
            name = ("E", g, kt, hp)
            act.wait_ge(*st.filled(l, it, name))
            if hp == 0:
                act.wait_ge(*pv_done.at(l, it, max(0, TT * g + kt - 1)))
            nc.scalar.activation(probs[:, kt % 2, hp * 2 * SEQ:hp * 2 * SEQ + n], st.tile(l, name)[:, 0:n],
                                 ACT.Exp).then_inc(st.free["act"].sem, 1)

        def act0(act, it, step):
            l = ALL0
            step.begin(l, it)
            act_copy_xnT(act, l, it)
            for m in range(KT):
                for name, bias in (("Q", bq0), ("K", bk0)):
                    act.wait_ge(*sc.filled(l, it, f"{name}{m}"))
                    if m == 0 and name == "Q":
                        act.wait_ge(*split.at(l, it))
                    nc.scalar.activation(src0[:, SLOT0[f"{name}{m}"], :], sc.tile(l, f"{name}{m}")[:], ACT.Identity,
                                         bias=bias[:, m:m + 1]).then_inc(sc.free["act"].sem, 1)
                for name in ("Q", "K"):
                    act.wait_ge(*done(sc, l, it, f"{name}{m}"))
                    dst = tq[:, m, :] if name == "Q" else src0[:, SLOT0[f"KN{m}"], :]
                    nc.scalar.activation(dst, src0[:, SLOT0[f"{name}{m}"], :], ACT.Tanh).then_inc(tanh_ready.sem, 1)
            for m in range(KT):
                act.wait_ge(*sc.filled(l, it, f"J{m}"))
                act.wait_ge(*split.at(l, it, 3))
                nc.scalar.activation(src0[:, SLOT0[f"J{m}"], :], sc.tile(l, f"J{m}")[:],
                                     ACT.Copy).then_inc(sc.free["act"].sem, 1)
            for i in range(8):
                act.wait_ge(*sc.filled(l, it, ("H", i)))
                nc.scalar.activation(hid0[:, i, :], sc.tile(l, ("H", i))[:], ACT.Gelu,
                                     bias=b10[:, i:i + 1]).then_inc(sc.free["act"].sem, 1)
            act_max_rows(act, l, it, 0)
            for g in range(GROUPS):
                for kt in range(TT):
                    for hp in range(2):
                        act_exp(act, l, it, g, kt, hp)
                    if kt == 0 and g < GROUPS - 1:
                        act_max_rows(act, l, it, g + 1)
                    if kt == 0 and g:
                        act_copy_sums(act, l, it, g - 1)
            act_copy_sums(act, l, it, GROUPS - 1)
            step.end()

        def dve_split(dve, l, it, step, i, src, scale, ready, n=P):
            dve.wait_ge(*ready)
            fence(dve)
            dve.wait_ge(*parts_stored[i % 2].at(l, it, 16 * max(0, i // 2)))
            step.mark(nc.vector.tensor_scalar(parts[0:n, i % 2, 0, :].bitcast(F32R), src, scale, None, ALU.mult))
            step.wait()
            nc.vector.scalar_tensor_tensor(parts[0:n, i % 2, 1, :].bitcast(F32R), src, scale, parts[0:n, i % 2, 0, :],
                                           ALU.mult, ALU.subtract).then_inc(split.sem, 1)

        def dve_values(dve, l, it, bias, n=NH):
            dve.wait_ge(*st.filled(l, it, "V"))
            for t in range(TT):
                src = st.tile(l, "V")[:, t * DIM:t * DIM + n * HD].rearrange("p (h e) -> p h e", e=HD)
                dst = vext[:, t, 0:n, 0:HD]
                if bias is None:
                    ins = nc.vector.tensor_copy(dst, src)
                else:
                    ins = nc.vector.tensor_tensor(dst, src, bias[:, :].rearrange("p (h e) -> p h e", e=HD), ALU.add)
            ins.then_inc(st.free["dve"].sem, 1)

        def dve_max(dve, l, it, step, g, i):
            name = ("S", g, i)
            h, qt = i // TT, i % TT
            dve.wait_ge(*sc.filled(l, it, name))
            nc.vector.tensor_reduce(nmax[:, g % 2, qt, h:h + 1], sc.tile(l, name)[:], AX, ALU.max,
                                    negate=True).then_inc(sc.free["dve"].sem, 1)

        def dve_split_max(dve, l, it, step, g, last):
            dve.wait_ge(*done(sc, l, it, last))
            step.mark(nc.vector.tensor_copy(msplit[:, g % 2, :, 0, :].bitcast(F32R), nmax[:, g % 2, :, :]))
            step.wait()
            nc.vector.tensor_tensor(msplit[:, g % 2, :, 1, :].bitcast(F32R), nmax[:, g % 2, :, :], msplit[:, g % 2, :, 0, :],
                                    ALU.subtract).then_inc(m_ready.sem, 1)

        def dve_invert_sums(dve, l, it, g):
            dve.wait_ge(*sc.filled(l, it, ("DT", g)))
            sums = sc.tile(l, ("DT", g))[:, :].rearrange("p (t h e) -> p t h e", t=TT, h=GH)[:, :, :, HD]
            nc.vector.reciprocal(rt[:, g % 2, :, :], sums).then_inc(sc.free["dve"].sem, 1)

        def dve_normalise_heads(dve, l, it, g):
            dve.wait_ge(*sc.filled(l, it, ("RB", g)))
            fence(dve)
            dve.wait_ge(*oc_loaded[g % 2].at(l, it, 16 * GH * (g // 2)))
            nc.vector.tensor_tensor(un[:, g % 2, :], sc.tile(l, ("RB", g))[:], uraw[:, g % 2, :],
                                    ALU.mult).then_inc(sc.free["dve"].sem, 1)

        def dve_add_out(dve, l, it):
            dve.wait_ge(*st.filled(l, it, "OUT"))
            fence(dve)
            dve.wait_ge(*xres_ready.at(l, it, 1))
            flat = xres[:, :, :].rearrange("p t f -> p (t f)")
            nc.vector.tensor_tensor(flat, st.tile(l, "OUT")[:], flat, ALU.add).then_inc(st.free["dve"].sem, 1)

        def dve0(dve, it, step):
            l = ALL0
            step.begin(l, it)

            def split(i):
                name = SPLITS0[i]
                ready = tanh_ready.at(l, it, 2 + 2 * (i - 4)) if name[:2] == "KN" else done(sc, l, it, name)
                dve_split(dve, l, it, step, i, src0[:, SLOT0[name], :], 0.25 if name[0] == "Q" else 1.0, ready)

            for i in range(4):
                split(i)
            dve_values(dve, l, it, vbias)
            for i in range(4):
                hb, k = i // 2, i % 2
                dve.wait_ge(*sc.filled(l, it, ("W1", i)))
                nc.vector.tensor_tensor(w1e[:, k, hb * 512:(hb + 1) * 512], sc.tile(l, ("W1", i))[:],
                                        w1[:, k, hb * 512:(hb + 1) * 512], ALU.add).then_inc(sc.free["dve"].sem, 1)
            for i in range(4, 8):
                split(i)
            for i in range(4):
                dve.wait_ge(*sc.filled(l, it, ("W2", i)))
                nc.vector.tensor_tensor(w2e[:, 2 * i:2 * i + 2, :].rearrange("p a n -> p (a n)"), sc.tile(l, ("W2", i))[:],
                                        w2[:, 2 * i:2 * i + 2, :].rearrange("p a n -> p (a n)"),
                                        ALU.add).then_inc(sc.free["dve"].sem, 1)
            for g in range(2):
                for i in range(16):
                    dve_max(dve, l, it, step, g, i)
                dve_split_max(dve, l, it, step, g, ("S", g, 15))
            ln_stats(dve, l, it, step, 1)
            for g in range(GROUPS):
                at = S3_AT if g == 1 else S_AT
                for n, (first, last) in enumerate(((0, at[2]), (at[2], at[3]), (at[3], 16))):
                    if g + 2 < GROUPS:
                        for i in range(first, last):
                            dve_max(dve, l, it, step, g + 2, i)
                    if g and n == 0:
                        dve_invert_sums(dve, l, it, g - 1)
                    if g and n == 1:
                        dve_normalise_heads(dve, l, it, g - 1)
                if g + 2 < GROUPS:
                    dve_split_max(dve, l, it, step, g + 2, ("S", g + 2, 15))
                if g == 1:
                    dve.wait_ge(*rows_loaded.at(l, it, 64))
                    ln_normalise(dve, l, it, 1)
            dve_invert_sums(dve, l, it, GROUPS - 1)
            dve_normalise_heads(dve, l, it, GROUPS - 1)
            dve_add_out(dve, l, it)
            step.end()

        def pool_residual(pool, l, it, step):
            pool.wait_ge(*xres_loaded.at(l, it, 16))
            nc.gpsimd.tensor_tensor(xres[:], xres[:], bias_bc[:, 0:1, :].to_broadcast([P, TT, DIM]),
                                    ALU.add).then_inc(xres_ready.sem, 1)

        def pool0(pool, it, step):
            l = ALL0
            step.begin(l, it)
            pool.wait_ge(*rows_loaded.at(l, it, 64))
            pool.wait_ge(*sc.full.at(l, it))
            fence(pool)
            for i in range(4):
                nc.gpsimd.tensor_scalar(ev1[:, i, :], rows[:, 0, :], lmask[:, i:i + 1], None,
                                        ALU.mult).then_inc(ev_ready.sem, 1)
                nc.gpsimd.tensor_scalar(ev2[:, :, 64 * i:64 * i + 64],
                                        rows[:, 2, :].rearrange("p (r j) -> p j r", j=4), lmask[:, i:i + 1], None,
                                        ALU.mult).then_inc(ev_ready.sem, 1)
            pool_residual(pool, l, it, step)
            ln_rsqrt(pool, l, it, step, 1)
            step.end()

        def sp_load_next(sp, l, it):
            sp.wait_ge(*xn_ready.at(l, it))
            fence(sp)
            sp.wait_ge(xs_copied, 32)
            sp.wait_ge(*y_stored.at(l, it))
            fence(sp)
            slot = it + (BATCH * LAYER[l] + (BATCH - 1 if l in (POST1, POST3) else 0))
            sp.dma_start(xl[:], xs_tok[slot + 1]).then_inc(x_loaded.sem, 16)
            sp.dma_start(xres[:], xs_tok[slot]).then_inc(xres_loaded.sem, 16)

        def sp_store_parts(sp, l, it, i, where):
            side, at, size, n = where
            sp.wait_ge(*split.at(l, it, i + 1))
            dst = parts_dram[side, 0:2 * size, :].rearrange("(a f) n -> f a n", a=2)
            sp.dma_start(dst[at:at + n, :, :], parts[0:n, i % 2, :, :]).then_inc(parts_stored[i % 2].sem, 16)

        def sp_stack(sp, l, it, g, side, tile, size, width, heads):
            src = parts_dram[side, 0:2 * size, :].rearrange("(a e h) n -> (a e) h n", a=2, e=width)
            for first, n, at in ((0, 2, 0), (0, 1, 2)) if side == 0 else ((0, 1, 0), (0, 2, 1)):
                sp.dma_start(tile[at * width:(at + n) * width], src[first * width:(first + n) * width, heads])\
                  .then_inc(stack_loaded[g].sem, 16)

        def sp_max_rows(sp, l, it, g, q_rows):
            sp.wait_ge(*done(pm, l, it, ("M", g)))
            sp.dma_start(m_dram[g], mrow[:, g % 2, :]).then_inc(m_stored.sem, 16)
            sp.wait_ge(*m_stored.at(l, it, 16 * (pm.order[l][("M", g)] + 1)))
            sp.dma_start(q_rows(g), m_dram[g].rearrange("(a h) n -> a h n", a=2)).then_inc(m_loaded[g % 2].sem, 16)

        def sp_gather_heads(sp, l, it, g):
            sp.wait_ge(*done(sc, l, it, ("RB", g)))
            for h in range(GH):
                at = 64 * (g % 2) + HD * h
                sp.dma_start(oc[at:at + HD, g // 2, :], un[32 * h:32 * h + HD, g % 2, :])\
                  .then_inc(oc_loaded[g % 2].sem, 16)

        def sp_store_out(sp, l, it):
            sp.wait_ge(*done(st, l, it, "OUT"))
            fence(sp)
            batch = it + (BATCH - 1 if l in (POST1, POST3) else 0)
            dst = xs_tok[batch + BATCH * (LAYER[l] + 1)] if LAYER[l] < LAYERS - 1 else out_tok[batch]
            sp.dma_start(dst, xres[:]).then_inc(y_stored.sem, 16)

        def sp_rounds(sp, l, it, stores, stack, q_rows):
            front, back = FRONT[l], BACK[l]
            if back:
                sp_load_next(sp, l, it)
                sp_max_rows(sp, l, it, 1, q_rows)
                sp_max_rows(sp, l, it, 2, q_rows)
            if front:
                for g in range(GROUPS):
                    sp.wait_ge(*stack_loaded[g].at(l, it))
                    fence(sp)
                for i, where in enumerate(stores):
                    sp_store_parts(sp, l, it, i, where)
                for i in range(2):
                    sp.wait_ge(*parts_stored[i].at(l, it, 16 * 2))
                    fence(sp)
                stack(0)
            if back:
                sp_max_rows(sp, l, it, 3, q_rows)
            if front:
                stack(1)
            if back:
                sp_gather_heads(sp, l, it, 0)
                sp_gather_heads(sp, l, it, 1)
            if front:
                stack(2)
                sp_max_rows(sp, l, it, 0, q_rows)
            if back:
                sp_gather_heads(sp, l, it, 2)
            if front:
                stack(3)
            if back:
                sp_gather_heads(sp, l, it, 3)
                sp_store_out(sp, l, it)

        def sp0(sp, it):
            l = ALL0
            for j, first in enumerate((1, 2, 9, 10)):
                if j == 0:
                    sp.wait_ge(*xn_ready.at(l, it))
                    fence(sp)
                    sp.wait_ge(*sc.full.at(l, it))
                    fence(sp)
                    sp.wait_ge(*ev_ready.at(l, it))
                sp.dma_start(rows[:, j, :], xn[first:first + 7:2, 0, 0:DIM]).then_inc(rows_loaded.sem, 16)
            sp_load_next(sp, l, it)
            for i in range(8):
                side, s, m = WHERE0[SPLITS0[i]]
                sp_store_parts(sp, l, it, i, (side, s * DIM + m * P, 2 * DIM, P))

            def stack(g):
                if g < 3:
                    sp.wait_ge(*st.full.at(l, it))
                    fence(sp)
                else:
                    sp.wait_ge(*st.filled(l, it, ("E", g - 3, TT - 1, 1)))
                for side, tile in enumerate((q_a, k_a)):
                    sp_stack(sp, l, it, g, side, tile[:, g % 3, :, :], 2 * DIM, 2 * HD, slice(GH * g, GH * g + GH))

            for i in range(2):
                sp.wait_ge(*parts_stored[i].at(l, it, 16 * 4))
                fence(sp)
            for g in range(3):
                stack(g)

            def q_rows(g):
                return q_a[96:98, g % 3, :, :]

            sp_max_rows(sp, l, it, 0, q_rows)
            sp_max_rows(sp, l, it, 1, q_rows)
            stack(3)
            sp_max_rows(sp, l, it, 2, q_rows)
            sp_gather_heads(sp, l, it, 0)
            sp_max_rows(sp, l, it, 3, q_rows)
            sp_gather_heads(sp, l, it, 1)
            sp_gather_heads(sp, l, it, 2)
            sp_gather_heads(sp, l, it, 3)
            sp_store_out(sp, l, it)

        l1 = ExitStack()
        q_1 = sb("q_1", [P, GROUPS, GH, SEQ], F32, l1)
        k_1 = sb("k_1", [P, GROUPS, SEQ], F32, l1)
        raw1 = sb("raw1", [P, 2, SEQ], F32, l1)
        rawk = sb("rawk", [32, 2, SEQ], F32, l1)
        rot1 = sb("rot1", [P, 2, SEQ], F32, l1)
        rotk = sb("rotk", [32, 2, SEQ], F32, l1)
        mul1 = sb("mul1", [P, 4, SEQ], F32, l1)
        mulk = sb("mulk", [32, 4, SEQ], F32, l1)
        wq1 = sb("wq1", [P, KT, DIM], F32, l1)
        wk1 = sb("wk1", [P, KT, 64], F32, l1)
        wv1 = sb("wv1", [P, KT, 64], F32, l1)
        wo1 = sb("wo1", [P, KT, DIM], F32, l1)
        cos1 = sb("cos1", [P, SEQ], F32, l1)
        sin1 = sb("sin1", [P, SEQ], F32, l1)
        cosk = sb("cosk", [32, SEQ], F32, l1)
        sink = sb("sink", [32, SEQ], F32, l1)
        w1x = sb("w1x", [P, KT, P], F32, l1)
        w1s = sb("w1s", [P, KT, P], F32, l1)
        b11 = sb("b11", [P, 1], F32, l1)
        w21 = sb("w21", [P, 64], F32, l1)
        b21 = sb("b21", [P, 64], F32, l1)
        tau = sb("tau", [P, 4], F32, l1)
        wih = sb("wih", [P, KT, 3 * DIM], F32, l1)
        whh = sb("whh", [P, KT, 3 * DIM], F32, l1)
        bih = sb("bih", [P, 6], F32, l1)
        bhh = sb("bhh", [P, 6], F32, l1)
        wvs = sb("wvs", [P, KT, DIM], F32, l1)
        bvs = sb("bvs", [P, KT], F32, l1)
        wos = sb("wos", [P, KT, DIM], F32, l1)
        slots = sb("slots", [64, DIM], F32, l1)
        slot_scale = sb("slot_scale", [64, 1], F32, l1)
        sixty_fourth = sb("sixty_fourth", [64, 2], F32, l1)
        ones_sq = sb("ones_sq", [P, P], F32, l1)
        slot_mean = sb("slot_mean", [P, KT], F32, l1)
        hsT = sb("hsT", [P, KT, 64], F32, l1)
        ghb = sb("ghb", [P, 6, 64], F32, l1)
        hid1 = sb("hid1", [P, SEQ], F32, l1)
        logits = sb("logits", [P, TT, 64], F32, l1)
        logits_r = sb("logits_r", [P, TT, 64], F32, l1)
        top = sb("top", [P, TT, 8], F32, l1)
        ntop = sb("ntop", [P, TT], F32, l1)
        e_all = sb("e_all", [P, TT, 64], F32, l1)
        e_rest = sb("e_rest", [P, TT, 64], F32, l1)
        asum = sb("asum", [P, 2, TT], F32, l1)
        alpha = sb("alpha", [P, TT, 64], F32, l1)
        alphaT = sb("alphaT", [64, SEQ], F32, l1)
        wsum = sb("wsum", [P, 2, 64], F32, l1)
        gi = sb("gi", [P, KT, 64], F32, l1)
        rz = sb("rz", [P, 4, 64], F32, l1)
        gru = sb("gru", [P, 6, 64], F32, l1)
        h_new = sb("h_new", [P, KT, 64], F32, l1)
        svT = sb("svT", [P, KT, 64], F32, l1)
        sv2 = sb("sv2", [64, DIM], F32, l1)
        l1.close()

        def bc(name, n, parts_n=P):
            return d[name].rearrange("(a n) -> a n", a=1).to_broadcast([parts_n, n])

        loads1 = [(wq1, d["wq1"]), (wk1, d["wk1"]), (wv1, d["wv1"]), (cos1, d["cos1"]), (sin1, d["sin1"]),
                  (cosk, d["cosk"]), (sink, d["sink"]), (w1x, d["w1x"]), (w1s, d["w1s"]), (b11, d["b11"]),
                  (w21, d["w21"]), (b21, bc("b21", 64)), (slots, d["slots"]), (slot_scale, d["slot_scale"]),
                  (whh, d["whh"]), (bih, d["bih"]), (bhh, d["bhh"]), (wih, d["wih"]), (wvs, d["wvs"]),
                  (bvs, d["bvs"]), (wos, d["wos"]), (wo1, d["wo1"])]
        loaded1 = sem("loaded1")
        N1 = 16 * (len(loads1) + 2)
        pe_set1, dve_set1, dve_pre1 = sem("pe_set1"), sem("dve_set1"), sem("dve_pre1")
        logits_done = sig("logits_done", [0, (2, 0), 0, 0], "vector")
        e_done = sig("e_done", [0, (1, 0), 0, 0], "scalar")
        alpha_done = sig("alpha_done", [0, (1, 0), 0, 0], "vector")
        gi_done = sig("gi_done", [0, 1, 0, 0], "vector")
        gates_in = sig("gates_in", [0, (0, 2), 0, 0], "vector")
        gates_out = sig("gates_out", [0, (0, 2), 0, 0], "scalar")
        h_done = sig("h_done", [0, 1, 0, 0], "vector")
        rotated = sig("rotated", [0, (4, 0), 0, 0], "vector")

        def sp_setup1(sp):
            sp.wait_ge(*y_stored.at(PRE1, 0))
            for dst, src in loads1:
                sp.dma_start(dst[:], src).then_inc(loaded1, 16)
            sp.dma_start(bias_bc[:, 0, :], bc("bo1", DIM)).then_inc(loaded1, 16)
            sp.dma_start(tau[:, 0:1], bc("tau", 1)).then_inc(loaded1, 16)

        def pe_setup1(pe):
            pe.wait_ge(dve_pre1, 5)
            for f in range(KT):
                nc.tensor.transpose(banks[0][:, f * 64:(f + 1) * 64], slots[:, f * P:(f + 1) * P], ident[0:64, 0:64])
            for f in range(KT):
                ins = nc.tensor.matmul(banks[0][:, 2 * P + f:2 * P + f + 1], slots[:, f * P:(f + 1) * P],
                                       sixty_fourth[:, 0:1], start=True, stop=True)
            ins.then_inc(pe_set1, 1)
            pe.wait_ge(dve_set1, 2)
            for k in range(KT):
                nc.tensor.matmul(banks[1][:, 0:1], w1s[:, k, :], slot_mean[:, k:k + 1], start=(k == 0), stop=(k == 1))
            for j in range(6):
                for k in range(KT):
                    ins = nc.tensor.matmul(banks[1][:, 64 + j * 64:128 + j * 64],
                                           whh[:, k, j * P:(j + 1) * P], hsT[:, k, :], start=(k == 0), stop=(k == 1))
            ins.then_inc(pe_set1, 1)

        def dve_setup1(dve):
            dve.wait_ge(loaded1, N1)
            nc.vector.tensor_scalar(slots[:], slots[:], slot_scale[:, 0:1], None, ALU.mult).then_inc(dve_pre1, 1)
            nc.vector.memset(sixty_fourth[:], 1.0 / 64).then_inc(dve_pre1, 1)
            nc.vector.memset(ones_sq[:], 1.0).then_inc(dve_pre1, 1)
            nc.vector.memset(k_1[32:50, :, :], 1.0).then_inc(dve_pre1, 1)
            nc.vector.tensor_scalar(tau[:, 1:2], tau[:, 0:1], -1.0, None, ALU.mult).then_inc(dve_pre1, 1)
            dve.wait_ge(dve_pre1, 5)
            nc.vector.tensor_tensor(tau[:, 2:3], tau[:, 0:1], tau[:, 1:2], ALU.max).then_inc(dve_pre1, 1)
            dve.wait_ge(dve_pre1, 6)
            nc.vector.tensor_scalar(tau[:, 2:3], tau[:, 2:3], 0.1, None, ALU.add).then_inc(dve_pre1, 1)
            dve.wait_ge(dve_pre1, 7)
            nc.vector.reciprocal(tau[:, 3:4], tau[:, 2:3]).then_inc(dve_pre1, 1)
            dve.wait_ge(dve_pre1, 8)
            nc.vector.tensor_scalar(b21[:], b21[:], tau[:, 3:4], None, ALU.mult).then_inc(dve_pre1, 1)
            dve.wait_ge(pe_set1, 1)
            nc.vector.tensor_copy(hsT[:, :, :].rearrange("p k n -> p (k n)"), banks[0][:, 0:P]).then_inc(dve_set1, 1)
            nc.vector.tensor_copy(slot_mean[:], banks[0][:, 2 * P:2 * P + KT]).then_inc(dve_set1, 1)
            dve.wait_ge(pe_set1, 2)
            nc.vector.tensor_tensor(b11[:], banks[1][:, 0:1], b11[:], ALU.add).then_inc(dve_set1, 1)
            nc.vector.tensor_tensor(ghb[:], banks[1][:, 64:448].rearrange("p (j n) -> p j n", j=6),
                                    bhh[:, :, None].to_broadcast([P, 6, 64]), ALU.add).then_inc(dve_set1, 1)
            dve.wait_ge(dve_set1, 4)
            nc.vector.tensor_tensor(ghb[:, 0:4, :], ghb[:, 0:4, :], bih[:, 0:4, None].to_broadcast([P, 4, 64]),
                                    ALU.add).then_inc(dve_set1, 1)
            dve.wait_ge(dve_set1, 5)
            dve.wait_ge(dve_pre1, 9)

        def kv_of_group(g, h):
            return g

        def pe1(pe, l, it):
            front, back = FRONT[l], BACK[l]

            def q(g, h):
                return q_1[0:48, g, h, :]

            def k(g, h):
                return k_1[0:48, g, :]

            def pair(g, h):
                return k_1[0:50, g, :], q_1[0:50, g, h, :]

            if back:
                for s in sc.vacated(l, it, "AT"):
                    pe.wait_ge(*s)
                fence(pe)
                pe.wait_ge(*alpha_done.at(l, it))
                fence(pe)
                for t in range(TT):
                    ins = nc.tensor.transpose(sc.tile(l, "AT")[0:64, t * P:(t + 1) * P], alpha[:, t, :], ident[:])
                ins.then_inc(sc.full.sem, 1)
                for s in sc.vacated(l, it, "SI"):
                    pe.wait_ge(*s)
                for f in range(KT + 1):
                    for t in range(TT):
                        lhs = xn[:, t, f * P:(f + 1) * P] if f < KT else ones_sq[:]
                        ins = nc.tensor.matmul(sc.tile(l, "SI")[:, f * 64:(f + 1) * 64], lhs, alpha[:, t, :],
                                               start=(t == 0), stop=(t == TT - 1))
                ins.then_inc(sc.full.sem, 1)
                pe_values(pe, l, it, wv1)
            for g in range(GROUPS):
                for kt in range(TT):
                    def maxima(first, last):
                        if back if g < 2 else front:
                            for i in range(first, last):
                                pe_scores(pe, l, it, (g + 2) % GROUPS, 4 * kt + i, q, k)

                    if back:
                        pe_scores_t(pe, l, it, g, kt, pair, lambda: maxima(0, 2))
                        if kt == 0 and g < GROUPS - 1:
                            pe_max_rows(pe, l, it, g + 1)
                    else:
                        maxima(0, 2)
                    if front and g == 0 and kt == 1:
                        pe_transpose_xn(pe, l, it)
                    if back and (g or kt):
                        pe_weigh(pe, l, it, GROUPS * g + kt - 1, kv_of_group)
                    maxima(2, 4)
                    if front and g == 3 and kt == 1:
                        pe_max_rows(pe, l, it, 0)
                    if front and g == 1 and kt == 1:
                        for s in sc.vacated(l, it, "L"):
                            pe.wait_ge(*s)
                        pe.wait_ge(*done(sc, l, it, "H"))
                        for t in range(TT):
                            ins = nc.tensor.matmul(sc.tile(l, "L")[:, t * 64:(t + 1) * 64], hid1[:, t * P:(t + 1) * P], w21[:],
                                                   start=True, stop=True)
                        ins.then_inc(sc.full.sem, 1)
                    if back and g and kt == 1:
                        pe_turn_sums(pe, l, it, g - 1)
                    if back and g and kt == 2:
                        pe_spread_sums(pe, l, it, g - 1)
                if front and g == 0:
                    pe.wait_ge(*done(st, l, it, "T"))
                    pe_project(pe, l, it, "QE", wq1, 0)
                    pe_project(pe, l, it, "QO", wq1, 1)
                    pe_project(pe, l, it, "KK", wk1, 0, 64)
                    pe_project(pe, l, it, "H", w1x, 0)
                if back and g == 1:
                    for s in sc.vacated(l, it, "GX"):
                        pe.wait_ge(*s)
                    pe.wait_ge(*gi_done.at(l, it, 1))
                    for j in range(6):
                        for k_ in range(KT):
                            ins = nc.tensor.matmul(sc.tile(l, "GX")[:, j * 64:(j + 1) * 64], wih[:, k_, j * P:(j + 1) * P],
                                                   gi[:, k_, :], start=(k_ == 0), stop=(k_ == 1))
                    ins.then_inc(sc.full.sem, 1)
                if back and g == 2:
                    for s in sc.vacated(l, it, "SV"):
                        pe.wait_ge(*s)
                    pe.wait_ge(*h_done.at(l, it, 1))
                    for m in range(KT):
                        for k_ in range(KT):
                            ins = nc.tensor.matmul(sc.tile(l, "SV")[:, m * 64:(m + 1) * 64], wvs[:, k_, m * P:(m + 1) * P],
                                                   h_new[:, k_, :], start=(k_ == 0), stop=(k_ == 1))
                    ins.then_inc(sc.full.sem, 1)
            if back:
                for s in sc.vacated(l, it, "Z2"):
                    pe.wait_ge(*s)
                pe.wait_ge(*done(sc, l, it, "SV"))
                for k_ in range(KT):
                    ins = nc.tensor.matmul(sc.tile(l, "Z2")[0:64, 0:DIM], svT[:, k_, :], wos[:, k_, :],
                                           start=(k_ == 0), stop=(k_ == 1))
                ins.then_inc(sc.full.sem, 1)
                pe_weigh(pe, l, it, GROUPS * TT - 1, kv_of_group)
                pe_turn_sums(pe, l, it, GROUPS - 1)
                for s in st.vacated(l, it, "OUT"):
                    pe.wait_ge(*s)
                pe.wait_ge(*done(sc, l, it, "Z2"))
                for t in range(TT):
                    nc.tensor.matmul(st.tile(l, "OUT")[:, t * DIM:(t + 1) * DIM], alphaT[:, t * P:(t + 1) * P], sv2[:],
                                     start=(t % 2 == 0), stop=False)
                pe_spread_sums(pe, l, it, GROUPS - 1)
                pe_out_heads(pe, l, it, wo1)

        def act1(act, l, it, step):
            front, back = FRONT[l], BACK[l]
            step.begin(l, it)
            if back:
                act.wait_ge(*sc.filled(l, it, "AT"))
                nc.scalar.activation(alphaT[:], sc.tile(l, "AT")[0:64, :], ACT.Copy).then_inc(sc.free["act"].sem, 1)
            for g in range(GROUPS):
                for kt in range(TT):
                    if back:
                        for hp in range(2):
                            act_exp(act, l, it, g, kt, hp)
                        if kt == 0 and g < GROUPS - 1:
                            act_max_rows(act, l, it, g + 1)
                        if kt == 0 and g:
                            act_copy_sums(act, l, it, g - 1)
                    if front and g == 0 and kt == 1:
                        act_copy_xnT(act, l, it)
                    if front and g == 3 and kt == 1:
                        act_max_rows(act, l, it, 0)
                if front and g == 0:
                    for m, name in enumerate(("QE", "QO")):
                        act.wait_ge(*sc.filled(l, it, name))
                        nc.scalar.activation(raw1[:, m, :], sc.tile(l, name)[:], ACT.Copy).then_inc(sc.free["act"].sem, 1)
                    act.wait_ge(*sc.filled(l, it, "KK"))
                    nc.scalar.activation(rawk[:, 0, :], sc.tile(l, "KK")[0:32, :], ACT.Copy)
                    nc.scalar.activation(rawk[:, 1, :], sc.tile(l, "KK")[32:64, :], ACT.Copy).then_inc(sc.free["act"].sem, 1)
                    act.wait_ge(*sc.filled(l, it, "H"))
                    nc.scalar.activation(hid1[:], sc.tile(l, "H")[:], ACT.Gelu, bias=b11[:, 0:1])\
                      .then_inc(sc.free["act"].sem, 1)
                if front and g == 1:
                    act.wait_ge(*logits_done.at(l, it, 2))
                    for t in range(TT):
                        nc.scalar.activation(e_all[:, t, :], logits[:, t, :], ACT.Exp, bias=ntop[:, t:t + 1])
                        ins = nc.scalar.activation(e_rest[:, t, :], logits_r[:, t, :], ACT.Exp, bias=ntop[:, t:t + 1])
                    ins.then_inc(e_done.sem, 1)
                if back and g == 1:
                    act.wait_ge(*gates_in.at(l, it, 1))
                    nc.scalar.activation(rz[:], rz[:], ACT.Tanh, scale=0.5).then_inc(gates_out.sem, 1)
                    act.wait_ge(*gates_in.at(l, it, 2))
                    for j in range(2):
                        ins = nc.scalar.activation(gru[:, 2 + j, :], gru[:, j, :], ACT.Tanh, bias=bih[:, 4 + j:5 + j])
                    ins.then_inc(gates_out.sem, 1)
                if back and g == 2:
                    act.wait_ge(*sc.filled(l, it, "SV"))
                    for m in range(KT):
                        ins = nc.scalar.activation(svT[:, m, :], sc.tile(l, "SV")[:, m * 64:(m + 1) * 64], ACT.Identity,
                                                   bias=bvs[:, m:m + 1])
                    ins.then_inc(sc.free["act"].sem, 1)
            if back:
                act.wait_ge(*sc.filled(l, it, "Z2"))
                nc.scalar.activation(sv2[:], sc.tile(l, "Z2")[0:64, 0:DIM], ACT.Copy).then_inc(sc.free["act"].sem, 1)
                act_copy_sums(act, l, it, GROUPS - 1)
            step.end()

        def dve1(dve, l, it, step):
            front, back = FRONT[l], BACK[l]
            step.begin(l, it)

            def rotate(raw, mul, rot, cos, sin):
                for j, (m, table) in enumerate(((0, cos), (1, sin), (0, sin), (1, cos))):
                    step.mark(nc.vector.tensor_tensor(mul[:, j, :], raw[:, m, :], table[:], ALU.mult))
                step.wait()
                nc.vector.tensor_tensor(rot[:, 0, :], mul[:, 0, :], mul[:, 1, :], ALU.subtract).then_inc(rotated.sem, 1)
                nc.vector.tensor_tensor(rot[:, 1, :], mul[:, 2, :], mul[:, 3, :], ALU.add).then_inc(rotated.sem, 1)

            def project():
                dve.wait_ge(*done(sc, l, it, "QO"))
                rotate(raw1, mul1, rot1, cos1, sin1)
                for m in range(2):
                    if back:
                        for i in range(2 * m, 2 * m + 2):
                            dve_max(dve, l, it, step, 3, i)
                    dve_split(dve, l, it, step, m, rot1[:, m, :], 1.0 / 16, rotated.at(l, it, 2))
                if back:
                    for i in range(4, 6):
                        dve_max(dve, l, it, step, 3, i)
                dve.wait_ge(*done(sc, l, it, "KK"))
                rotate(rawk, mulk, rotk, cosk, sink)
                for m in range(2):
                    dve_split(dve, l, it, step, 2 + m, rotk[:, m, :], 1.0, rotated.at(l, it, 4), 32)

            def route():
                dve.wait_ge(*sc.filled(l, it, "L"))
                nc.vector.scalar_tensor_tensor(logits[:], sc.tile(l, "L")[:, 0:256].rearrange("p (t n) -> p t n", t=TT),
                                               tau[:, 3:4], b21[:, None, :].to_broadcast([P, TT, 64]),
                                               ALU.mult, ALU.add).then_inc(sc.free["dve"].sem, 1)
                dve.wait_ge(*done(sc, l, it, "L"))
                fence(dve)
                for t in range(TT):
                    step.mark(nc.vector.max(top[:, t, :], logits[:, t, :]))
                step.wait()
                nc.vector.tensor_scalar(ntop[:], top[:, :, 0], -1.0, None, ALU.mult).then_inc(logits_done.sem, 1)
                for t in range(TT):
                    ins = nc.vector.match_replace(logits_r[:, t, :], top[:, t, :], logits[:, t, :], -1e30)
                ins.then_inc(logits_done.sem, 1)

            def weigh_slots():
                dve.wait_ge(*e_done.at(l, it, 1))
                step.mark(nc.vector.tensor_tensor(e_all[:], e_all[:], e_rest[:], ALU.subtract))
                step.wait()
                step.mark(nc.vector.tensor_reduce(asum[:, 0, :], e_all[:], AX, ALU.add))
                step.wait()
                step.mark(nc.vector.reciprocal(asum[:, 1, :], asum[:, 0, :]))
                step.wait()
                nc.vector.tensor_tensor(alpha[:], e_all[:], asum[:, 1, :, None].to_broadcast([P, TT, 64]),
                                        ALU.mult).then_inc(alpha_done.sem, 1)

            def slot_means():
                dve.wait_ge(*sc.filled(l, it, "SI"))
                step.mark(nc.vector.tensor_scalar(wsum[:, 0, :], sc.tile(l, "SI")[:, 128:192], 1e-8, None, ALU.add))
                step.wait()
                step.mark(nc.vector.reciprocal(wsum[:, 1, :], wsum[:, 0, :]))
                step.wait()
                step.mark(nc.vector.tensor_tensor(gi[:], sc.tile(l, "SI")[:, 0:128].rearrange("p (k n) -> p k n", k=KT),
                                                  wsum[:, 1:2, :].to_broadcast([P, KT, 64]), ALU.mult))
                step.wait()
                dve.sem_inc(gi_done.sem, 1)
                dve.sem_inc(sc.free["dve"].sem, 1)

            def update_slots():
                gx = sc.tile(l, "GX")[:, 0:384].rearrange("p (j n) -> p j n", j=6)
                dve.wait_ge(*sc.filled(l, it, "GX"))
                nc.vector.tensor_tensor(rz[:], gx[:, 0:4, :], ghb[:, 0:4, :], ALU.add).then_inc(gates_in.sem, 1)
                dve.wait_ge(*gates_out.at(l, it, 1))
                step.mark(nc.vector.tensor_scalar(rz[:], rz[:], 0.5, 0.5, ALU.mult, ALU.add))
                step.wait()
                step.mark(nc.vector.tensor_tensor(gru[:, 4:6, :], rz[:, 0:2, :], ghb[:, 4:6, :], ALU.mult))
                step.wait()
                step.mark(nc.vector.tensor_tensor(gru[:, 0:2, :], gx[:, 4:6, :], gru[:, 4:6, :], ALU.add))
                step.wait()
                dve.sem_inc(gates_in.sem, 1)
                dve.sem_inc(sc.free["dve"].sem, 1)
                dve.wait_ge(*gates_out.at(l, it, 2))
                step.mark(nc.vector.tensor_tensor(gru[:, 4:6, :], hsT[:], gru[:, 2:4, :], ALU.subtract))
                step.wait()
                step.mark(nc.vector.tensor_tensor(gru[:, 4:6, :], gru[:, 4:6, :], rz[:, 2:4, :], ALU.mult))
                step.wait()
                nc.vector.tensor_tensor(h_new[:], gru[:, 4:6, :], gru[:, 2:4, :], ALU.add).then_inc(h_done.sem, 1)

            def maxima(g, first, last):
                for i in range(first, last):
                    dve_max(dve, l, it, step, g, i)
                if last == 16:
                    dve_split_max(dve, l, it, step, g, ("S", g, 15))

            if back:
                slot_means()
                dve_values(dve, l, it, None, 4)
                ln_stats(dve, l, it, step, 1)
                maxima(2, 0, 4)
                ln_normalise(dve, l, it, 1)
                maxima(2, 4, 16)
            if front:
                project()
            if back:
                maxima(3, 6 if front else 0, 8)
            if front:
                route()
            if back:
                dve_invert_sums(dve, l, it, 0)
                maxima(3, 8, 12)
                dve_normalise_heads(dve, l, it, 0)
                maxima(3, 12, 16)
            if front:
                weigh_slots()
            if back:
                update_slots()
            for g in range(2):
                for first, last in ((0, 8), (8, 12), (12, 16)):
                    if front:
                        maxima(g, first, last)
                    if back and first == 0:
                        dve_invert_sums(dve, l, it, g + 1)
                    if back and first == 8:
                        dve_normalise_heads(dve, l, it, g + 1)
            if back:
                dve_invert_sums(dve, l, it, GROUPS - 1)
                dve_normalise_heads(dve, l, it, GROUPS - 1)
                dve_add_out(dve, l, it)
            step.end()

        def pool1(pool, l, it, step):
            step.begin(l, it)
            if BACK[l]:
                ln_rsqrt(pool, l, it, step, 1)
                pool_residual(pool, l, it, step)
            step.end()

        def sp1(sp, l, it):
            def stack(g):
                if BACK[l]:
                    sp.wait_ge(*st.filled(l, it, ("E", g, TT - 1, 1)))
                heads = slice(GH * g, GH * g + GH)
                sp_stack(sp, l, it, g, 0, q_1[:, g, :, :], DIM, HD, heads)
                sp_stack(sp, l, it, g, 1, k_1[:, g:g + 1, :], 64, HD, slice(g, g + 1))

            sp_rounds(sp, l, it, [(i // 2, (i % 2) * (P if i < 2 else 32), DIM if i < 2 else 64, P if i < 2 else 32)
                                  for i in range(4)], stack, lambda g: q_1[48:50, g, :, :])

        full.close()
        l3 = ExitStack()
        raw = ExitStack()
        fc1_q = sb("fc1_q", [P, KT * 1024], I32, raw)
        fc1_s = sb("fc1_s", [P, KT * 1024], F32, raw)
        fc2_q = sb("fc2_q", [P, 8 * DIM], I32, raw)
        fc2_s = sb("fc2_s", [P, 8 * DIM], F32, raw)
        raw.close()
        q_3 = sb("q_3", [P, GROUPS, GH, SEQ], F32, l3)
        k_3 = sb("k_3", [P, GROUPS, GH, SEQ], F32, l3)
        src3 = sb("src3", [P, 4, SEQ], F32, l3)
        wq3 = sb("wq3", [P, KT, DIM], F32, l3)
        wk3 = sb("wk3", [P, KT, DIM], F32, l3)
        wv3 = sb("wv3", [P, KT, DIM], F32, l3)
        wo3 = sb("wo3", [P, KT, DIM], F32, l3)
        mask_q = sb("mask_q", [P, 3, DIM], BF16, l3)
        mask_k = sb("mask_k", [P, 2, DIM], BF16, l3)
        gamma = sb("gamma", [P, KT], F32, l3)
        beta = sb("beta", [P, KT], F32, l3)
        hn = sb("hn", [P, TT, DIM], F32, l3)
        hT = sb("hT", [P, KT, SEQ], F32, l3)
        stats3 = sb("stats3", [P, TT, 6], F32, l3)
        mv3 = sb("mv3", [P, TT, 2], F32, l3)
        veps3 = sb("veps3", [P, TT], F32, l3)
        rstd3 = sb("rstd3", [P, TT], F32, l3)
        fc1 = sb("fc1", [P, KT, 1024], F32, l3)
        fc2 = sb("fc2", [P, 8, DIM], F32, l3)
        fc1_b = sb("fc1_b", [P, 8], F32, l3)
        probs3 = sb("probs3", [P, 2, GH * BAND], F32, l3)
        hid3 = sb("hid3", [P, 8, SEQ], F32, l3)
        l3.close()
        attn.close()

        loads3 = [(wq3, d["wq3"]), (wk3, d["wk3"]), (wv3, d["wv3"]), (mask_q, d["mask_q"]), (mask_k, d["mask_k"]),
                  (gamma, d["gamma"]), (beta, d["beta"]), (fc1_q, d["fc1_q"]), (fc1_s, bc("fc1_s", KT * 1024)),
                  (fc1_b, d["fc1_b"]), (fc2_q, d["fc2_q"]), (fc2_s, bc("fc2_s", 8 * DIM)), (wo3, d["wo3"])]
        loaded3 = sem("loaded3")
        N3 = 16 * (len(loads3) + 1)
        dve_set3, pool_set3 = sem("dve_set3"), sem("pool_set3")
        moments3 = sig("moments3", [0, 0, 0, TT], "vector")
        rstd3_ready = sig("rstd3_ready", [0, 0, 0, 1], "gpsimd")
        hn_ready = sig("hn_ready", [0, 0, 0, TT], "vector")

        def sp_setup3(sp):
            sp.wait_ge(*y_stored.at(PRE3, 0))
            for dst, src in loads3:
                sp.dma_start(dst[:], src).then_inc(loaded3, 16)
            sp.dma_start(bias_bc[:, 0, :], bc("fc2_b", DIM)).then_inc(loaded3, 16)

        def dve_setup3(dve):
            dve.wait_ge(loaded3, N3)
            nc.vector.memset(k_3[32:50, :, :, :], 1.0).then_inc(dve_set3, 1)
            nc.vector.scalar_tensor_tensor(fc1[:, :, :].rearrange("p k n -> p (k n)"), fc1_q[:], -128.0, fc1_s[:],
                                           ALU.add, ALU.mult).then_inc(dve_set3, 1)
            nc.vector.tensor_scalar(fc2_s[:], fc2_s[:], 0.5, None, ALU.mult).then_inc(dve_set3, 1)
            dve.wait_ge(dve_set3, 3)
            nc.vector.scalar_tensor_tensor(fc2[:, :, :].rearrange("p k n -> p (k n)"), fc2_q[:], -128.0, fc2_s[:],
                                           ALU.add, ALU.mult).then_inc(dve_set3, 1)

        def pool_setup3(pool):
            pool.wait_ge(loaded3, N3)
            nc.gpsimd.memset(vext[:, :, :, HD:32], 1.0).then_inc(pool_set3, 1)
            nc.gpsimd.tensor_scalar(bias_bc[:, 0, :], bias_bc[:, 0, :], 0.5, None, ALU.mult).then_inc(pool_set3, 1)

        def pe3(pe, l, it):
            front, back = FRONT[l], BACK[l]

            def hidden(i):
                if i == 0:
                    pe.wait_ge(*done(st, l, it, "T2"))
                pe_project(pe, l, it, ("H", i), fc1, i, P, hT)

            def scores(g, i):
                h, j = i // 2, i % 2
                name = ("S", g, i)
                if i == 0:
                    pe.wait_ge(*stack_ready(l, it, g))
                for s in sc.vacated(l, it, name):
                    pe.wait_ge(*s)
                tile = sc.tile(l, name)
                nc.tensor.matmul(tile[:], ident_bf[:], mask_q[:, j:j + 2, :].rearrange("p a n -> p (a n)"),
                                 start=True, stop=False)
                for n in range(2):
                    qt = 2 * j + n
                    first = max(0, qt - 1) * P
                    width = (qt + 1) * P - first
                    ins = nc.tensor.matmul(tile[:, (n + 1) * DIM - width:(n + 1) * DIM], q_3[0:48, g, h, qt * P:(qt + 1) * P].bitcast(F32R),
                                           k_3[0:48, g, h, first:first + width].bitcast(F32R), start=False, stop=(n == 1))
                ins.then_inc(sc.full.sem, 1)

            def scores_t(g, h):
                name = ("E", g, h)
                if h == 0:
                    pe.wait_ge(*max_rows_loaded(l, it, g))
                for s in st.vacated(l, it, name):
                    pe.wait_ge(*s)
                tile = st.tile(l, name)
                mask = mask_k[:, :, :].rearrange("p a n -> p (a n)")
                for j in range(2):
                    n = SEQ - P * j
                    nc.tensor.matmul(tile[:, j * SEQ:j * SEQ + n], ident_bf[:], mask[:, 0:n], start=True, stop=False)
                    for kt in (2 * j, 2 * j + 1):
                        w = min(2 * P, SEQ - kt * P)
                        ins = nc.tensor.matmul(tile[:, kt * DIM:kt * DIM + w], k_3[0:50, g, h, kt * P:(kt + 1) * P].bitcast(F32R),
                                               q_3[0:50, g, h, kt * P:kt * P + w].bitcast(F32R), start=False, stop=(kt % 2 == 1))
                ins.then_inc(st.full.sem, 1)

            def weigh(g):
                pe.wait_ge(*done(st, l, it, ("E", g, GH - 1)))
                for s in pu.vacated(l, it, ("U", g)):
                    pe.wait_ge(*s)
                for qt in range(TT):
                    for kt in range(max(0, qt - 1), qt + 1):
                        for h in range(GH):
                            at = kt * DIM + (qt - kt) * P
                            ins = nc.tensor.matmul(bank_u[32 * h:32 * h + 32, qt * P:(qt + 1) * P],
                                                   vext[:, kt, GH * g + h, :], probs3[:, g % 2, h * BAND + at:h * BAND + at + P],
                                                   start=(kt == max(0, qt - 1)), stop=(kt == qt))
                ins.then_inc(pv_done.sem, 1)

            if back:
                pe_values(pe, l, it, wv3)
                for s in st.vacated(l, it, "T2"):
                    pe.wait_ge(*s)
                pe.wait_ge(*hn_ready.at(l, it, TT))
                for f in range(KT):
                    for t in range(TT):
                        ins = nc.tensor.transpose(st.tile(l, "T2")[:, f * SEQ + t * P:f * SEQ + (t + 1) * P],
                                                  hn[:, t, f * P:(f + 1) * P], ident[:])
                ins.then_inc(st.full.sem, 1)
                for i in range(4):
                    hidden(i)
            for g in range(GROUPS):
                for h in range(GH):
                    if back:
                        scores_t(g, h)
                        if h == 0 and g < GROUPS - 1:
                            pe_max_rows(pe, l, it, g + 1)
                    if back if g < 2 else front:
                        for i in range(2):
                            scores((g + 2) % GROUPS, 2 * h + i)
                    if back and h == 0 and g:
                        weigh(g - 1)
                    if back and g and h == 1:
                        pe_turn_sums(pe, l, it, g - 1)
                    if back and g and h == 2:
                        pe_spread_sums(pe, l, it, g - 1)
                    if front and h == 1 and g == 3:
                        pe_max_rows(pe, l, it, 0)
                if front and g == 0:
                    pe_transpose_xn(pe, l, it)
                    pe.wait_ge(*done(st, l, it, "T"))
                    pe_project(pe, l, it, "Q0", wq3, 0)
                    pe_project(pe, l, it, "K0", wk3, 0)
                    pe_project(pe, l, it, "Q1", wq3, 1)
                    pe_project(pe, l, it, "K1", wk3, 1)
                if back and g == 1:
                    for i in range(4, 8):
                        hidden(i)
            if back:
                for s in st.vacated(l, it, "OUT"):
                    pe.wait_ge(*s)
                pe.wait_ge(*done(sc, l, it, ("H", 7)))
                for t in range(TT):
                    for i in range(8):
                        nc.tensor.matmul(st.tile(l, "OUT")[:, t * DIM:(t + 1) * DIM], hid3[:, i, t * P:(t + 1) * P],
                                         fc2[:, i, :], start=(i == 0 and t % 2 == 0), stop=False)
                    if t == 0:
                        weigh(GROUPS - 1)
                    if t == 1:
                        pe_turn_sums(pe, l, it, GROUPS - 1)
                    if t == 2:
                        pe_spread_sums(pe, l, it, GROUPS - 1)
                pe_out_heads(pe, l, it, wo3)

        def act3(act, l, it, step):
            front, back = FRONT[l], BACK[l]
            step.begin(l, it)

            def hidden(i):
                act.wait_ge(*sc.filled(l, it, ("H", i)))
                nc.scalar.activation(hid3[:, i, :], sc.tile(l, ("H", i))[:], ACT.Silu,
                                     bias=fc1_b[:, i:i + 1]).then_inc(sc.free["act"].sem, 1)

            if back:
                act.wait_ge(*st.filled(l, it, "T2"))
                for f in range(KT):
                    ins = nc.scalar.activation(hT[:, f, :], st.tile(l, "T2")[:, f * SEQ:(f + 1) * SEQ], ACT.Identity,
                                               bias=beta[:, f:f + 1], scale=gamma[:, f:f + 1])
                ins.then_inc(st.free["act"].sem, 1)
                for i in range(4):
                    hidden(i)
            for g in range(GROUPS):
                for h in range(GH):
                    if back:
                        name = ("E", g, h)
                        act.wait_ge(*st.filled(l, it, name))
                        if h == 0:
                            act.wait_ge(*pv_done.at(l, it, max(0, g - 1)))
                        nc.scalar.activation(probs3[:, g % 2, h * BAND:(h + 1) * BAND], st.tile(l, name)[:, 0:BAND],
                                             ACT.Exp).then_inc(st.free["act"].sem, 1)
                        if h == 0 and g < GROUPS - 1:
                            act_max_rows(act, l, it, g + 1)
                        if h == 0 and g:
                            act_copy_sums(act, l, it, g - 1)
                    if front and h == 1 and g == 3:
                        act_max_rows(act, l, it, 0)
                if front and g == 0:
                    act_copy_xnT(act, l, it)
                    for i, name in enumerate(("Q0", "K0", "Q1", "K1")):
                        act.wait_ge(*sc.filled(l, it, name))
                        if i == 0:
                            act.wait_ge(*split.at(l, it))
                        nc.scalar.activation(src3[:, i, :], sc.tile(l, name)[:], ACT.Copy).then_inc(sc.free["act"].sem, 1)
                if back and g == 1:
                    for i in range(4, 8):
                        hidden(i)
            if back:
                act_copy_sums(act, l, it, GROUPS - 1)
            step.end()

        def dve3(dve, l, it, step):
            front, back = FRONT[l], BACK[l]
            step.begin(l, it)

            def maxima(g, first, last):
                for i in range(first, last):
                    h, j = i // 2, i % 2
                    dve.wait_ge(*sc.filled(l, it, ("S", g, i)))
                    nc.vector.tensor_reduce(nmax[:, g % 2, 2 * j:2 * j + 2, h],
                                            sc.tile(l, ("S", g, i))[:, :].rearrange("p (a n) -> p a n", a=2), AX, ALU.max,
                                            negate=True).then_inc(sc.free["dve"].sem, 1)
                if last == 8:
                    dve_split_max(dve, l, it, step, g, ("S", g, 7))

            if back:
                dve.wait_ge(*xn_ready.at(l, it))
                for t in range(TT):
                    step.mark(nc.vector.bn_stats(stats3[:, t, :], xn[:, t, 0:DIM]))
                step.wait()
                fence(dve)
                for t in range(TT):
                    nc.vector.bn_aggr(mv3[:, t, :], stats3[:, t, :]).then_inc(moments3.sem, 1)
                dve_values(dve, l, it, None)
                dve.wait_ge(*rstd3_ready.at(l, it, 1))
                for t in range(TT):
                    nc.vector.tensor_scalar(hn[:, t, :], xn[:, t, 0:DIM], mv3[:, t, 0:1], rstd3[:, t:t + 1],
                                            ALU.subtract, ALU.mult).then_inc(hn_ready.sem, 1)
                ln_stats(dve, l, it, step, 1)
                maxima(2, 0, 4)
                dve.wait_ge(*xres_ready.at(l, it, 1))
                ln_normalise(dve, l, it, 1)
                maxima(2, 4, 8)
            if front:
                for i, name in enumerate(("Q0", "K0", "Q1", "K1")):
                    dve_split(dve, l, it, step, i, src3[:, i, :], 1.0 if i % 2 else 0.25, done(sc, l, it, name))
            for g, part in ((3, back), (0, front), (1, front)):
                for first, last in ((0, 4), (4, 6), (6, 8)):
                    if part:
                        maxima(g, first, last)
                    if back and first == 0:
                        dve_invert_sums(dve, l, it, (g + 1) % GROUPS)
                    if back and first == 4:
                        dve_normalise_heads(dve, l, it, (g + 1) % GROUPS)
            if back:
                dve_invert_sums(dve, l, it, GROUPS - 1)
                dve_normalise_heads(dve, l, it, GROUPS - 1)
                dve_add_out(dve, l, it)
            step.end()

        def pool3(pool, l, it, step):
            step.begin(l, it)
            if BACK[l]:
                pool.wait_ge(*moments3.at(l, it, TT))
                fence(pool)
                step.mark(nc.gpsimd.tensor_scalar(veps3[:], mv3[:, :, 1], EPS, None, ALU.add))
                step.wait()
                nc.gpsimd.tensor_tensor(rstd3[:], veps3[:], mhalf[:], ALU.pow).then_inc(rstd3_ready.sem, 1)
                ln_rsqrt(pool, l, it, step, 1)
                pool.wait_ge(*xres_loaded.at(l, it, 16))
                step.mark(nc.gpsimd.tensor_tensor(xres[:], xres[:], bias_bc[:, 0:1, :].to_broadcast([P, TT, DIM]), ALU.add))
                step.wait()
                nc.gpsimd.tensor_tensor(xres[:], xres[:], xn[:, :, 0:DIM], ALU.add).then_inc(xres_ready.sem, 1)
            step.end()

        def sp3(sp, l, it):
            def stack(g):
                if BACK[l]:
                    sp.wait_ge(*st.filled(l, it, ("E", g, GH - 1)))
                for side, tile in enumerate((q_3, k_3)):
                    sp_stack(sp, l, it, g, side, tile[:, g, :, :], DIM, HD, slice(GH * g, GH * g + GH))

            sp_rounds(sp, l, it, [(i % 2, i // 2 * P, DIM, P) for i in range(4)], stack, lambda g: q_3[48:50, g, :, :])

        l2 = ExitStack()
        win = sb("win", [P, KT, 1024], F32, l2)
        conv = sb("conv", [P, CT, 4], F32, l2)
        wx = sb("wx", [P, CT, 48], F32, l2)
        wx_raw = sb("wx_raw", [P, CT, 32], F32, l2)
        wdb = sb("wdb", [48, SEQ], F32, l2)
        bdt = sb("bdt", [P, CT], F32, l2)
        dpar = sb("dpar", [P, CT], F32, l2)
        wout = sb("wout", [P, CT, DIM], F32, l2)
        wg = sb("wg", [P, KT, 8], F32, l2)
        prio = sb("prio", [P, 8], F32, l2)
        moe_a = sb("moe_a", [P, NE, KT, 352], F32, l2)
        moe_b = sb("moe_b", [P, NE, KT, 352], F32, l2)
        moe_c = sb("moe_c", [P, NE, 3, DIM], F32, l2)
        xc = sb("xc", [P, CT, SEQ + 3], F32, l2)
        cv = sb("cv", [P, CT, SEQ], F32, l2)
        u = sb("u", [P, CT, SEQ], F32, l2)
        sz = sb("sz", [P, CT, SEQ], F32, l2)
        xp = sb("xp", [48, SEQ], F32, l2)
        dtb = sb("dtb", [P, CT, SEQ], F32, l2)
        ub = sb("ub", [P, CT, SEQ], F32, l2)
        sil = sb("sil", [P, 2, SEQ], F32, l2)
        hm = sb("hm", [P, 2, 3, SEQ], F32, l2)
        rl = sb("rl", [P, TT, 8], F32, l2)
        hot = sb("hot", [P, 2, TT, 8], F32, l2)
        tmp8 = sb("tmp8", [P, 2, TT, 8], F32, l2)
        vtop = sb("vtop", [P, 8, TT], F32, l2)
        wtok = sb("wtok", [P, TT, 8], F32, l2)
        l2.close()

        loads2 = [(win, d["win"]), (wg, d["wg"]), (prio, bc("prio", 8)), (conv, d["conv"]), (wx_raw, d["wx"]),
                  (bdt, d["bdt"]), (dpar, d["dpar"])]
        loaded2, loaded2b, dve_set2 = sem("loaded2"), sem("loaded2b"), sem("dve_set2")
        N2 = 16 * len(loads2)
        moe_loaded = [sem(f"moe_loaded{e}") for e in range(NE)]
        cv_ready = sig("cv_ready", [0, 0, CT, 0], "vector")
        u_ready = sig("u_ready", [0, 0, CT, 0], "scalar")
        dt_raw = sig("dt_raw", [0, 0, CT, 0], "vector")
        dt_ready = sig("dt_ready", [0, 0, CT, 0], "scalar")
        gap_ready = sig("gap_ready", [0, 0, 1, 0], "vector")
        gap_exp = sig("gap_exp", [0, 0, 1, 0], "scalar")
        hm_ready = sig("hm_ready", [0, 0, 3 * NE, 0], "vector")
        y_ready = sig("y_ready", [0, 0, 1, 0], "vector")

        def sp_setup2(sp):
            sp.wait_ge(*y_stored.at(ALL2, 0))
            for dst, src in loads2:
                sp.dma_start(dst[:], src).then_inc(loaded2, 16)
            for e in (8, 9, 0):
                for dst, name in ((moe_a, "moe_a"), (moe_b, "moe_b"), (moe_c, "moe_c")):
                    sp.dma_start(dst[:, e], d[name][:, e]).then_inc(moe_loaded[e], 16)
            sp.dma_start(wdb[0:16, :], d["wdt"]).then_inc(loaded2b, 16)
            sp.dma_start(wdb[32:48, :], d["wbp"]).then_inc(loaded2b, 16)
            sp.dma_start(wout[:], d["wout"]).then_inc(loaded2b, 16)
            for e in range(1, 8):
                for dst, name in ((moe_a, "moe_a"), (moe_b, "moe_b"), (moe_c, "moe_c")):
                    sp.dma_start(dst[:, e], d[name][:, e]).then_inc(moe_loaded[e], 16)

        def dve_setup2(dve):
            dve.wait_ge(loaded2, N2)
            nc.vector.memset(xc[:, :, 0:3], 0.0).then_inc(dve_set2, 1)
            nc.vector.memset(wx[:, :, 16:32], 0.0).then_inc(dve_set2, 1)
            nc.vector.tensor_copy(wx[:, :, 0:16], wx_raw[:, :, 0:16]).then_inc(dve_set2, 1)
            nc.vector.tensor_copy(wx[:, :, 32:48], wx_raw[:, :, 16:32]).then_inc(dve_set2, 1)

        def pe2(pe, it):
            l = ALL2
            pe_transpose_xn(pe, l, it)
            pe.wait_ge(*done(st, l, it, "T"))
            for s in sc.vacated(l, it, "R"):
                pe.wait_ge(*s)
            for t in range(TT):
                for k in range(KT):
                    ins = nc.tensor.matmul(sc.tile(l, "R")[:, t * 8:t * 8 + 8], xnT[:, k, t * P:(t + 1) * P], wg[:, k, :],
                                           start=(k == 0), stop=(k == 1))
            ins.then_inc(sc.full.sem, 1)
            for c in range(CT):
                pe_project(pe, l, it, ("XC", c), win, c)
            for c in range(CT):
                pe_project(pe, l, it, ("Z", c), win, CT + c)

            def expert_in(e):
                pe.wait_ge(moe_loaded[e], 48)
                for i, (at, n) in enumerate(HT):
                    pe_project(pe, l, it, ("A", e, i), moe_a[:, e], 0, n, None, at)
                    pe_project(pe, l, it, ("B", e, i), moe_b[:, e], 0, n, None, at)

            def expert_out(e, order):
                for s in st.vacated(l, it, ("Y", e)):
                    pe.wait_ge(*s)
                pe.wait_ge(*hm_ready.at(l, it, 3 * order + 3))
                for t in range(TT):
                    for i, (at, n) in enumerate(HT):
                        ins = nc.tensor.matmul(st.tile(l, ("Y", e))[:, t * DIM:(t + 1) * DIM],
                                               hm[0:n, order % 2, i, t * P:(t + 1) * P], moe_c[0:n, e, i, :],
                                               start=(i == 0), stop=(i == 2))
                ins.then_inc(st.full.sem, 1)

            expert_in(8)
            expert_in(9)
            expert_out(8, 0)
            for s in sc.vacated(l, it, "XP"):
                pe.wait_ge(*s)
            pe.wait_ge(*u_ready.at(l, it, CT))
            for c in range(CT):
                ins = nc.tensor.matmul(sc.tile(l, "XP")[0:48, :], wx[:, c, :], u[:, c, :], start=(c == 0), stop=(c == CT - 1))
            ins.then_inc(sc.full.sem, 1)
            expert_in(0)
            expert_out(9, 1)
            pe.wait_ge(loaded2b, 48)
            pe.wait_ge(*done(sc, l, it, "XP"))
            for c in range(CT):
                for s in sc.vacated(l, it, ("DT", c)):
                    pe.wait_ge(*s)
                nc.tensor.matmul(sc.tile(l, ("DT", c))[:], wdb[0:16, c * P:(c + 1) * P], xp[0:16, :],
                                 start=True, stop=True).then_inc(sc.full.sem, 1)
                for s in sc.vacated(l, it, ("BP", c)):
                    pe.wait_ge(*s)
                nc.tensor.matmul(sc.tile(l, ("BP", c))[:], wdb[32:48, c * P:(c + 1) * P], xp[32:48, :],
                                 start=True, stop=True).then_inc(sc.full.sem, 1)
            for e in range(1, 8):
                expert_in(e)
                expert_out(e - 1, e + 1)
            for s in st.vacated(l, it, "OUT"):
                pe.wait_ge(*s)
            pe.wait_ge(*y_ready.at(l, it, 1))
            for t in range(TT):
                for c in range(CT):
                    ins = nc.tensor.matmul(st.tile(l, "OUT")[:, t * DIM:(t + 1) * DIM], cv[:, c, t * P:(t + 1) * P],
                                           wout[:, c, :], start=(c == 0), stop=(c == CT - 1))
            ins.then_inc(st.full.sem, 1)
            expert_out(7, 9)

        def act2(act, it, step):
            l = ALL2
            step.begin(l, it)
            act_copy_xnT(act, l, it)
            for c in range(CT):
                act.wait_ge(*sc.filled(l, it, ("XC", c)))
                nc.scalar.activation(xc[:, c, 3:SEQ + 3], sc.tile(l, ("XC", c))[:], ACT.Copy).then_inc(sc.free["act"].sem, 1)
            for c in range(CT):
                act.wait_ge(*sc.filled(l, it, ("Z", c)))
                nc.scalar.activation(sz[:, c, :], sc.tile(l, ("Z", c))[:], ACT.Silu).then_inc(sc.free["act"].sem, 1)

            def expert(e, order):
                for i, (at, n) in enumerate(HT):
                    act.wait_ge(*sc.filled(l, it, ("A", e, i)))
                    act.wait_ge(*hm_ready.at(l, it, max(0, 3 * order + i - 1)))
                    nc.scalar.activation(sil[0:n, (3 * order + i) % 2, :], sc.tile(l, ("A", e, i))[0:n, :],
                                         ACT.Silu).then_inc(sc.free["act"].sem, 1)

            expert(8, 0)
            for c in range(CT):
                act.wait_ge(*cv_ready.at(l, it, c + 1))
                nc.scalar.activation(u[:, c, :], cv[:, c, :], ACT.Silu).then_inc(u_ready.sem, 1)
            expert(9, 1)
            act.wait_ge(*sc.filled(l, it, "XP"))
            nc.scalar.activation(xp[:], sc.tile(l, "XP")[0:48, :], ACT.Copy).then_inc(sc.free["act"].sem, 1)
            expert(0, 2)
            expert(1, 3)
            act.wait_ge(*gap_ready.at(l, it, 1))
            nc.scalar.activation(vtop[:, 4, :], vtop[:, 3, :], ACT.Exp).then_inc(gap_exp.sem, 1)
            act.wait_ge(*dt_raw.at(l, it, CT))
            for c in range(CT):
                step.mark(nc.scalar.activation(dtb[:, c, :], dtb[:, c, :], ACT.Exp))
            for c in range(CT):
                step.wait(c + 1)
                nc.scalar.activation(dtb[:, c, :], dtb[:, c, :], ACT.Ln, bias=1.0).then_inc(dt_ready.sem, 1)
            for e in range(2, 8):
                expert(e, e + 2)
            step.end()

        def dve2(dve, it, step):
            l = ALL2
            step.begin(l, it)
            dve.wait_ge(*sc.filled(l, it, "R"))
            nc.vector.tensor_copy(rl[:], sc.tile(l, "R")[:, 0:32].rearrange("p (t e) -> p t e", t=TT))\
              .then_inc(sc.free["dve"].sem, 1)
            dve.wait_ge(*done(sc, l, it, "R"))
            pr = prio[:, None, :].to_broadcast([P, TT, 8])
            for j in range(2):
                def col(r):
                    return vtop[:, r, :, None].to_broadcast([P, TT, 8])
                step.mark(nc.vector.tensor_reduce(vtop[:, j, :], rl[:], AX, ALU.max))
                step.wait()
                step.mark(nc.vector.tensor_tensor(tmp8[:, 0], rl[:], col(j), ALU.is_equal))
                step.wait()
                step.mark(nc.vector.tensor_tensor(tmp8[:, 1], tmp8[:, 0], pr, ALU.mult))
                step.wait()
                step.mark(nc.vector.tensor_reduce(vtop[:, 2, :], tmp8[:, 1], AX, ALU.max))
                step.wait()
                step.mark(nc.vector.tensor_tensor(hot[:, j], tmp8[:, 1], col(2), ALU.is_equal))
                step.wait()
                if j == 0:
                    step.mark(nc.vector.scalar_tensor_tensor(rl[:], hot[:, 0], -3.0e38, rl[:], ALU.mult, ALU.add))
                    step.wait()
            nc.vector.tensor_tensor(vtop[:, 3, :], vtop[:, 1, :], vtop[:, 0, :], ALU.subtract).then_inc(gap_ready.sem, 1)

            def convolve(c):
                dve.wait_ge(*done(sc, l, it, ("XC", c)))
                step.mark(nc.vector.tensor_scalar(cv[:, c, :], xc[:, c, 0:SEQ], conv[:, c, 0:1], None, ALU.mult))
                for j in range(1, 4):
                    step.wait()
                    ins = nc.vector.scalar_tensor_tensor(cv[:, c, :], xc[:, c, j:j + SEQ], conv[:, c, j:j + 1], cv[:, c, :],
                                                         ALU.mult, ALU.add)
                    if j < 3:
                        step.mark(ins)
                ins.then_inc(cv_ready.sem, 1)

            def expert(e, order):
                for i, (at, n) in enumerate(HT):
                    dve.wait_ge(*done(sc, l, it, ("A", e, i)))
                    fence(dve)
                    dve.wait_ge(*sc.filled(l, it, ("B", e, i)))
                    nc.vector.tensor_tensor(hm[0:n, order % 2, i, :], sc.tile(l, ("B", e, i))[0:n, :],
                                            sil[0:n, (3 * order + i) % 2, :], ALU.mult).then_inc(hm_ready.sem, 1)
                    dve.wait_ge(*hm_ready.at(l, it, 3 * order + i + 1))
                    dve.sem_inc(sc.free["dve"].sem, 1)

            def add(e):
                dve.wait_ge(*st.filled(l, it, ("Y", e)))
                fence(dve)
                dve.wait_ge(*xres_loaded.at(l, it, 16))
                tile = st.tile(l, ("Y", e))
                if e >= 8:
                    flat = xres[:, :, :].rearrange("p t f -> p (t f)")
                    ins = nc.vector.tensor_tensor(flat, tile[:], flat, ALU.add)
                else:
                    for t in range(TT):
                        ins = nc.vector.scalar_tensor_tensor(xres[:, t, :], tile[:, t * DIM:(t + 1) * DIM],
                                                             wtok[:, t, e:e + 1], xres[:, t, :], ALU.mult, ALU.add)
                ins.then_inc(st.free["dve"].sem, 1)
                dve.wait_ge(*done(st, l, it, ("Y", e)))

            convolve(0)
            convolve(1)
            for order, e in enumerate((8,)):
                expert(e, 0)
            convolve(2)
            convolve(3)
            expert(9, 1)
            add(8)
            expert(0, 2)
            add(9)
            for c in range(CT):
                dve.wait_ge(*sc.filled(l, it, ("DT", c)))
                nc.vector.tensor_scalar(dtb[:, c, :], sc.tile(l, ("DT", c))[:], bdt[:, c:c + 1], 2.0, ALU.add, ALU.min)\
                  .then_inc(dt_raw.sem, 1)
                dve.wait_ge(*dt_raw.at(l, it, c + 1))
                dve.sem_inc(sc.free["dve"].sem, 1)
                dve.wait_ge(*sc.filled(l, it, ("BP", c)))
                nc.vector.tensor_tensor(ub[:, c, :], sc.tile(l, ("BP", c))[:], u[:, c, :], ALU.mult)\
                  .then_inc(sc.free["dve"].sem, 1)
            expert(1, 3)
            dve.wait_ge(*gap_exp.at(l, it, 1))
            step.mark(nc.vector.tensor_scalar(vtop[:, 5, :], vtop[:, 4, :], 1.0, None, ALU.add))
            step.wait()
            step.mark(nc.vector.reciprocal(vtop[:, 6, :], vtop[:, 5, :]))
            step.wait()
            step.mark(nc.vector.tensor_tensor(vtop[:, 7, :], vtop[:, 4, :], vtop[:, 6, :], ALU.mult))
            step.wait()
            for j in range(2):
                step.mark(nc.vector.tensor_tensor(hot[:, j], hot[:, j], vtop[:, 6 + j, :, None].to_broadcast([P, TT, 8]),
                                                  ALU.mult))
            step.wait()
            step.mark(nc.vector.tensor_tensor(wtok[:], hot[:, 0], hot[:, 1], ALU.add))
            step.wait()
            add(0)
            for e in range(2, 8):
                expert(e, e + 2)
                add(e - 1)
                if e - 2 < CT:
                    c = e - 2
                    dve.wait_ge(*dt_ready.at(l, it, c + 1))
                    step.mark(nc.vector.tensor_scalar(dtb[:, c, :], dtb[:, c, :], 1e-4, 1.0, ALU.max, ALU.min))
                    step.wait()
                    step.mark(nc.vector.tensor_scalar(dtb[:, c, :], dtb[:, c, :], -1.0, 1.0, ALU.mult, ALU.add))
                    step.wait()
                    step.mark(nc.vector.tensor_tensor_scan(cv[:, c, :], dtb[:, c, :], ub[:, c, :], 0.0, ALU.mult, ALU.add))
                    step.wait()
                    step.mark(nc.vector.scalar_tensor_tensor(cv[:, c, :], u[:, c, :], dpar[:, c:c + 1], cv[:, c, :],
                                                             ALU.mult, ALU.add))
                    step.wait()
                    ins = nc.vector.tensor_tensor(cv[:, c, :], cv[:, c, :], sz[:, c, :], ALU.mult)
                    if c == CT - 1:
                        ins.then_inc(y_ready.sem, 1)
                if e == 6:
                    ln_stats(dve, l, it, step, 1)
                if e == 7:
                    ln_normalise(dve, l, it, 1)
            dve.wait_ge(*st.filled(l, it, "OUT"))
            flat = xres[:, :, :].rearrange("p t f -> p (t f)")
            nc.vector.tensor_tensor(flat, st.tile(l, "OUT")[:], flat, ALU.add).then_inc(st.free["dve"].sem, 1)
            dve.wait_ge(*done(st, l, it, "OUT"))
            add(7)
            step.end()

        def pool2(pool, it, step):
            l = ALL2
            step.begin(l, it)
            ln_rsqrt(pool, l, it, step, 1)
            step.end()

        def sp2(sp, it):
            l = ALL2
            sp_load_next(sp, l, it)
            sp.wait_ge(*st.full.at(l, it, st.full.per[l]))
            fence(sp)
            sp.wait_ge(*done(st, l, it, ("Y", 7)))
            fence(sp)
            batch = it + (BATCH - 1 if l in (POST1, POST3) else 0)
            dst = xs_tok[batch + BATCH * (LAYER[l] + 1)] if LAYER[l] < LAYERS - 1 else out_tok[batch]
            sp.dma_start(dst, xres[:]).then_inc(y_stored.sem, 16)

        loads0 = [(ident, d["ident"]), (wq0, d["wq0"]), (wk0, d["wk0"]), (wv0, d["wv0"]), (bq0, d["bq0"]), (bk0, d["bk0"]),
                  (vbias, bc("bv0", DIM)), (w1, d["w1"]), (j_rows, d["j0"]), (same_head, d["same_head"]),
                  (lam, bc("lam0", 1)), (lscale, bc("scale0", 1, 4)), (b10, d["b10"]), (w2, d["w2"]), (wo0, d["wo0"])]
        N0 = 16 * (len(loads0) + 2)

        @block.sync
        def _(sp):
            open_signals(sp, "sync")
            sp.dma_start(xl[:], x_tok[0]).then_inc(x_loaded.sem, 16)
            for dst, src in loads0:
                sp.dma_start(dst[:], src).then_inc(consts, 16)
            sp.dma_start(bias_bc[:, 0, :], bc("bo0", DIM)).then_inc(consts, 16)
            sp.dma_start(bias_bc[:, 1, :], bc("b20", DIM)).then_inc(consts, 16)
            with sp.Fori(0, BATCH) as it:
                sp0(sp, it)
            sp_setup1(sp)
            sp1(sp, PRE1, 0)
            with sp.Fori(0, BATCH - 1) as it:
                sp1(sp, MAIN1, it)
            sp1(sp, POST1, 0)
            sp_setup2(sp)
            with sp.Fori(0, BATCH) as it:
                sp2(sp, it)
            sp_setup3(sp)
            sp3(sp, PRE3, 0)
            with sp.Fori(0, BATCH - 1) as it:
                sp3(sp, MAIN3, it)
            sp3(sp, POST3, 0)
            sp.wait_ge(y_stored.sem, y_stored.start + 16 * BATCH * LAYERS)

        @block.gpsimd
        def _(pool):
            open_signals(pool, "gpsimd")
            step = Chain(pool, sem("pool_step"), spread([1, 1, 1, 3]), 2)
            nc.gpsimd.memset(mhalf[:], -0.5).then_inc(step.sig.sem, 1)
            pool.wait_ge(step.sig.sem, 1)
            pool.wait_ge(ln_moments.sem, TT)
            fence(pool)
            nc.gpsimd.tensor_scalar(veps[:], mv[:, :, 1], EPS, None, ALU.add).then_inc(step.sig.sem, 1)
            pool.wait_ge(step.sig.sem, 2)
            nc.gpsimd.tensor_tensor(rstd[:], veps[:], mhalf[:], ALU.pow).then_inc(ln_rstd.sem, 1)
            pool.wait_ge(consts, N0)
            nc.gpsimd.memset(xn[:, :, DIM:DIM + 1], 1.0).then_inc(pool_setup, 1)
            nc.gpsimd.memset(vext[:, :, :, HD:32], 1.0).then_inc(pool_setup, 1)
            nc.gpsimd.tensor_tensor(bias_bc[:, 0, :], bias_bc[:, 0, :], bias_bc[:, 1, :], ALU.add).then_inc(pool_setup, 1)
            pool.wait_ge(dve_setup, 6)
            pool.wait_ge(pool_setup, 3)
            with pool.Fori(0, BATCH) as it:
                pool0(pool, it, step)
            pool.wait_ge(loaded1, N1)
            pool.wait_ge(dve_pre1, 9)
            pool1(pool, PRE1, 0, step)
            with pool.Fori(0, BATCH - 1) as it:
                pool1(pool, MAIN1, it, step)
            pool1(pool, POST1, 0, step)
            pool.wait_ge(loaded2, N2)
            with pool.Fori(0, BATCH) as it:
                pool2(pool, it, step)
            pool_setup3(pool)
            pool.wait_ge(pool_set3, 2)
            pool3(pool, PRE3, 0, step)
            with pool.Fori(0, BATCH - 1) as it:
                pool3(pool, MAIN3, it, step)
            pool3(pool, POST3, 0, step)

        @block.scalar
        def _(act):
            open_signals(act, "scalar")
            step = Chain(act, sem("act_step"), spread([0, 0, 4, 0]))
            act.sem_inc(step.sig.sem, 1)
            act.dma_start(xs[0:BATCH, :, :], d["x"]).then_inc(xs_copied, 16)
            act.dma_start(xs[BATCH * LAYERS, :, :], d["x"][0]).then_inc(xs_copied, 16)
            act.wait_ge(dve_setup, 6)
            act.wait_ge(pool_setup, 3)
            with act.Fori(0, BATCH) as it:
                act0(act, it, step)
            act.wait_ge(dve_set1, 5)
            act.wait_ge(dve_pre1, 9)
            act1(act, PRE1, 0, step)
            with act.Fori(0, BATCH - 1) as it:
                act1(act, MAIN1, it, step)
            act1(act, POST1, 0, step)
            act.wait_ge(dve_set2, 4)
            with act.Fori(0, BATCH) as it:
                act2(act, it, step)
            act.wait_ge(dve_set3, 4)
            act3(act, PRE3, 0, step)
            with act.Fori(0, BATCH - 1) as it:
                act3(act, MAIN3, it, step)
            act3(act, POST3, 0, step)

        @block.vector
        def _(dve):
            open_signals(dve, "vector")
            step = Chain(dve, sem("dve_step"), spread(STEPS_DVE), TT)
            dve.wait_ge(x_loaded.sem, 16)
            for t in range(TT):
                nc.vector.bn_stats(stats[:, t, :], xl[:, t, :]).then_inc(step.sig.sem, 1)
            dve.wait_ge(step.sig.sem, TT)
            fence(dve)
            for t in range(TT):
                nc.vector.bn_aggr(mv[:, t, :], stats[:, t, :]).then_inc(ln_moments.sem, 1)
            ln_normalise(dve, 0, 0, 0)
            dve.wait_ge(consts, N0)
            nc.vector.tensor_copy(ident_bf[:], ident[:]).then_inc(dve_setup, 1)
            nc.vector.memset(k_a[96:98, :, :, :], 1.0).then_inc(dve_setup, 1)
            nc.vector.tensor_scalar(lmask[:], ident[0:4, 0:4], lscale[:, 0:1], None, ALU.mult).then_inc(dve_setup, 1)
            nc.vector.tensor_scalar(same_head[:], same_head[:], lam[:, 0:1], None, ALU.mult).then_inc(dve_setup, 1)
            dve.wait_ge(dve_setup, 4)
            for k in range(KT):
                nc.vector.tensor_tensor(jbd[:, k, :, :], j_rows[:, k, :, None].to_broadcast([P, HD, NH]),
                                        same_head[:, None, :].to_broadcast([P, HD, NH]), ALU.mult).then_inc(dve_setup, 1)
            dve.wait_ge(pool_setup, 3)
            with dve.Fori(0, BATCH) as it:
                dve0(dve, it, step)
            dve_setup1(dve)
            dve1(dve, PRE1, 0, step)
            with dve.Fori(0, BATCH - 1) as it:
                dve1(dve, MAIN1, it, step)
            dve1(dve, POST1, 0, step)
            dve_setup2(dve)
            dve.wait_ge(dve_set2, 4)
            with dve.Fori(0, BATCH) as it:
                dve2(dve, it, step)
            dve_setup3(dve)
            dve.wait_ge(pool_set3, 2)
            dve3(dve, PRE3, 0, step)
            with dve.Fori(0, BATCH - 1) as it:
                dve3(dve, MAIN3, it, step)
            dve3(dve, POST3, 0, step)

        @block.tensor
        def _(pe):
            open_signals(pe, "tensor")
            pe.wait_ge(dve_setup, 6)
            pe.wait_ge(pool_setup, 3)
            with pe.Fori(0, BATCH) as it:
                pe0(pe, it)
            pe_setup1(pe)
            pe.wait_ge(dve_set1, 5)
            pe.wait_ge(dve_pre1, 9)
            pe1(pe, PRE1, 0)
            with pe.Fori(0, BATCH - 1) as it:
                pe1(pe, MAIN1, it)
            pe1(pe, POST1, 0)
            pe.wait_ge(dve_set2, 4)
            with pe.Fori(0, BATCH) as it:
                pe2(pe, it)
            pe.wait_ge(dve_set3, 4)
            pe.wait_ge(pool_set3, 2)
            pe3(pe, PRE3, 0)
            with pe.Fori(0, BATCH - 1) as it:
                pe3(pe, MAIN3, it)
            pe3(pe, POST3, 0)


def kernel(**inputs):
    import numpy as np
    from concourse import bacc
    from concourse.bass_utils import run_bass_kernel_spmd

    def arr(name):
        return np.ascontiguousarray(inputs[name])

    def by_rows(w):
        return np.ascontiguousarray(w.reshape(-1, P, w.shape[-1]).transpose(1, 0, 2))

    def columns(b):
        return np.ascontiguousarray(b.reshape(-1, P).T)

    def dim_major(w):
        return w.reshape(NH, HD, *w.shape[1:]).swapaxes(0, 1).reshape(w.shape)

    a = {
        "x": arr("L0_attn_x"),
        "ident": np.eye(P, dtype=np.float32),
        "wq0": by_rows(dim_major(arr("L0_attn_Wq")).T),
        "wk0": by_rows(dim_major(arr("L0_attn_Wk")).T),
        "wv0": by_rows(arr("L0_attn_Wv").T),
        "wo0": by_rows(arr("L0_attn_Wo").T),
        "bq0": columns(dim_major(arr("L0_attn_bq"))),
        "bk0": columns(dim_major(arr("L0_attn_bk"))),
        "bv0": arr("L0_attn_bv"),
        "bo0": arr("L0_attn_bo"),
        "j0": by_rows(arr("L0_attn_J_attn").swapaxes(0, 1).reshape(DIM, HD)),
        "same_head": np.tile(np.eye(NH, dtype=np.float32), (P // NH, 1)),
        "lam0": arr("L0_attn_lambda_attn").reshape(1),
        "w1": by_rows(arr("L0_ffn_W1").T),
        "b10": columns(arr("L0_ffn_b1")),
        "w2": by_rows(arr("L0_ffn_W2").T),
        "b20": arr("L0_ffn_b2"),
        "scale0": arr("L0_ffn_scale").reshape(1),
    }
    def even_odd(w, heads):
        return w.reshape(DIM, heads, HD // 2, 2).transpose(0, 3, 2, 1).reshape(DIM, heads * HD)

    inverse = (1.0 / 10000.0 ** (np.arange(0, DIM, 2, dtype=np.float32) / np.float32(DIM))).astype(np.float32)
    angle = np.arange(SEQ, dtype=np.float32)[:, None] * inverse[None, :]
    angle_q = angle.reshape(SEQ, NH, HD // 2).transpose(2, 1, 0).reshape(P, SEQ)
    angle_k = np.repeat(angle[:, :HD // 2].T, 4, axis=0)
    w1_1 = arr("L1_ffn_w1")
    a |= {
        "wq1": by_rows(even_odd(arr("L1_attn_Wq"), NH)),
        "wk1": by_rows(even_odd(arr("L1_attn_Wk"), 4)),
        "wv1": by_rows(arr("L1_attn_Wv")),
        "wo1": by_rows(arr("L1_attn_Wo")),
        "cos1": np.cos(angle_q), "sin1": np.sin(angle_q),
        "cosk": np.cos(angle_k), "sink": np.sin(angle_k),
        "w1x": by_rows(w1_1[:, :DIM].T), "w1s": by_rows(w1_1[:, DIM:].T),
        "b11": columns(arr("L1_ffn_b1")),
        "w21": np.ascontiguousarray(arr("L1_ffn_w2").T),
        "b21": arr("L1_ffn_b2"),
        "tau": arr("L1_ffn_tau"),
        "slots": arr("L1_ffn_slot_init"), "slot_scale": arr("L1_ffn_slot_scale"),
        "wih": by_rows(arr("L1_ffn_gru_wih").T), "whh": by_rows(arr("L1_ffn_gru_whh").T),
        "bih": columns(arr("L1_ffn_gru_bih")), "bhh": columns(arr("L1_ffn_gru_bhh")),
        "wvs": by_rows(arr("L1_ffn_wv").T), "bvs": columns(arr("L1_ffn_bv")),
        "wos": by_rows(arr("L1_ffn_wo").T), "bo1": arr("L1_ffn_bo"),
    }
    def experts(name, shared):
        w = np.concatenate([arr(name), shared], axis=0)
        return np.ascontiguousarray(w.reshape(NE, -1, P, w.shape[-1]).transpose(2, 0, 1, 3))

    def halves(name):
        return arr(name).reshape(DIM, 2, 352).transpose(1, 0, 2)

    w3 = np.concatenate([arr("L2_ffn_W3"), arr("L2_ffn_Ws3").reshape(2, 352, DIM)], axis=0)
    w3 = np.concatenate([w3, np.zeros((NE, 32, DIM), np.float32)], axis=1)
    conv_w = arr("L2_attn_conv_w").reshape(CT, P, 4).transpose(1, 0, 2)
    a |= {
        "win": by_rows(arr("L2_attn_W_in")),
        "conv": np.ascontiguousarray(conv_w),
        "wx": by_rows(arr("L2_attn_W_x")),
        "wdt": arr("L2_attn_W_dt"), "wbp": arr("L2_attn_W_Bp"),
        "bdt": columns(arr("L2_attn_b_dt")), "dpar": columns(arr("L2_attn_D_param")),
        "wout": by_rows(arr("L2_attn_W_out")),
        "wg": by_rows(arr("L2_ffn_Wg")),
        "prio": np.arange(8, 0, -1, dtype=np.float32),
        "moe_a": experts("L2_ffn_W1", halves("L2_ffn_Ws1")),
        "moe_b": experts("L2_ffn_W2", halves("L2_ffn_Ws2")),
        "moe_c": np.ascontiguousarray(w3.reshape(NE, 3, P, DIM).transpose(2, 0, 1, 3)),
    }
    import ml_dtypes
    key, query = np.arange(P)[:, None], np.arange(P)[None, :]
    low = np.float32(-1e30)
    own = np.where(key <= query, 0, low)
    after = np.where(key > query, 0, low)
    a |= {
        "wq3": by_rows(dim_major(arr("L3_attn_Wq")).T), "wk3": by_rows(dim_major(arr("L3_attn_Wk")).T),
        "wv3": by_rows(arr("L3_attn_Wv").T), "wo3": by_rows(arr("L3_attn_Wo").T),
        "mask_q": np.concatenate([np.full((P, P), low), own.T, after.T, own.T, after.T, own.T], axis=1)
        .reshape(P, 3, DIM).astype(ml_dtypes.bfloat16),
        "mask_k": np.concatenate([own, after, own, after], axis=1).reshape(P, 2, DIM).astype(ml_dtypes.bfloat16),
        "gamma": columns(arr("L3_ffn_ln_gamma")), "beta": columns(arr("L3_ffn_ln_beta")),
        "fc1_q": by_rows(arr("L3_ffn_fc1_q")).reshape(P, -1), "fc1_s": arr("L3_ffn_fc1_scales").reshape(-1),
        "fc2_q": by_rows(arr("L3_ffn_fc2_q")).reshape(P, -1), "fc2_s": arr("L3_ffn_fc2_scales").reshape(-1),
        "fc1_b": columns(arr("L3_ffn_fc1_bias")), "fc2_b": arr("L3_ffn_fc2_bias"),
    }
    nc = bacc.Bacc("TRN2", target_bir_lowering=False, num_devices=1)
    d = {n: nc.dram_tensor(f"in_{n}", v.shape, mybir.dt.from_np(v.dtype), kind="ExternalInput").ap()
         for n, v in a.items()}
    out = nc.dram_tensor("out_0", (BATCH, SEQ, DIM), F32, kind="ExternalOutput").ap()
    build(nc, d, out)
    r = run_bass_kernel_spmd(nc, [{f"in_{n}": v for n, v in a.items()}], core_ids=[0])
    return r.results[0]["out_0"]
```
